# Optimizing a Trainium2 kernel written in Bass

```python
import numpy as np
import jax
import jax.numpy as jnp

def _softmax(x, axis=-1):
    return jax.nn.softmax(x, axis=axis)

def _gelu(x):
    return jax.nn.gelu(x, approximate=True)

def _silu(x):
    return jax.nn.silu(x)

def _sigmoid(x):
    return jax.nn.sigmoid(x)

def _layernorm(x, axis=-1, eps=1e-05):
    m = jnp.mean(x, axis=axis, keepdims=True)
    v = jnp.var(x, axis=axis, keepdims=True)
    return (x - m) / jnp.sqrt(v + eps)

def _scatter_add(tgt, idx, src, axis=0):
    return tgt.at[idx].add(src)

def _segment_sum(src, seg, n):
    return jax.ops.segment_sum(src, seg, n)
kernel_name = 'mk_decoder_preln_d4_seqx_r8_14319c'

def setup_inputs(seed: int=0):
    np.random.seed(seed)
    _w = jnp.asarray

    def _rec_inputs():
        import jax
        import jax.numpy as jnp
        _rk = jax.random.key(seed)
        x = 7.22e-05 + 1 * jax.random.normal(jax.random.fold_in(_rk, 1), (8, 128, 128), jnp.float32)
        _lenS = 128 - jax.random.randint(jax.random.fold_in(_rk, 7), (8,), 0, max(1, 128 // 4) + 1, jnp.int32)
        _lenS2 = 128 - jax.random.randint(jax.random.fold_in(_rk, 8), (8,), 0, max(1, 128 // 4) + 1, jnp.int32)
        _ctx_768P = jax.random.normal(jax.random.fold_in(_rk, 11), (8, 16, 96), jnp.float32)
        _ctx_768c = jax.random.dirichlet(jax.random.fold_in(_rk, 511), 0.3 * jnp.ones((16,), jnp.float32), (8, 128))
        _ctx_768t = jnp.einsum('bsk,bkd->bsd', _ctx_768c, _ctx_768P)
        _ctx_768t = _ctx_768t * jax.lax.rsqrt(jnp.mean(jnp.square(_ctx_768t)) + 1e-12) * 0.953939
        ctx_768 = 2.09791e-05 + 1.00001 * (_ctx_768t + 0.3 * jax.random.normal(jax.random.fold_in(_rk, 611), (8, 128, 96), jnp.float32))
        _validS = jnp.arange(128)[None, :] < _lenS[:, None]
        _validS2 = jnp.arange(128)[None, :] < _lenS2[:, None]
        _causal = jnp.tril(jnp.ones((128, 128), dtype=bool))
        mask_BxS_bf1 = jnp.ones((8, 128), dtype=bool)
        mask_BxS2_bf1 = jnp.ones((8, 128), dtype=bool)
        mask_BxS2_bk0 = jnp.logical_not(jnp.broadcast_to(_validS2[:, :], (8, 128)))
        return (x, ctx_768, mask_BxS_bf1, mask_BxS2_bf1, mask_BxS2_bk0)
    x, ctx_768, mask_BxS_bf1, mask_BxS2_bf1, mask_BxS2_bk0 = _rec_inputs()

    def _L0_attn_setup():
        import jax, jax.numpy as jnp
        import numpy as np
        DIM, HEADS, K = (128, 16, 64)
        key = jax.random.key(seed)
        ks = jax.random.split(key, 5)
        b, n = (4, 512)
        x = jax.random.normal(ks[0], (b, n, DIM), dtype=jnp.float32)
        s = 1.0 / np.sqrt(DIM)
        Wq = jax.random.normal(ks[1], (DIM, HEADS * K), dtype=jnp.float32) * s
        Wk = jax.random.normal(ks[2], (DIM, HEADS * K), dtype=jnp.float32) * s
        Wv = jax.random.normal(ks[3], (DIM, HEADS * K), dtype=jnp.float32) * s
        Wo = jax.random.normal(ks[4], (HEADS * K, DIM), dtype=jnp.float32) * (1.0 / np.sqrt(HEADS * K))
        return {'x': x, 'Wq': Wq, 'Wk': Wk, 'Wv': Wv, 'Wo': Wo}
    _L0_attn_all = _L0_attn_setup()
    _L0_attn_in = {k: v for k, v in _L0_attn_all.items() if k in ('Wq', 'Wk', 'Wv', 'Wo')}
    del _L0_attn_all

    def _L0_xattn_setup():
        import jax, jax.numpy as jnp
        import numpy as np
        HEADS = 8
        DIM_HEAD = 64
        SCALE = DIM_HEAD ** (-0.5)
        key = jax.random.key(seed)
        ks = jax.random.split(key, 7)
        b, n, m = (4, 256, 128)
        qd, cd, inner = (128, 96, HEADS * DIM_HEAD)
        s = lambda fan_in: 1.0 / np.sqrt(fan_in)
        return {'x': jax.random.normal(ks[0], (b, n, qd), jnp.float32), 'context': jax.random.normal(ks[1], (b, m, cd), jnp.float32), 'Wq': jax.random.normal(ks[2], (qd, inner), jnp.float32) * s(qd), 'Wk': jax.random.normal(ks[3], (cd, inner), jnp.float32) * s(cd), 'Wv': jax.random.normal(ks[4], (cd, inner), jnp.float32) * s(cd), 'Wout': jax.random.normal(ks[5], (inner, qd), jnp.float32) * s(inner), 'bout': jax.random.normal(ks[6], (qd,), jnp.float32) * 0.01}
    _L0_xattn_all = _L0_xattn_setup()
    _L0_xattn_in = {k: v for k, v in _L0_xattn_all.items() if k in ('Wq', 'Wk', 'Wv', 'Wout', 'bout')}
    del _L0_xattn_all

    def _L0_ffn_setup():
        import jax, jax.numpy as jnp
        import numpy as np
        DIM = 128
        NUM_EXPERTS = 8
        HIDDEN = 512
        CAP_FACTOR = 2.0
        B, S = (4, 256)
        key = jax.random.key(seed)
        ks = jax.random.split(key, 6)
        scale_r = 1.0 / np.sqrt(DIM)
        scale_1 = 1.0 / np.sqrt(DIM)
        scale_2 = 1.0 / np.sqrt(HIDDEN)
        return {'x': jax.random.normal(ks[0], (B, S, DIM), dtype=jnp.float32), 'router_w': jax.random.uniform(ks[1], (NUM_EXPERTS, DIM), jnp.float32, -scale_r, scale_r), 'w1': jax.random.uniform(ks[2], (NUM_EXPERTS, DIM, HIDDEN), jnp.float32, -scale_1, scale_1), 'b1': jax.random.uniform(ks[3], (NUM_EXPERTS, HIDDEN), jnp.float32, -scale_1, scale_1), 'w2': jax.random.uniform(ks[4], (NUM_EXPERTS, HIDDEN, DIM), jnp.float32, -scale_2, scale_2), 'b2': jax.random.uniform(ks[5], (NUM_EXPERTS, DIM), jnp.float32, -scale_2, scale_2)}
    _L0_ffn_all = _L0_ffn_setup()
    _L0_ffn_in = {k: v for k, v in _L0_ffn_all.items() if k in ('router_w', 'w1', 'b1', 'w2', 'b2')}
    del _L0_ffn_all

    def _L1_attn_setup():
        import jax, jax.numpy as jnp
        import numpy as np
        B, T, E = (4, 256, 128)
        H, HS = (16, 64)
        key = jax.random.key(seed)
        ks = jax.random.split(key, 6)
        return {'x': jax.random.normal(ks[0], (B, T, E), dtype=jnp.float32), 'Wq': jax.random.normal(ks[1], (H, E, HS), dtype=jnp.float32) * 0.02, 'Wk': jax.random.normal(ks[2], (H, E, HS), dtype=jnp.float32) * 0.02, 'Wv': jax.random.normal(ks[3], (H, E, HS), dtype=jnp.float32) * 0.02, 'proj_w': jax.random.normal(ks[4], (E, H * HS), dtype=jnp.float32) * 0.02, 'proj_b': jax.random.normal(ks[5], (E,), dtype=jnp.float32) * 0.02}
    _L1_attn_all = _L1_attn_setup()
    _L1_attn_in = {k: v for k, v in _L1_attn_all.items() if k in ('Wq', 'Wk', 'Wv', 'proj_w', 'proj_b')}
    del _L1_attn_all

    def _L1_xattn_setup():
        import jax, jax.numpy as jnp
        import numpy as np
        B, T, DT, G, DV = (16, 64, 128, 72, 96)
        H, DH = (4, 32)
        INNER = H * DH
        HID = 4 * DT
        N_STATE = 64
        K_TOP = 32

        def layernorm(x, g, b, eps=1e-05):
            m = x.mean(-1, keepdims=True)
            v = x.var(-1, keepdims=True)
            return (x - m) * jax.lax.rsqrt(v + eps) * g + b

        def s4d(x, log_dt, A_re, A_im, C_re, C_im, D_skip):
            Bb, L, D = x.shape
            dt = jnp.exp(log_dt)
            A = A_re + 1j * A_im
            C = C_re + 1j * C_im
            dtA = dt[:, None] * A
            dC = C * (jnp.exp(dtA) - 1.0) / A
            powers = jnp.exp(dtA[:, :, None] * jnp.arange(L))
            K = 2.0 * jnp.einsum('dn,dnl->dl', dC, powers).real
            n = 2 * L
            Kf = jnp.fft.rfft(K, n=n, axis=-1)
            xf = jnp.fft.rfft(x, n=n, axis=1)
            y = jnp.fft.irfft(xf * Kf.T[None], n=n, axis=1)[:, :L]
            return y + x * D_skip
        key = jax.random.key(seed)
        ks = jax.random.split(key, 16)
        s = 0.02
        inp = {'x_text': jax.random.normal(ks[0], (B, T, DT), jnp.float32), 'x_vision': jax.random.normal(ks[1], (B, G, DV), jnp.float32), 'text_mask': jnp.ones((B, T), bool), 'vision_mask': jnp.ones((B, G), bool), 'Wq': jax.random.normal(ks[2], (DT, INNER), jnp.float32) * s, 'Wk': jax.random.normal(ks[3], (DV, INNER), jnp.float32) * s, 'Wv': jax.random.normal(ks[4], (DV, DT), jnp.float32) * s, 'W_film_in': jax.random.normal(ks[5], (DT, 2 * DT), jnp.float32) * s, 'b_film_in': jnp.zeros((2 * DT,), jnp.float32), 'W_film_out': jax.random.normal(ks[6], (DT, 2 * DT), jnp.float32) * s, 'b_film_out': jnp.zeros((2 * DT,), jnp.float32), 'g_norm_in': jnp.ones((DT,), jnp.float32), 'b_norm_in': jnp.zeros((DT,), jnp.float32), 'g_norm_out': jnp.ones((DT,), jnp.float32), 'b_norm_out': jnp.zeros((DT,), jnp.float32), 'g_ffn': jnp.ones((DT,), jnp.float32), 'b_ffn': jnp.zeros((DT,), jnp.float32), 'W1': jax.random.normal(ks[7], (DT, HID), jnp.float32) * s, 'b1': jnp.zeros((HID,), jnp.float32), 'W2': jax.random.normal(ks[8], (HID, DT), jnp.float32) * s, 'b2': jnp.zeros((DT,), jnp.float32), 'log_dt': jnp.log(0.001) + jax.random.uniform(ks[9], (DT,), jnp.float32) * (jnp.log(0.1) - jnp.log(0.001)), 'A_re': -0.5 * jnp.ones((DT, N_STATE), jnp.float32), 'A_im': jnp.tile(jnp.pi * jnp.arange(N_STATE, dtype=jnp.float32), (DT, 1)), 'C_re': jax.random.normal(ks[10], (DT, N_STATE), jnp.float32) * 0.5 ** 0.5, 'C_im': jax.random.normal(ks[11], (DT, N_STATE), jnp.float32) * 0.5 ** 0.5, 'D_skip': jax.random.normal(ks[12], (DT,), jnp.float32), 'mod_gate': jnp.array(0.5, jnp.float32)}
        return inp
    _L1_xattn_all = _L1_xattn_setup()
    _L1_xattn_in = {k: v for k, v in _L1_xattn_all.items() if k in ('Wq', 'Wk', 'Wv', 'W_film_in', 'b_film_in', 'W_film_out', 'b_film_out', 'g_norm_in', 'b_norm_in', 'g_norm_out', 'b_norm_out', 'g_ffn', 'b_ffn', 'W1', 'b1', 'W2', 'b2', 'log_dt', 'A_re', 'A_im', 'C_re', 'C_im', 'D_skip', 'mod_gate')}
    del _L1_xattn_all

    def _L1_ffn_setup():
        import jax, jax.numpy as jnp
        import numpy as np
        DIM = 128
        DEPTH = 2
        HEADS = 8
        DIM_HEAD = 64
        WINDOW = 64
        INNER = HEADS * DIM_HEAD
        HID = int(DIM * 4 * 2 / 3)
        B, N = (2, 1024)
        QK_SCALE = 8.0

        def shift_token(t):
            t1, t2 = jnp.split(t, 2, axis=-1)
            t2 = jnp.pad(t2, ((0, 0), (1, 0), (0, 0)))[:, :-1]
            return jnp.concatenate([t1, t2], axis=-1)

        def l2norm(t):
            return t / jnp.clip(jnp.linalg.norm(t, axis=-1, keepdims=True), 1e-12)

        def rotate_half(x):
            x1, x2 = jnp.split(x, 2, axis=-1)
            return jnp.concatenate([-x2, x1], axis=-1)

        def rotary_xpos(q, k):
            n = q.shape[-2]
            half_idx = jnp.arange(0, DIM_HEAD, 2, dtype=jnp.float32)
            inv_freq = 1.0 / 10000.0 ** (half_idx / DIM_HEAD)
            t = jnp.arange(n, dtype=jnp.float32)
            freqs = t[:, None] * inv_freq[None, :]
            freqs = jnp.concatenate([freqs, freqs], axis=-1)
            base = (half_idx + 0.4 * DIM_HEAD) / (1.4 * DIM_HEAD)
            power = (t - n // 2) / float(WINDOW // 2)
            scale = base[None, :] ** power[:, None]
            scale = jnp.concatenate([scale, scale], axis=-1)
            cos, sin = (jnp.cos(freqs), jnp.sin(freqs))
            q = q * cos * scale + rotate_half(q) * sin * scale
            k = k * cos / scale + rotate_half(k) * sin / scale
            return (q, k)

        def local_attention(q, k, v):
            b, h, n, d = q.shape
            w = n // WINDOW
            bq = q.reshape(b, h, w, WINDOW, d) * QK_SCALE
            bk = k.reshape(b, h, w, WINDOW, d)
            bv = v.reshape(b, h, w, WINDOW, d)

            def look_around(t):
                p = jnp.pad(t, ((0, 0), (0, 0), (1, 0), (0, 0), (0, 0)))
                return jnp.concatenate([p[:, :, :w], p[:, :, 1:]], axis=3)
            bk, bv = (look_around(bk), look_around(bv))
            bt = jnp.arange(n).reshape(w, WINDOW)
            btp = jnp.pad(bt, ((1, 0), (0, 0)), constant_values=-1)
            btk = jnp.concatenate([btp[:w], btp[1:]], axis=1)
            sim = jnp.einsum('bhwid,bhwjd->bhwij', bq, bk)
            i = bt[:, :, None]
            j = btk[:, None, :]
            mask = (i < j) | (i > j + WINDOW) | (j == -1)
            sim = jnp.where(mask, -jnp.finfo(sim.dtype).max, sim)
            attn = jax.nn.softmax(sim, axis=-1)
            out = jnp.einsum('bhwij,bhwjd->bhwid', attn, bv)
            return out.reshape(b, h, n, d)

        def _layer(x, wqkv, qs, ksc, wo, lg, lb, w1, b1, w2, b2):
            b, n, _ = x.shape
            h = shift_token(x)
            qkv = h @ wqkv
            q, k, v = jnp.split(qkv, 3, axis=-1)
            to_heads = lambda t: t.reshape(b, n, HEADS, DIM_HEAD).transpose(0, 2, 1, 3)
            q, k, v = (to_heads(q), to_heads(k), to_heads(v))
            q = l2norm(q) * qs
            k = l2norm(k) * ksc
            q, k = rotary_xpos(q, k)
            o = local_attention(q, k, v)
            o = o.transpose(0, 2, 1, 3).reshape(b, n, INNER)
            x = x + o @ wo
            h = shift_token(x)
            mu = h.mean(-1, keepdims=True)
            var = h.var(-1, keepdims=True)
            h = (h - mu) / jnp.sqrt(var + 1e-05) * lg + lb
            h = h @ w1 + b1
            a, g = jnp.split(h, 2, axis=-1)
            h = a * jax.nn.gelu(g, approximate=False)
            x = x + h @ w2 + b2
            return x
        key = jax.random.key(seed)
        ks = jax.random.split(key, 6)
        return {'x': jax.random.normal(ks[0], (B, N, DIM), jnp.float32), 'wqkv': jax.random.normal(ks[1], (DEPTH, DIM, 3 * INNER), jnp.float32) * 0.02, 'q_scale': jnp.ones((DEPTH, DIM_HEAD), jnp.float32), 'k_scale': jnp.ones((DEPTH, DIM_HEAD), jnp.float32), 'wo': jax.random.normal(ks[2], (DEPTH, INNER, DIM), jnp.float32) * 0.02, 'ln_g': jnp.ones((DEPTH, DIM), jnp.float32), 'ln_b': jnp.zeros((DEPTH, DIM), jnp.float32), 'w1': jax.random.normal(ks[3], (DEPTH, DIM, 2 * HID), jnp.float32) * 0.02, 'b1': jnp.zeros((DEPTH, 2 * HID), jnp.float32), 'w2': jax.random.normal(ks[4], (DEPTH, HID, DIM), jnp.float32) * 0.02, 'b2': jnp.zeros((DEPTH, DIM), jnp.float32)}
    _L1_ffn_all = _L1_ffn_setup()
    _L1_ffn_in = {k: v for k, v in _L1_ffn_all.items() if k in ('wqkv', 'q_scale', 'k_scale', 'wo', 'ln_g', 'ln_b', 'w1', 'b1', 'w2', 'b2')}
    del _L1_ffn_all

    def _L2_attn_setup():
        import jax, jax.numpy as jnp
        import numpy as np
        NUM_HEADS = 16
        MAX_REL = 128

        def _rel_embeds(table, q_len, k_len):
            dist = jnp.arange(q_len)[:, None] - jnp.arange(k_len)[None, :]
            idx = jnp.clip(dist, -MAX_REL, MAX_REL) + MAX_REL
            return table[idx]
        key = jax.random.key(seed)
        ks = jax.random.split(key, 11)
        B, T, E = (4, 128, 128)
        D = E // NUM_HEADS
        P = 2 * MAX_REL + 1
        s = 0.02
        return {'hidden_states': jax.random.normal(ks[0], (B, T, E), jnp.float32), 'Wq': jax.random.normal(ks[1], (E, E), jnp.float32) * s, 'bq': jax.random.normal(ks[2], (E,), jnp.float32) * s, 'Wk': jax.random.normal(ks[3], (E, E), jnp.float32) * s, 'bk': jax.random.normal(ks[4], (E,), jnp.float32) * s, 'Wv': jax.random.normal(ks[5], (E, E), jnp.float32) * s, 'bv': jax.random.normal(ks[6], (E,), jnp.float32) * s, 'Wo': jax.random.normal(ks[7], (E, E), jnp.float32) * s, 'bo': jax.random.normal(ks[8], (E,), jnp.float32) * s, 'rel_k_emb': jax.random.normal(ks[9], (P, D), jnp.float32) * s, 'rel_v_emb': jax.random.normal(ks[10], (P, D), jnp.float32) * s}
    _L2_attn_all = _L2_attn_setup()
    _L2_attn_in = {k: v for k, v in _L2_attn_all.items() if k in ('Wq', 'bq', 'Wk', 'bk', 'Wv', 'bv', 'Wo', 'bo', 'rel_k_emb', 'rel_v_emb')}
    del _L2_attn_all

    def _L2_xattn_setup():
        import jax, jax.numpy as jnp
        import numpy as np
        DIM = 128
        CTX_DIM = 96
        HEADS = 16
        key = jax.random.key(seed)
        ks = jax.random.split(key, 7)
        B, N, M = (4, 512, 32)
        x = jax.random.normal(ks[0], (B, N, DIM), dtype=jnp.float32)
        context = jax.random.normal(ks[1], (B, M, CTX_DIM), dtype=jnp.float32)
        context_mask = jnp.ones((B, M), dtype=bool)
        s_d = 1.0 / np.sqrt(DIM)
        s_c = 1.0 / np.sqrt(CTX_DIM)
        Wq = jax.random.normal(ks[2], (DIM, DIM), dtype=jnp.float32) * s_d
        Wk = jax.random.normal(ks[3], (CTX_DIM, DIM), dtype=jnp.float32) * s_c
        Wv = jax.random.normal(ks[4], (CTX_DIM, DIM), dtype=jnp.float32) * s_c
        Wo = jax.random.normal(ks[5], (DIM, DIM), dtype=jnp.float32) * s_d
        return {'x': x, 'context': context, 'context_mask': context_mask, 'Wq': Wq, 'Wk': Wk, 'Wv': Wv, 'Wo': Wo}
    _L2_xattn_all = _L2_xattn_setup()
    _L2_xattn_in = {k: v for k, v in _L2_xattn_all.items() if k in ('Wq', 'Wk', 'Wv', 'Wo')}
    del _L2_xattn_all

    def _L2_ffn_setup():
        import jax, jax.numpy as jnp
        import numpy as np
        TOP_K = 2
        key = jax.random.key(seed)
        k1, k2, k3, k4 = jax.random.split(key, 4)
        B, N, D, E, F = (4, 256, 128, 8, 512)
        x = jax.random.normal(k1, (B, N, D), dtype=jnp.float32)
        gate_w = jax.random.normal(k2, (D, E), dtype=jnp.float32) * D ** (-0.5)
        w1 = jax.random.normal(k3, (E, D, F), dtype=jnp.float32) * D ** (-0.5)
        w2 = jax.random.normal(k4, (E, F, D), dtype=jnp.float32) * F ** (-0.5)
        return {'x': x, 'gate_w': gate_w, 'w1': w1, 'w2': w2}
    _L2_ffn_all = _L2_ffn_setup()
    _L2_ffn_in = {k: v for k, v in _L2_ffn_all.items() if k in ('gate_w', 'w1', 'w2')}
    del _L2_ffn_all

    def _L3_attn_setup():
        import jax, jax.numpy as jnp
        import numpy as np
        import math
        B, T, C = (2, 256, 128)
        H, L = (16, 64)
        DH = C // H
        DHE = DH // 2
        THETA = 10000.0

        def _rope_cache(t, dim):
            inv_freq = 1.0 / THETA ** (jnp.arange(0, dim, 2, dtype=jnp.float32) / dim)
            freqs = jnp.arange(t, dtype=jnp.float32)[:, None] * inv_freq[None, :]
            emb = jnp.concatenate((freqs, freqs), axis=-1)
            return (jnp.cos(emb), jnp.sin(emb))

        def _apply_rope(x, cos, sin):
            x1 = x[..., 0::2]
            x2 = x[..., 1::2]
            rot = jnp.stack((-x2, x1), axis=-1).reshape(x.shape)
            return x * cos[None, None] + rot * sin[None, None]
        key = jax.random.key(seed)
        ks = jax.random.split(key, 10)
        s = 0.02
        return {'x': jax.random.normal(ks[0], (B, T, C), jnp.float32), 'Wq_down': jax.random.normal(ks[1], (C, H * L), jnp.float32) * s, 'Wk_down': jax.random.normal(ks[2], (C, H * L), jnp.float32) * s, 'Wv_down': jax.random.normal(ks[3], (C, H * L), jnp.float32) * s, 'Wq_up_c': jax.random.normal(ks[4], (L, DHE), jnp.float32) * s, 'Wq_up_e': jax.random.normal(ks[5], (L, DHE), jnp.float32) * s, 'Wk_up_c': jax.random.normal(ks[6], (L, DHE), jnp.float32) * s, 'Wk_up_e': jax.random.normal(ks[7], (L, DHE), jnp.float32) * s, 'Wv_up': jax.random.normal(ks[8], (L, DH), jnp.float32) * s, 'Wc': jax.random.normal(ks[9], (C, C), jnp.float32) * s}
    _L3_attn_all = _L3_attn_setup()
    _L3_attn_in = {k: v for k, v in _L3_attn_all.items() if k in ('Wq_down', 'Wk_down', 'Wv_down', 'Wq_up_c', 'Wq_up_e', 'Wk_up_c', 'Wk_up_e', 'Wv_up', 'Wc')}
    del _L3_attn_all

    def _L3_xattn_setup():
        import jax, jax.numpy as jnp
        import numpy as np
        DIM_IN, DIM_LAT, DIM_HEAD = (96, 128, 64)
        INNER = max(DIM_LAT, DIM_IN)
        HEADS = INNER // DIM_HEAD
        SCALE = DIM_HEAD ** (-0.5)
        RMS_EPS = 1e-08
        LN_EPS = 1e-05

        def layernorm(x, g, b):
            mu = jnp.mean(x, axis=-1, keepdims=True)
            var = jnp.mean((x - mu) ** 2, axis=-1, keepdims=True)
            return (x - mu) * jax.lax.rsqrt(var + LN_EPS) * g + b

        def rmsnorm(x, gamma):
            norm = jnp.sqrt(jnp.sum(x * x, axis=-1, keepdims=True)) * x.shape[-1] ** (-0.5)
            return x / jnp.maximum(norm, RMS_EPS) * gamma
        key = jax.random.key(seed)
        ks = jax.random.split(key, 12)
        b, n, m = (4, 512, 64)
        x = jax.random.normal(ks[0], (b, n, DIM_IN), jnp.float32)
        latents = jax.random.normal(ks[1], (b, m, DIM_LAT), jnp.float32)
        mask = jax.random.randint(ks[2], (b, n), 0, 2).astype(bool)
        s = lambda k, sh, fan: jax.random.normal(k, sh, jnp.float32) * fan ** (-0.5)
        return {'x': x, 'latents': latents, 'mask': mask, 'ln_x_g': jnp.ones((DIM_IN,), jnp.float32), 'ln_x_b': jnp.zeros((DIM_IN,), jnp.float32), 'ln_l_g': jnp.ones((DIM_LAT,), jnp.float32), 'ln_l_b': jnp.zeros((DIM_LAT,), jnp.float32), 'qn_g': jnp.ones((DIM_HEAD,), jnp.float32), 'kn_g': jnp.ones((DIM_HEAD,), jnp.float32), 'Wq': s(ks[3], (INNER, DIM_LAT), DIM_LAT), 'Wkv': s(ks[4], (2 * INNER, DIM_IN), DIM_IN), 'Wlkv': s(ks[5], (2 * INNER, DIM_LAT), DIM_LAT), 'Wo': s(ks[6], (DIM_LAT, INNER), INNER), 'bo': jnp.zeros((DIM_LAT,), jnp.float32)}
    _L3_xattn_all = _L3_xattn_setup()
    _L3_xattn_in = {k: v for k, v in _L3_xattn_all.items() if k in ('ln_x_g', 'ln_x_b', 'ln_l_g', 'ln_l_b', 'qn_g', 'kn_g', 'Wq', 'Wkv', 'Wlkv', 'Wo', 'bo')}
    del _L3_xattn_all

    def _L3_ffn_setup():
        import jax, jax.numpy as jnp
        import numpy as np
        import math
        N_EXP = 8
        TOP_K = 2
        CAPACITY_FACTOR = 1.25

        def _capacity(num_tokens):
            cap = math.floor(TOP_K * CAPACITY_FACTOR * num_tokens / N_EXP)
            cap += cap % 2
            return int(cap)
        key = jax.random.key(seed)
        k1, k2, k3, k4 = jax.random.split(key, 4)
        B, C, d = (4, 128, 128)
        x = jax.random.normal(k1, (B, C, d), dtype=jnp.float32)
        w_g = jax.random.normal(k2, (d, N_EXP), dtype=jnp.float32) * 0.02
        c_fc = jax.random.normal(k3, (N_EXP, d, 4 * d), dtype=jnp.float32) * 0.02
        c_proj = jax.random.normal(k4, (N_EXP, 4 * d, d), dtype=jnp.float32) * 0.02
        return {'x': x, 'w_g': w_g, 'c_fc': c_fc, 'c_proj': c_proj}
    _L3_ffn_all = _L3_ffn_setup()
    _L3_ffn_in = {k: v for k, v in _L3_ffn_all.items() if k in ('w_g', 'c_fc', 'c_proj')}
    del _L3_ffn_all
    return {'x': x, 'ctx_768': ctx_768, 'mask_BxS_bf1': mask_BxS_bf1, 'mask_BxS2_bf1': mask_BxS2_bf1, 'mask_BxS2_bk0': mask_BxS2_bk0, 'L0_attn_Wq': _L0_attn_in['Wq'], 'L0_attn_Wk': _L0_attn_in['Wk'], 'L0_attn_Wv': _L0_attn_in['Wv'], 'L0_attn_Wo': _L0_attn_in['Wo'], 'L0_xattn_Wq': _L0_xattn_in['Wq'], 'L0_xattn_Wk': _L0_xattn_in['Wk'], 'L0_xattn_Wv': _L0_xattn_in['Wv'], 'L0_xattn_Wout': _L0_xattn_in['Wout'], 'L0_xattn_bout': _L0_xattn_in['bout'], 'L0_ffn_router_w': _L0_ffn_in['router_w'], 'L0_ffn_w1': _L0_ffn_in['w1'], 'L0_ffn_b1': _L0_ffn_in['b1'], 'L0_ffn_w2': _L0_ffn_in['w2'], 'L0_ffn_b2': _L0_ffn_in['b2'], 'L1_attn_Wq': _L1_attn_in['Wq'], 'L1_attn_Wk': _L1_attn_in['Wk'], 'L1_attn_Wv': _L1_attn_in['Wv'], 'L1_attn_proj_w': _L1_attn_in['proj_w'], 'L1_attn_proj_b': _L1_attn_in['proj_b'], 'L1_xattn_Wq': _L1_xattn_in['Wq'], 'L1_xattn_Wk': _L1_xattn_in['Wk'], 'L1_xattn_Wv': _L1_xattn_in['Wv'], 'L1_xattn_W_film_in': _L1_xattn_in['W_film_in'], 'L1_xattn_b_film_in': _L1_xattn_in['b_film_in'], 'L1_xattn_W_film_out': _L1_xattn_in['W_film_out'], 'L1_xattn_b_film_out': _L1_xattn_in['b_film_out'], 'L1_xattn_g_norm_in': _L1_xattn_in['g_norm_in'], 'L1_xattn_b_norm_in': _L1_xattn_in['b_norm_in'], 'L1_xattn_g_norm_out': _L1_xattn_in['g_norm_out'], 'L1_xattn_b_norm_out': _L1_xattn_in['b_norm_out'], 'L1_xattn_g_ffn': _L1_xattn_in['g_ffn'], 'L1_xattn_b_ffn': _L1_xattn_in['b_ffn'], 'L1_xattn_W1': _L1_xattn_in['W1'], 'L1_xattn_b1': _L1_xattn_in['b1'], 'L1_xattn_W2': _L1_xattn_in['W2'], 'L1_xattn_b2': _L1_xattn_in['b2'], 'L1_xattn_log_dt': _L1_xattn_in['log_dt'], 'L1_xattn_A_re': _L1_xattn_in['A_re'], 'L1_xattn_A_im': _L1_xattn_in['A_im'], 'L1_xattn_C_re': _L1_xattn_in['C_re'], 'L1_xattn_C_im': _L1_xattn_in['C_im'], 'L1_xattn_D_skip': _L1_xattn_in['D_skip'], 'L1_xattn_mod_gate': _L1_xattn_in['mod_gate'], 'L1_ffn_wqkv': _L1_ffn_in['wqkv'], 'L1_ffn_q_scale': _L1_ffn_in['q_scale'], 'L1_ffn_k_scale': _L1_ffn_in['k_scale'], 'L1_ffn_wo': _L1_ffn_in['wo'], 'L1_ffn_ln_g': _L1_ffn_in['ln_g'], 'L1_ffn_ln_b': _L1_ffn_in['ln_b'], 'L1_ffn_w1': _L1_ffn_in['w1'], 'L1_ffn_b1': _L1_ffn_in['b1'], 'L1_ffn_w2': _L1_ffn_in['w2'], 'L1_ffn_b2': _L1_ffn_in['b2'], 'L2_attn_Wq': _L2_attn_in['Wq'], 'L2_attn_bq': _L2_attn_in['bq'], 'L2_attn_Wk': _L2_attn_in['Wk'], 'L2_attn_bk': _L2_attn_in['bk'], 'L2_attn_Wv': _L2_attn_in['Wv'], 'L2_attn_bv': _L2_attn_in['bv'], 'L2_attn_Wo': _L2_attn_in['Wo'], 'L2_attn_bo': _L2_attn_in['bo'], 'L2_attn_rel_k_emb': _L2_attn_in['rel_k_emb'], 'L2_attn_rel_v_emb': _L2_attn_in['rel_v_emb'], 'L2_xattn_Wq': _L2_xattn_in['Wq'], 'L2_xattn_Wk': _L2_xattn_in['Wk'], 'L2_xattn_Wv': _L2_xattn_in['Wv'], 'L2_xattn_Wo': _L2_xattn_in['Wo'], 'L2_ffn_gate_w': _L2_ffn_in['gate_w'], 'L2_ffn_w1': _L2_ffn_in['w1'], 'L2_ffn_w2': _L2_ffn_in['w2'], 'L3_attn_Wq_down': _L3_attn_in['Wq_down'], 'L3_attn_Wk_down': _L3_attn_in['Wk_down'], 'L3_attn_Wv_down': _L3_attn_in['Wv_down'], 'L3_attn_Wq_up_c': _L3_attn_in['Wq_up_c'], 'L3_attn_Wq_up_e': _L3_attn_in['Wq_up_e'], 'L3_attn_Wk_up_c': _L3_attn_in['Wk_up_c'], 'L3_attn_Wk_up_e': _L3_attn_in['Wk_up_e'], 'L3_attn_Wv_up': _L3_attn_in['Wv_up'], 'L3_attn_Wc': _L3_attn_in['Wc'], 'L3_xattn_ln_x_g': _L3_xattn_in['ln_x_g'], 'L3_xattn_ln_x_b': _L3_xattn_in['ln_x_b'], 'L3_xattn_ln_l_g': _L3_xattn_in['ln_l_g'], 'L3_xattn_ln_l_b': _L3_xattn_in['ln_l_b'], 'L3_xattn_qn_g': _L3_xattn_in['qn_g'], 'L3_xattn_kn_g': _L3_xattn_in['kn_g'], 'L3_xattn_Wq': _L3_xattn_in['Wq'], 'L3_xattn_Wkv': _L3_xattn_in['Wkv'], 'L3_xattn_Wlkv': _L3_xattn_in['Wlkv'], 'L3_xattn_Wo': _L3_xattn_in['Wo'], 'L3_xattn_bo': _L3_xattn_in['bo'], 'L3_ffn_w_g': _L3_ffn_in['w_g'], 'L3_ffn_c_fc': _L3_ffn_in['c_fc'], 'L3_ffn_c_proj': _L3_ffn_in['c_proj']}

def reference(x, ctx_768, mask_BxS_bf1, mask_BxS2_bf1, mask_BxS2_bk0, L0_attn_Wq, L0_attn_Wk, L0_attn_Wv, L0_attn_Wo, L0_xattn_Wq, L0_xattn_Wk, L0_xattn_Wv, L0_xattn_Wout, L0_xattn_bout, L0_ffn_router_w, L0_ffn_w1, L0_ffn_b1, L0_ffn_w2, L0_ffn_b2, L1_attn_Wq, L1_attn_Wk, L1_attn_Wv, L1_attn_proj_w, L1_attn_proj_b, L1_xattn_Wq, L1_xattn_Wk, L1_xattn_Wv, L1_xattn_W_film_in, L1_xattn_b_film_in, L1_xattn_W_film_out, L1_xattn_b_film_out, L1_xattn_g_norm_in, L1_xattn_b_norm_in, L1_xattn_g_norm_out, L1_xattn_b_norm_out, L1_xattn_g_ffn, L1_xattn_b_ffn, L1_xattn_W1, L1_xattn_b1, L1_xattn_W2, L1_xattn_b2, L1_xattn_log_dt, L1_xattn_A_re, L1_xattn_A_im, L1_xattn_C_re, L1_xattn_C_im, L1_xattn_D_skip, L1_xattn_mod_gate, L1_ffn_wqkv, L1_ffn_q_scale, L1_ffn_k_scale, L1_ffn_wo, L1_ffn_ln_g, L1_ffn_ln_b, L1_ffn_w1, L1_ffn_b1, L1_ffn_w2, L1_ffn_b2, L2_attn_Wq, L2_attn_bq, L2_attn_Wk, L2_attn_bk, L2_attn_Wv, L2_attn_bv, L2_attn_Wo, L2_attn_bo, L2_attn_rel_k_emb, L2_attn_rel_v_emb, L2_xattn_Wq, L2_xattn_Wk, L2_xattn_Wv, L2_xattn_Wo, L2_ffn_gate_w, L2_ffn_w1, L2_ffn_w2, L3_attn_Wq_down, L3_attn_Wk_down, L3_attn_Wv_down, L3_attn_Wq_up_c, L3_attn_Wq_up_e, L3_attn_Wk_up_c, L3_attn_Wk_up_e, L3_attn_Wv_up, L3_attn_Wc, L3_xattn_ln_x_g, L3_xattn_ln_x_b, L3_xattn_ln_l_g, L3_xattn_ln_l_b, L3_xattn_qn_g, L3_xattn_kn_g, L3_xattn_Wq, L3_xattn_Wkv, L3_xattn_Wlkv, L3_xattn_Wo, L3_xattn_bo, L3_ffn_w_g, L3_ffn_c_fc, L3_ffn_c_proj):
    import jax
    import jax.numpy as jnp

    def _L0_attn_ref(x, Wq, Wk, Wv, Wo):
        import jax, jax.numpy as jnp
        import numpy as np
        DIM, HEADS, K = (128, 16, 64)
        b, n, d = x.shape
        h, dk = (HEADS, K)
        q = (x @ Wq).reshape(b, n, h, dk)
        k = (x @ Wk).reshape(b, n, h, dk)
        v = (x @ Wv).reshape(b, n, h, dk)
        k_sm = jax.nn.softmax(k, axis=1)
        qk = jnp.einsum('bnhd,bnhe->bhde', q, k_sm)
        qkv = jnp.einsum('bhde,bnhe->bnhd', qk, v)
        out = qkv.reshape(b, n, h * dk)
        return out @ Wo

    def _L0_xattn_ref(x, context, Wq, Wk, Wv, Wout, bout):
        import jax, jax.numpy as jnp
        import numpy as np
        HEADS = 8
        DIM_HEAD = 64
        SCALE = DIM_HEAD ** (-0.5)
        b, n, _ = x.shape
        m = context.shape[1]
        q = (x @ Wq).reshape(b, n, HEADS, DIM_HEAD)
        k = (context @ Wk).reshape(b, m, HEADS, DIM_HEAD)
        v = (context @ Wv).reshape(b, m, HEADS, DIM_HEAD)
        sim = jnp.einsum('bihd,bjhd->bhij', q, k) * SCALE
        attn = jax.nn.softmax(sim, axis=-1)
        out = jnp.einsum('bhij,bjhd->bihd', attn, v).reshape(b, n, HEADS * DIM_HEAD)
        return out @ Wout + bout

    def _L0_ffn_ref(x, router_w, w1, b1, w2, b2):
        import jax, jax.numpy as jnp
        import numpy as np
        DIM = 128
        NUM_EXPERTS = 8
        HIDDEN = 512
        CAP_FACTOR = 2.0
        B, S = (4, 256)
        Bz, Sz, Dz = x.shape
        E = router_w.shape[0]
        capacity = max(1, int(Sz * CAP_FACTOR / E) + 1)
        scores = jax.nn.softmax(jnp.einsum('bsd,ed->bse', x, router_w), axis=-1)
        scores_t = jnp.swapaxes(scores, 1, 2)
        gate_vals, sel_idx = jax.lax.top_k(scores_t, capacity)
        b_idx = jnp.arange(Bz)[:, None, None]
        tokens = x[b_idx, sel_idx]
        h = jnp.einsum('becd,edh->bech', tokens, w1) + b1[None, :, None, :]
        h = jax.nn.gelu(h, approximate=False)
        y = jnp.einsum('bech,ehd->becd', h, w2) + b2[None, :, None, :]
        gated = y * gate_vals[..., None]
        out = jnp.zeros_like(x).at[b_idx, sel_idx].add(gated)
        return out

    def _L1_attn_ref(x, Wq, Wk, Wv, proj_w, proj_b):
        import jax, jax.numpy as jnp
        import numpy as np
        B, T, E = (4, 256, 128)
        H, HS = (16, 64)
        b, t, e = x.shape
        h, _, hs = Wq.shape
        q = jnp.einsum('bxy,iyk->bxik', x, Wq).reshape(h, b, t, hs)
        k = jnp.einsum('bxy,iyk->bxik', x, Wk).reshape(h, b, t, hs)
        v = jnp.einsum('bxy,iyk->bxik', x, Wv).reshape(h, b, t, hs)
        wei = jnp.einsum('hbqd,hbkd->hbqk', q, k) * hs ** (-0.5)
        causal = jnp.tril(jnp.ones((t, t), dtype=bool))
        wei = jnp.where(causal, wei, -jnp.inf)
        wei = jax.nn.softmax(wei, axis=-1)
        out = jnp.einsum('hbqk,hbkd->hbqd', wei, v)
        out = out.reshape(b, t, h * hs)
        out = out @ proj_w.T + proj_b
        return out

    def _L1_xattn_ref(x_text, x_vision, text_mask, vision_mask, Wq, Wk, Wv, W_film_in, b_film_in, W_film_out, b_film_out, g_norm_in, b_norm_in, g_norm_out, b_norm_out, g_ffn, b_ffn, W1, b1, W2, b2, log_dt, A_re, A_im, C_re, C_im, D_skip, mod_gate):
        import jax, jax.numpy as jnp
        import numpy as np
        B, T, DT, G, DV = (16, 64, 128, 72, 96)
        H, DH = (4, 32)
        INNER = H * DH
        HID = 4 * DT
        N_STATE = 64
        K_TOP = 32

        def layernorm(x, g, b, eps=1e-05):
            m = x.mean(-1, keepdims=True)
            v = x.var(-1, keepdims=True)
            return (x - m) * jax.lax.rsqrt(v + eps) * g + b

        def s4d(x, log_dt, A_re, A_im, C_re, C_im, D_skip):
            Bb, L, D = x.shape
            dt = jnp.exp(log_dt)
            A = A_re + 1j * A_im
            C = C_re + 1j * C_im
            dtA = dt[:, None] * A
            dC = C * (jnp.exp(dtA) - 1.0) / A
            powers = jnp.exp(dtA[:, :, None] * jnp.arange(L))
            K = 2.0 * jnp.einsum('dn,dnl->dl', dC, powers).real
            n = 2 * L
            Kf = jnp.fft.rfft(K, n=n, axis=-1)
            xf = jnp.fft.rfft(x, n=n, axis=1)
            y = jnp.fft.irfft(xf * Kf.T[None], n=n, axis=1)[:, :L]
            return y + x * D_skip
        Bb, Tt, D = x_text.shape
        Gg = x_vision.shape[1]
        Q = (x_text @ Wq).reshape(Bb, Tt, H, DH)
        K = (x_vision @ Wk).reshape(Bb, Gg, H, DH)
        scores = jnp.einsum('bthd,bghd->bhtg', Q, K) / np.sqrt(DH).astype(np.float32)
        scores = jnp.where(vision_mask[:, None, None, :], scores, -jnp.inf)
        topv, topi = jax.lax.top_k(scores, K_TOP)
        probs = jax.nn.softmax(topv, axis=-1)
        bi = jnp.arange(Bb)[:, None, None, None]
        hi = jnp.arange(H)[None, :, None, None]
        ti = jnp.arange(Tt)[None, None, :, None]
        attn = jnp.zeros_like(scores).at[bi, hi, ti, topi].set(probs)
        attn_mean = attn.mean(axis=1)
        V = x_vision @ Wv
        c_t = jnp.einsum('btg,bgd->btd', attn_mean, V)
        c_t = c_t * text_mask[..., None]
        x = layernorm(x_text, g_norm_in, b_norm_in)
        scale_in, shift_in = jnp.split(c_t @ W_film_in + b_film_in, 2, axis=-1)
        x = x * (1.0 + mod_gate * scale_in) + mod_gate * shift_in
        y = s4d(x, log_dt, A_re, A_im, C_re, C_im, D_skip)
        scale_out, shift_out = jnp.split(c_t @ W_film_out + b_film_out, 2, axis=-1)
        y = y * (1.0 + mod_gate * scale_out) + mod_gate * shift_out
        xt = x_text + y
        h = layernorm(xt, g_ffn, b_ffn)
        h = jax.nn.gelu(h @ W1 + b1, approximate=False) @ W2 + b2
        xt = xt + h
        return layernorm(xt, g_norm_out, b_norm_out)

    def _L1_ffn_ref(x, wqkv, q_scale, k_scale, wo, ln_g, ln_b, w1, b1, w2, b2):
        import jax, jax.numpy as jnp
        import numpy as np
        DIM = 128
        DEPTH = 2
        HEADS = 8
        DIM_HEAD = 64
        WINDOW = 64
        INNER = HEADS * DIM_HEAD
        HID = int(DIM * 4 * 2 / 3)
        B, N = (2, 1024)
        QK_SCALE = 8.0

        def shift_token(t):
            t1, t2 = jnp.split(t, 2, axis=-1)
            t2 = jnp.pad(t2, ((0, 0), (1, 0), (0, 0)))[:, :-1]
            return jnp.concatenate([t1, t2], axis=-1)

        def l2norm(t):
            return t / jnp.clip(jnp.linalg.norm(t, axis=-1, keepdims=True), 1e-12)

        def rotate_half(x):
            x1, x2 = jnp.split(x, 2, axis=-1)
            return jnp.concatenate([-x2, x1], axis=-1)

        def rotary_xpos(q, k):
            n = q.shape[-2]
            half_idx = jnp.arange(0, DIM_HEAD, 2, dtype=jnp.float32)
            inv_freq = 1.0 / 10000.0 ** (half_idx / DIM_HEAD)
            t = jnp.arange(n, dtype=jnp.float32)
            freqs = t[:, None] * inv_freq[None, :]
            freqs = jnp.concatenate([freqs, freqs], axis=-1)
            base = (half_idx + 0.4 * DIM_HEAD) / (1.4 * DIM_HEAD)
            power = (t - n // 2) / float(WINDOW // 2)
            scale = base[None, :] ** power[:, None]
            scale = jnp.concatenate([scale, scale], axis=-1)
            cos, sin = (jnp.cos(freqs), jnp.sin(freqs))
            q = q * cos * scale + rotate_half(q) * sin * scale
            k = k * cos / scale + rotate_half(k) * sin / scale
            return (q, k)

        def local_attention(q, k, v):
            b, h, n, d = q.shape
            w = n // WINDOW
            bq = q.reshape(b, h, w, WINDOW, d) * QK_SCALE
            bk = k.reshape(b, h, w, WINDOW, d)
            bv = v.reshape(b, h, w, WINDOW, d)

            def look_around(t):
                p = jnp.pad(t, ((0, 0), (0, 0), (1, 0), (0, 0), (0, 0)))
                return jnp.concatenate([p[:, :, :w], p[:, :, 1:]], axis=3)
            bk, bv = (look_around(bk), look_around(bv))
            bt = jnp.arange(n).reshape(w, WINDOW)
            btp = jnp.pad(bt, ((1, 0), (0, 0)), constant_values=-1)
            btk = jnp.concatenate([btp[:w], btp[1:]], axis=1)
            sim = jnp.einsum('bhwid,bhwjd->bhwij', bq, bk)
            i = bt[:, :, None]
            j = btk[:, None, :]
            mask = (i < j) | (i > j + WINDOW) | (j == -1)
            sim = jnp.where(mask, -jnp.finfo(sim.dtype).max, sim)
            attn = jax.nn.softmax(sim, axis=-1)
            out = jnp.einsum('bhwij,bhwjd->bhwid', attn, bv)
            return out.reshape(b, h, n, d)

        def _layer(x, wqkv, qs, ksc, wo, lg, lb, w1, b1, w2, b2):
            b, n, _ = x.shape
            h = shift_token(x)
            qkv = h @ wqkv
            q, k, v = jnp.split(qkv, 3, axis=-1)
            to_heads = lambda t: t.reshape(b, n, HEADS, DIM_HEAD).transpose(0, 2, 1, 3)
            q, k, v = (to_heads(q), to_heads(k), to_heads(v))
            q = l2norm(q) * qs
            k = l2norm(k) * ksc
            q, k = rotary_xpos(q, k)
            o = local_attention(q, k, v)
            o = o.transpose(0, 2, 1, 3).reshape(b, n, INNER)
            x = x + o @ wo
            h = shift_token(x)
            mu = h.mean(-1, keepdims=True)
            var = h.var(-1, keepdims=True)
            h = (h - mu) / jnp.sqrt(var + 1e-05) * lg + lb
            h = h @ w1 + b1
            a, g = jnp.split(h, 2, axis=-1)
            h = a * jax.nn.gelu(g, approximate=False)
            x = x + h @ w2 + b2
            return x
        for l in range(DEPTH):
            x = _layer(x, wqkv[l], q_scale[l], k_scale[l], wo[l], ln_g[l], ln_b[l], w1[l], b1[l], w2[l], b2[l])
        return x

    def _L2_attn_ref(hidden_states, Wq, bq, Wk, bk, Wv, bv, Wo, bo, rel_k_emb, rel_v_emb):
        import jax, jax.numpy as jnp
        import numpy as np
        NUM_HEADS = 16
        MAX_REL = 128

        def _rel_embeds(table, q_len, k_len):
            dist = jnp.arange(q_len)[:, None] - jnp.arange(k_len)[None, :]
            idx = jnp.clip(dist, -MAX_REL, MAX_REL) + MAX_REL
            return table[idx]
        B, T, E = hidden_states.shape
        H = NUM_HEADS
        D = E // H
        scaling = jnp.sqrt(jnp.asarray(D, hidden_states.dtype))
        q = hidden_states @ Wq.T + bq
        k = hidden_states @ Wk.T + bk
        v = hidden_states @ Wv.T + bv
        qh = q.reshape(B, T, H, D).transpose(0, 2, 1, 3)
        kh = k.reshape(B, T, H, D).transpose(0, 2, 1, 3)
        vh = v.reshape(B, T, H, D).transpose(0, 2, 1, 3)
        score1 = jnp.einsum('bhqd,bhkd->bhqk', qh, kh)
        rel_k = _rel_embeds(rel_k_emb, T, T)
        s2 = jnp.einsum('bhqd,qkd->qbhk', qh, rel_k)
        s2 = s2.reshape(T, H, B, T).transpose(2, 1, 0, 3)
        scores = (score1 + s2) / scaling
        attn = jax.nn.softmax(scores, axis=-1)
        w1 = jnp.einsum('bhqk,bhkd->bhqd', attn, vh)
        rel_v = _rel_embeds(rel_v_emb, T, T)
        se = attn.reshape(B * H, T, T).transpose(1, 0, 2)
        w2 = jnp.einsum('qnk,qkd->qnd', se, rel_v)
        w2 = w2.reshape(T, H, B, D).transpose(2, 1, 0, 3)
        out = (w1 + w2).transpose(0, 2, 1, 3).reshape(B, T, E)
        return out @ Wo.T + bo

    def _L2_xattn_ref(x, context, context_mask, Wq, Wk, Wv, Wo):
        import jax, jax.numpy as jnp
        import numpy as np
        DIM = 128
        CTX_DIM = 96
        HEADS = 16
        B, N, _ = x.shape
        M = context.shape[1]
        hd = DIM // HEADS
        scale = hd ** (-0.5)
        q = (x @ Wq).reshape(B, N, HEADS, hd).transpose(0, 2, 1, 3)
        k = (context @ Wk).reshape(B, M, HEADS, hd).transpose(0, 2, 1, 3)
        v = (context @ Wv).reshape(B, M, HEADS, hd).transpose(0, 2, 1, 3)
        scores = jnp.einsum('bhid,bhjd->bhij', q, k) * scale
        max_neg = -jnp.finfo(scores.dtype).max
        scores = jnp.where(context_mask[:, None, None, :], scores, max_neg)
        attn = jax.nn.softmax(scores, axis=-1)
        out = jnp.einsum('bhij,bhjd->bhid', attn, v)
        out = out.transpose(0, 2, 1, 3).reshape(B, N, DIM)
        return out @ Wo

    def _L2_ffn_ref(x, gate_w, w1, w2):
        import jax, jax.numpy as jnp
        import numpy as np
        TOP_K = 2
        E = gate_w.shape[-1]
        gate_logits = jnp.einsum('bnd,de->bne', x, gate_w)
        gate_probs = jax.nn.softmax(gate_logits, axis=-1)
        top_k_probs, top_k_idx = jax.lax.top_k(gate_probs, TOP_K)
        top_k_weights = top_k_probs / jnp.sum(top_k_probs, axis=-1, keepdims=True)
        comb = jnp.sum(jax.nn.one_hot(top_k_idx, E, dtype=x.dtype) * top_k_weights[..., None], axis=2)
        h = jax.nn.gelu(jnp.einsum('bnd,edf->benf', x, w1))
        expert_out = jnp.einsum('benf,efd->bend', h, w2)
        output = jnp.einsum('bne,bend->bnd', comb, expert_out)
        return output

    def _L3_attn_ref(x, Wq_down, Wk_down, Wv_down, Wq_up_c, Wq_up_e, Wk_up_c, Wk_up_e, Wv_up, Wc):
        import jax, jax.numpy as jnp
        import numpy as np
        import math
        B, T, C = (2, 256, 128)
        H, L = (16, 64)
        DH = C // H
        DHE = DH // 2
        THETA = 10000.0

        def _rope_cache(t, dim):
            inv_freq = 1.0 / THETA ** (jnp.arange(0, dim, 2, dtype=jnp.float32) / dim)
            freqs = jnp.arange(t, dtype=jnp.float32)[:, None] * inv_freq[None, :]
            emb = jnp.concatenate((freqs, freqs), axis=-1)
            return (jnp.cos(emb), jnp.sin(emb))

        def _apply_rope(x, cos, sin):
            x1 = x[..., 0::2]
            x2 = x[..., 1::2]
            rot = jnp.stack((-x2, x1), axis=-1).reshape(x.shape)
            return x * cos[None, None] + rot * sin[None, None]
        b, t, c = x.shape
        q_lat = (x @ Wq_down).reshape(b, t, H, L)
        k_lat = (x @ Wk_down).reshape(b, t, H, L)
        v_lat = (x @ Wv_down).reshape(b, t, H, L)
        q_c = jnp.einsum('bthl,ld->bhtd', q_lat, Wq_up_c)
        q_e = jnp.einsum('bthl,ld->bhtd', q_lat, Wq_up_e)
        k_c = jnp.einsum('bthl,ld->bhtd', k_lat, Wk_up_c)
        k_e = jnp.einsum('bthl,ld->bhtd', k_lat, Wk_up_e)
        v = jnp.einsum('bthl,ld->bhtd', v_lat, Wv_up)
        cos, sin = _rope_cache(t, DHE)
        q = jnp.concatenate([q_c, _apply_rope(q_e, cos, sin)], axis=-1)
        k = jnp.concatenate([k_c, _apply_rope(k_e, cos, sin)], axis=-1)
        scale = 1.0 / math.sqrt(DH)
        scores = jnp.einsum('bhqd,bhkd->bhqk', q, k) * scale
        causal = jnp.tril(jnp.ones((t, t), dtype=bool))
        scores = jnp.where(causal[None, None], scores, -jnp.inf)
        att = jax.nn.softmax(scores, axis=-1)
        y = jnp.einsum('bhqk,bhkd->bhqd', att, v)
        y = y.transpose(0, 2, 1, 3).reshape(b, t, c)
        return y @ Wc

    def _L3_xattn_ref(x, latents, mask, ln_x_g, ln_x_b, ln_l_g, ln_l_b, qn_g, kn_g, Wq, Wkv, Wlkv, Wo, bo):
        import jax, jax.numpy as jnp
        import numpy as np
        DIM_IN, DIM_LAT, DIM_HEAD = (96, 128, 64)
        INNER = max(DIM_LAT, DIM_IN)
        HEADS = INNER // DIM_HEAD
        SCALE = DIM_HEAD ** (-0.5)
        RMS_EPS = 1e-08
        LN_EPS = 1e-05

        def layernorm(x, g, b):
            mu = jnp.mean(x, axis=-1, keepdims=True)
            var = jnp.mean((x - mu) ** 2, axis=-1, keepdims=True)
            return (x - mu) * jax.lax.rsqrt(var + LN_EPS) * g + b

        def rmsnorm(x, gamma):
            norm = jnp.sqrt(jnp.sum(x * x, axis=-1, keepdims=True)) * x.shape[-1] ** (-0.5)
            return x / jnp.maximum(norm, RMS_EPS) * gamma
        b, n, _ = x.shape
        m = latents.shape[1]
        xn = layernorm(x, ln_x_g, ln_x_b)
        ln = layernorm(latents, ln_l_g, ln_l_b)
        q = ln @ Wq.T
        kv = jnp.concatenate([xn @ Wkv.T, ln @ Wlkv.T], axis=1)
        k, v = (kv[..., :INNER], kv[..., INNER:])
        split_heads = lambda t: t.reshape(t.shape[0], t.shape[1], HEADS, DIM_HEAD).transpose(0, 2, 1, 3)
        q, k, v = (split_heads(q), split_heads(k), split_heads(v))
        qn = rmsnorm(q, qn_g) * SCALE
        kn = rmsnorm(k, kn_g)
        attn = jnp.einsum('bhid,bhjd->bhij', qn, kn)
        full_mask = jnp.pad(mask, ((0, 0), (0, m)), constant_values=True)
        attn = jnp.where(full_mask[:, None, None, :], attn, -jnp.finfo(attn.dtype).max)
        attn = jax.nn.softmax(attn, axis=-1)
        out = jnp.einsum('bhij,bhjd->bhid', attn, v)
        out = out.transpose(0, 2, 1, 3).reshape(b, m, INNER)
        return out @ Wo.T + bo

    def _L3_ffn_ref(x, w_g, c_fc, c_proj):
        import jax, jax.numpy as jnp
        import numpy as np
        import math
        N_EXP = 8
        TOP_K = 2
        CAPACITY_FACTOR = 1.25

        def _capacity(num_tokens):
            cap = math.floor(TOP_K * CAPACITY_FACTOR * num_tokens / N_EXP)
            cap += cap % 2
            return int(cap)
        B, C, d = x.shape
        T = B * C
        cap = _capacity(T)
        xt = x.reshape(T, d)
        logits = xt @ w_g
        top_v, top_i = jax.lax.top_k(logits, TOP_K)
        full = jnp.full_like(logits, -jnp.inf)
        full = full.at[jnp.arange(T)[:, None], top_i].set(top_v)
        probs = jax.nn.softmax(full, axis=-1)
        exp_mask = jax.nn.one_hot(top_i, N_EXP, dtype=jnp.int32)
        exp_mask = jnp.transpose(exp_mask, (1, 0, 2))
        exp_rank = jnp.cumsum(exp_mask.reshape(TOP_K * T, N_EXP), axis=0) - 1
        exp_rank = exp_rank.reshape(TOP_K, T, N_EXP)
        exp_mask = exp_mask * (exp_rank < cap).astype(jnp.int32)
        exp_rank = jnp.sum(exp_mask * exp_rank, axis=-1)
        exp_weights = exp_mask.astype(x.dtype) * probs[None]
        rank_oh = jax.nn.one_hot(exp_rank, cap, dtype=x.dtype)
        cb_weight = jnp.einsum('kte,ktc->tec', exp_weights, rank_oh)
        sec_mask = (cb_weight != 0).astype(x.dtype)
        exp_batches = jnp.einsum('tec,td->ecd', sec_mask, xt)
        h = jax.nn.gelu(jnp.einsum('ecd,edf->ecf', exp_batches, c_fc), approximate=False)
        exp_out = jnp.einsum('ecf,efd->ecd', h, c_proj)
        out = cb_weight.reshape(T, N_EXP * cap) @ exp_out.reshape(N_EXP * cap, d)
        return out.reshape(B, C, d)
    x = x + _L0_attn_ref(_layernorm(x, axis=-1), L0_attn_Wq, L0_attn_Wk, L0_attn_Wv, L0_attn_Wo)
    x = x + _L0_xattn_ref(_layernorm(x, axis=-1), ctx_768, L0_xattn_Wq, L0_xattn_Wk, L0_xattn_Wv, L0_xattn_Wout, L0_xattn_bout)
    x = x + _L0_ffn_ref(_layernorm(x, axis=-1), L0_ffn_router_w, L0_ffn_w1, L0_ffn_b1, L0_ffn_w2, L0_ffn_b2)
    x = x + _L1_attn_ref(_layernorm(x, axis=-1), L1_attn_Wq, L1_attn_Wk, L1_attn_Wv, L1_attn_proj_w, L1_attn_proj_b)
    x = x + _L1_xattn_ref(_layernorm(x, axis=-1), ctx_768, mask_BxS_bf1, mask_BxS2_bf1, L1_xattn_Wq, L1_xattn_Wk, L1_xattn_Wv, L1_xattn_W_film_in, L1_xattn_b_film_in, L1_xattn_W_film_out, L1_xattn_b_film_out, L1_xattn_g_norm_in, L1_xattn_b_norm_in, L1_xattn_g_norm_out, L1_xattn_b_norm_out, L1_xattn_g_ffn, L1_xattn_b_ffn, L1_xattn_W1, L1_xattn_b1, L1_xattn_W2, L1_xattn_b2, L1_xattn_log_dt, L1_xattn_A_re, L1_xattn_A_im, L1_xattn_C_re, L1_xattn_C_im, L1_xattn_D_skip, L1_xattn_mod_gate)
    x = x + _L1_ffn_ref(_layernorm(x, axis=-1), L1_ffn_wqkv, L1_ffn_q_scale, L1_ffn_k_scale, L1_ffn_wo, L1_ffn_ln_g, L1_ffn_ln_b, L1_ffn_w1, L1_ffn_b1, L1_ffn_w2, L1_ffn_b2)
    x = x + _L2_attn_ref(_layernorm(x, axis=-1), L2_attn_Wq, L2_attn_bq, L2_attn_Wk, L2_attn_bk, L2_attn_Wv, L2_attn_bv, L2_attn_Wo, L2_attn_bo, L2_attn_rel_k_emb, L2_attn_rel_v_emb)
    x = x + _L2_xattn_ref(_layernorm(x, axis=-1), ctx_768, mask_BxS2_bf1, L2_xattn_Wq, L2_xattn_Wk, L2_xattn_Wv, L2_xattn_Wo)
    x = x + _L2_ffn_ref(_layernorm(x, axis=-1), L2_ffn_gate_w, L2_ffn_w1, L2_ffn_w2)
    x = x + _L3_attn_ref(_layernorm(x, axis=-1), L3_attn_Wq_down, L3_attn_Wk_down, L3_attn_Wv_down, L3_attn_Wq_up_c, L3_attn_Wq_up_e, L3_attn_Wk_up_c, L3_attn_Wk_up_e, L3_attn_Wv_up, L3_attn_Wc)
    x = x + _L3_xattn_ref(ctx_768, _layernorm(x, axis=-1), mask_BxS2_bk0, L3_xattn_ln_x_g, L3_xattn_ln_x_b, L3_xattn_ln_l_g, L3_xattn_ln_l_b, L3_xattn_qn_g, L3_xattn_kn_g, L3_xattn_Wq, L3_xattn_Wkv, L3_xattn_Wlkv, L3_xattn_Wo, L3_xattn_bo)
    x = x + _L3_ffn_ref(_layernorm(x, axis=-1), L3_ffn_w_g, L3_ffn_c_fc, L3_ffn_c_proj)
    return x

_drawn_inputs = setup_inputs


def setup_inputs(seed=0):
    import zlib

    import numpy as np

    out = dict(_drawn_inputs(seed))
    spreads = {'L1_xattn_b_film_in': (0.0, 0.1),
     'L1_xattn_b_film_out': (0.0, 0.341),
     'L1_xattn_g_norm_in': (1.0, 0.2),
     'L1_xattn_b_norm_in': (0.0, 0.1),
     'L1_xattn_g_norm_out': (1.0, 0.2),
     'L1_xattn_b_norm_out': (0.0, 0.1),
     'L1_xattn_g_ffn': (1.0, 0.6),
     'L1_xattn_b_ffn': (0.0, 0.8),
     'L1_xattn_b1': (0.0, 0.8),
     'L1_xattn_b2': (0.0, 0.3),
     'L1_xattn_A_re': (-0.5, 0.6),
     'L1_ffn_q_scale': (1.0, 0.6),
     'L1_ffn_k_scale': (1.0, 0.6),
     'L1_ffn_ln_g': (1.0, 0.6),
     'L1_ffn_ln_b': (0.0, 0.8),
     'L1_ffn_b1': (0.0, 0.8),
     'L1_ffn_b2': (0.0, 0.779),
     'L3_xattn_ln_x_g': (1.0, 0.6),
     'L3_xattn_ln_x_b': (0.0, 2.0),
     'L3_xattn_ln_l_g': (1.0, 0.6),
     'L3_xattn_ln_l_b': (0.0, 1.999),
     'L3_xattn_qn_g': (1.0, 0.6),
     'L3_xattn_kn_g': (1.0, 0.6),
     'L3_xattn_bo': (0.0, 1.854)}
    factors = {'L0_xattn_bout': 5.54,
     'L0_ffn_b1': 8.0,
     'L0_ffn_b2': 7.337,
     'L1_attn_Wq': 8.0,
     'L1_attn_Wk': 8.0,
     'L1_attn_proj_b': 3.052,
     'L1_xattn_Wq': 8.0,
     'L1_xattn_Wk': 8.0,
     'L1_xattn_Wv': 6.272,
     'L1_xattn_W_film_in': 6.247,
     'L1_xattn_W_film_out': 7.598,
     'L1_xattn_W1': 3.962,
     'L1_xattn_W2': 3.474,
     'L1_ffn_wqkv': 2.774,
     'L1_ffn_wo': 2.918,
     'L1_ffn_w1': 7.915,
     'L1_ffn_w2': 7.067,
     'L2_attn_Wq': 8.0,
     'L2_attn_bq': 64.0,
     'L2_attn_Wk': 8.0,
     'L2_attn_bk': 64.0,
     'L2_attn_Wv': 6.41,
     'L2_attn_bv': 32.871,
     'L2_attn_Wo': 8.0,
     'L2_attn_bo': 54.448,
     'L2_attn_rel_k_emb': 60.108,
     'L2_attn_rel_v_emb': 64.0,
     'L3_attn_Wq_down': 8.0,
     'L3_attn_Wk_down': 8.0,
     'L3_attn_Wv_down': 8.0,
     'L3_attn_Wq_up_c': 8.0,
     'L3_attn_Wq_up_e': 8.0,
     'L3_attn_Wk_up_c': 8.0,
     'L3_attn_Wk_up_e': 8.0,
     'L3_attn_Wv_up': 8.0,
     'L3_attn_Wc': 8.0,
     'L3_ffn_w_g': 6.157,
     'L3_ffn_c_fc': 5.473,
     'L3_ffn_c_proj': 5.354,
     'L2_xattn_Wq': 5.862,
     'L2_xattn_Wk': 5.756,
     'L2_ffn_gate_w': 2.81,
     'L2_ffn_w1': 3.072,
     'L2_ffn_w2': 2.691,
     'L3_xattn_Wq': 2.988,
     'L3_xattn_Wkv': 4.729}
    for name, (base, spread) in spreads.items():
        noise = np.random.default_rng([zlib.crc32(name.encode()), seed]).standard_normal(out[name].shape)
        drawn = base * np.exp(spread * noise) if base else spread * noise
        out[name] = jnp.asarray(drawn.astype(out[name].dtype))
    for name, factor in factors.items():
        out[name] = (out[name] * factor).astype(out[name].dtype)
    return out
```

```python
from contextlib import ExitStack

import numpy as np

import concourse.bass as bass
from concourse import mybir

LAYERS = (0, 1, 2, 3, 4, 5, 6, 7, 8, 9, 10, 11)

ALU = mybir.AluOpType
ACT = mybir.ActivationFunctionType
F32 = mybir.dt.float32
AX_X = mybir.AxisListType.X
ds = bass.ds

P = 128
B = 8
PAIRS = B // 2
D = 128
CTX = 96
BANK = 512
BIG = 3.0e38


class Marks:

    def __init__(self, sem, names, base=0):
        self.sem, self.names, self.now, self.base = sem, list(names), 0, base
        assert len(set(self.names)) == len(self.names)

    def turn(self):
        return len(self.names)

    def mark(self, name):
        assert self.names[self.now % len(self.names)] == name, (self.names[self.now % len(self.names)], name)
        self.now += 1
        return 1

    def at(self, name, it=0):
        return (it + 1) * len(self.names) + (self.base + self.names.index(name) + 1)


class Core:

    def __init__(self, nc, ctx):
        self.nc, self.ctx = nc, ctx
        self.ln_sem = {n: self.sem(f"ln_{n}") for n in ("dve", "pool", "pe", "act")}
        self.ln_passed = dict.fromkeys(self.ln_sem, 0)

    def sbuf(self, name, shape, dt=F32):
        return self.ctx.enter_context(self.nc.sbuf_tensor(name, shape, dt))

    def sem(self, name):
        return self.ctx.enter_context(self.nc.semaphore(name))

    def marks(self, name, names):
        return Marks(self.sem(name), names)

    def ln_marks(self, engine, names):
        m = Marks(self.ln_sem[engine], names, self.ln_passed[engine])
        self.ln_passed[engine] += len(m.names)
        return m


class Carve:

    def __init__(self, tensor):
        self.tensor, self.at = tensor, 0

    def take(self, *shape):
        n = int(np.prod(shape))
        ap = self.tensor[:, self.at:self.at + n]
        self.at += n
        assert self.at <= self.tensor.shape[1], self.at
        if len(shape) == 2:
            ap = ap.rearrange("p (a b) -> p a b", a=shape[0])
        if len(shape) == 3:
            ap = ap.rearrange("p (a b c) -> p a b c", a=shape[0], b=shape[1])
        return ap


def layernorm_all(core, tag, src=None, out=None, outT=None, gain=None, bias=None, width=D,
                  turn=True):
    nc = core.nc
    src = core.x if src is None else src
    out = core.xn if out is None else out
    outT = core.xnT if outT is None else outT
    last = ["out1"] if turn else []
    V = core.ln_marks("dve", [f"stat{b}" for b in range(B)] + ["half"] + [f"aggr{b}" for b in range(B)]
                      + ["eps"] + [f"xn{b}" for b in range(B)] + last)
    G = core.ln_marks("pool", ["rstd"])
    T = core.ln_marks("pe", [f"t{b}" for b in range(B)] if turn else [])
    A = core.ln_marks("act", ["out0"] if turn else [])
    st, mv, rstd, ve = core.ln_st, core.ln_mv, core.ln_rstd, core.ln_ve
    with nc.Block(f"{tag}_ln", no_gpsimd_drain=True) as block:

        @block.vector
        def _(dve):
            for b in range(B):
                nc.vector.bn_stats(st[:, b, :], src[:, b, 0:width]).then_inc(V.sem, V.mark(f"stat{b}"))
            nc.vector.memset(ve[:, B:], -0.5).then_inc(V.sem, V.mark("half"))
            for b in range(B):
                dve.wait_ge(V.sem, V.at(f"stat{b}", -1))
                nc.vector.bn_aggr(mv[:, b, :], st[:, b, :]).then_inc(V.sem, V.mark(f"aggr{b}"))
            dve.wait_ge(V.sem, V.at(f"aggr{B - 1}", -1))
            nc.vector.tensor_scalar(ve[:, 0:B], mv[:, :, 1], 1e-5, None, ALU.add).then_inc(V.sem, V.mark("eps"))
            dve.wait_ge(G.sem, G.at("rstd", -1))
            for b in range(B):
                nc.vector.tensor_scalar(out[:, b, 0:width], src[:, b, 0:width], mv[:, b, 0:1], rstd[:, b:b + 1],
                                        ALU.subtract, ALU.mult).then_inc(V.sem, V.mark(f"xn{b}"))
            if not turn:
                return
            dve.wait_ge(T.sem, T.at(f"t{B - 1}", -1))
            if gain is None:
                v = nc.vector.tensor_copy(outT[0:width, BANK:], core.ps[1][0:width, :])
            else:
                v = nc.vector.tensor_scalar(outT[0:width, BANK:], core.ps[1][0:width, :], gain, bias,
                                            ALU.mult, ALU.add)
            v.then_inc(V.sem, V.mark("out1"))

        @block.gpsimd
        def _(pool):
            pool.wait_ge(V.sem, V.at("eps", -1))
            nc.gpsimd.tensor_tensor(rstd[:, :], ve[:, 0:B], ve[:, B:], ALU.pow).then_inc(G.sem, G.mark("rstd"))

        @block.tensor
        def _(pe):
            for b in range(B if turn else 0):
                pe.wait_ge(V.sem, V.at(f"xn{b}", -1))
                nc.tensor.transpose(core.ps[b // 4][0:width, (b % 4) * P:(b % 4 + 1) * P], out[:, b, 0:width],
                                    core.ident[:, :]).then_inc(T.sem, T.mark(f"t{b}"))

        @block.scalar
        def _(act):
            if not turn:
                return
            act.wait_ge(T.sem, T.at("t3", -1))
            if gain is None:
                a = nc.scalar.copy(outT[0:width, 0:BANK], core.ps[0][0:width, :])
            else:
                a = nc.scalar.activation(outT[0:width, 0:BANK], core.ps[0][0:width, :], ACT.Identity,
                                         bias=bias, scale=gain)
            a.then_inc(A.sem, A.mark("out0"))


class Softmax:

    def __init__(self, core, c, groups, keys, V, A, G, T, banks_s, banks_t, mask=None):
        self.core, self.nc, self.groups, self.keys = core, core.nc, groups, keys
        self.V, self.A, self.G, self.T = V, A, G, T
        self.banks_s, self.banks_t, self.mask = banks_s, banks_t, mask
        self.ahead = len(banks_s)
        self.hd = BANK // keys
        self.prob = c.take(self.ahead, BANK)
        self.probT = c.take(2, BANK)
        self.masked = c.take(self.ahead, BANK) if mask is not None else None
        self.top = c.take(self.ahead, self.hd)
        self.total = c.take(self.ahead, self.hd)
        self.inv = c.take(self.ahead, self.hd)

    def marks_dve(self, g):
        return ([f"mask{g}"] if self.mask is not None else []) + [f"max{g}"]

    def before(self, m, name, g, it):
        return m.at(f"{name}{g % len(self.groups)}", it if g >= 0 else it - 1)

    def pe_scores(self, pe, it, g):
        nc, grp, u = self.nc, self.groups[g], g % self.ahead
        if self.mask is not None:
            pe.wait_ge(self.V.sem, self.before(self.V, "mask", g - self.ahead, it))
        else:
            pe.wait_ge(self.A.sem, self.before(self.A, "exp", g - self.ahead, it))
        bank = self.core.ps[self.banks_s[u]]
        for j, (q, k) in enumerate(zip(grp["q"], grp["k"])):
            mm = nc.tensor.matmul(bank[:, j * self.keys:(j + 1) * self.keys], q, k, start=True, stop=True)
        mm.then_inc(self.T.sem, self.T.mark(f"s{g}"))

    def dve_max(self, dve, it, g):
        nc, u = self.nc, g % self.ahead
        dve.wait_ge(self.T.sem, self.T.at(f"s{g}", it))
        src = self.core.ps[self.banks_s[u]][:, :]
        dve.wait_ge(self.A.sem, self.before(self.A, "exp", g - self.ahead, it))
        if self.mask is not None:
            nc.vector.tensor_tensor(self.masked[:, u, :].rearrange("p (h k) -> p h k", h=self.hd),
                                    src.rearrange("p (h k) -> p h k", h=self.hd),
                                    self.mask(g),
                                    ALU.add).then_inc(self.V.sem, self.V.mark(f"mask{g}"))
            dve.wait_ge(self.V.sem, self.V.at(f"mask{g}", it))
            src = self.masked[:, u, :]
        nc.vector.tensor_reduce(self.top[:, u, :], src.rearrange("p (h k) -> p h k", h=self.hd), AX_X,
                                ALU.max, negate=True).then_inc(self.V.sem, self.V.mark(f"max{g}"))

    def act_exp(self, act, it, g):
        nc, u = self.nc, g % self.ahead
        act.wait_ge(self.V.sem, self.V.at(f"max{g}", it))
        act.wait_ge(self.T.sem, self.before(self.T, "t", g - self.ahead, it))
        src = self.masked[:, u, :] if self.mask is not None else self.core.ps[self.banks_s[u]][:, :]
        for j in range(self.hd):
            sl = slice(j * self.keys, (j + 1) * self.keys)
            e = nc.scalar.activation(self.prob[:, u, sl], src[:, sl], ACT.Exp, bias=self.top[:, u, j:j + 1],
                                     accum_out=self.total[:, u, j:j + 1])
        e.then_inc(self.A.sem, self.A.mark(f"exp{g}"))

    def dve_recip(self, dve, it, g):
        u = g % self.ahead
        dve.wait_ge(self.A.sem, self.A.at(f"exp{g}", it))
        dve.wait_ge(self.G.sem, self.before(self.G, "norm", g - self.ahead, it))
        self.nc.vector.reciprocal(self.inv[:, u, :], self.total[:, u, :]) \
            .then_inc(self.V.sem, self.V.mark(f"inv{g}"))

    def pool_norm(self, pool, it, g):
        u = g % self.ahead
        pool.wait_ge(self.V.sem, self.V.at(f"inv{g}", it))
        v = self.prob[:, u, :].rearrange("p (h k) -> p h k", h=self.hd)
        self.nc.gpsimd.tensor_tensor(v, v, self.inv[:, u, :].unsqueeze(2).broadcast_to([P, self.hd, self.keys]),
                                     ALU.mult).then_inc(self.G.sem, self.G.mark(f"norm{g}"))

    def pe_turn(self, pe, it, g):
        pe.wait_ge(self.G.sem, self.G.at(f"norm{g}", it))
        pe.wait_ge(self.V.sem, self.before(self.V, "pT", g - 2, it))
        bank = self.core.ps[self.banks_t[g % 2]]
        for j in range(BANK // P):
            mm = self.nc.tensor.transpose(bank[:, j * P:(j + 1) * P], self.prob[:, g % self.ahead, j * P:(j + 1) * P],
                                          self.core.ident[:, :])
        mm.then_inc(self.T.sem, self.T.mark(f"t{g}"))

    def dve_copy(self, dve, it, g):
        u = g % 2
        dve.wait_ge(self.T.sem, self.T.at(f"t{g}", it))
        dve.wait_ge(self.T.sem, self.before(self.T, "o", g - 2, it))
        self.nc.vector.tensor_copy(self.probT[:, u, :], self.core.ps[self.banks_t[u]][:, :]) \
            .then_inc(self.V.sem, self.V.mark(f"pT{g}"))

    def pe_values(self, pe, it, g):
        u, grp = g % 2, self.groups[g]
        pe.wait_ge(self.V.sem, self.V.at(f"pT{g}", it))
        blocks = self.keys // P
        for j in range(self.hd):
            for kb in range(blocks):
                i = j * blocks + kb
                mm = self.nc.tensor.matmul(grp["o"][j], grp["v"][i], self.probT[:, u, i * P:(i + 1) * P],
                                           start=(kb == 0), stop=(kb == blocks - 1))
        mm.then_inc(self.T.sem, self.T.mark(f"o{g}"))

    def names(self):
        n, ahead = len(self.groups), self.ahead
        t, v = [f"s{g}" for g in range(ahead)], []
        for g in range(ahead):
            v += self.marks_dve(g)
        for g in range(n):
            t += ([f"s{g + ahead}"] if g + ahead < n else []) + [f"t{g}"] + ([f"o{g - 1}"] if g > 0 else [])
            v += [f"inv{g}"] + (self.marks_dve(g + ahead) if g + ahead < n else []) + ([f"pT{g - 1}"] if g > 0 else [])
        return (v + [f"pT{n - 1}"], [f"exp{g}" for g in range(n)], [f"norm{g}" for g in range(n)],
                t + [f"o{n - 1}"])

    def run_pe(self, pe, it, before_turns=None, before_values=None):
        n = len(self.groups)
        for g in range(self.ahead):
            self.pe_scores(pe, it, g)
        if before_turns is not None:
            before_turns()
        for g in range(n + 1):
            if g + self.ahead < n:
                self.pe_scores(pe, it, g + self.ahead)
            if g < n:
                self.pe_turn(pe, it, g)
            if g > 0:
                if before_values is not None:
                    before_values(g - 1)
                self.pe_values(pe, it, g - 1)

    def run_dve(self, dve, it):
        n = len(self.groups)
        for g in range(self.ahead):
            self.dve_max(dve, it, g)
        for g in range(n + 1):
            if g < n:
                self.dve_recip(dve, it, g)
            if g + self.ahead < n:
                self.dve_max(dve, it, g + self.ahead)
            if g > 0:
                self.dve_copy(dve, it, g - 1)

    def run_act(self, act, it):
        for g in range(len(self.groups)):
            self.act_exp(act, it, g)

    def run_pool(self, pool, it):
        for g in range(len(self.groups)):
            self.pool_norm(pool, it, g)


def for_heads(bias, n=4):
    return bias.unsqueeze(1).broadcast_to([bias.shape[0], n, bias.shape[1]])


def names_of(groups, masked, ahead):
    probe = Softmax.__new__(Softmax)
    probe.groups, probe.mask, probe.ahead = [None] * groups, (True if masked else None), ahead
    return probe.names()


def layer_l0_xattn(core, tag, w):
    nc, ps = core.nc, core.ps
    H, K = 8, 64
    CH = H * K // P
    c = Carve(core.scratch)
    wq, wk, wv = w.take(H * K), w.take(H * K), w.take(H * K)
    wo, bo = w.take(CH, D), w.take(D)
    qT, kT, v = c.take(CH, 2 * P), c.take(CH, 2 * P), c.take(2, H * K)
    ctx2, oT = c.take(2 * P), c.take(2, BANK)
    vs, as_, gs, ts = names_of(4, False, 4)
    V = core.marks(f"{tag}_dve", ["k0", "k1", "v1"] + vs + ["x0", "x1"])
    A = core.marks(f"{tag}_act", ["q0", "q1", "v0"] + as_ + ["oT0", "oT1"])
    G = core.marks(f"{tag}_pool", ["ctx"] + gs)
    T = core.marks(f"{tag}_pe", ["q0", "q1", "k0", "k1", "v0", "v1"] + ts + ["y0", "y1"])
    groups = []
    for u in range(2):
        for par in range(2):
            rows, tok = slice(K * par, K * par + K), slice(u * P, u * P + P)
            groups.append(dict(
                q=[qT[rows, i, tok] for i in range(CH)], k=[kT[rows, i, tok] for i in range(CH)],
                v=[v[:, u, (2 * i + par) * K:(2 * i + par + 1) * K] for i in range(CH)],
                o=[ps[2 + u][rows, i * P:(i + 1) * P] for i in range(CH)]))
    sm = Softmax(core, c, groups, P, V, A, G, T, (6, 7, 4, 5), (0, 1))
    layernorm_all(core, tag)
    with nc.Block(tag, no_gpsimd_drain=True) as block:

        @block.gpsimd
        def _(pool):
            pool.sem_inc(G.sem, G.turn())
            with pool.Fori(0, PAIRS) as it:
                pool.wait_ge(T.sem, T.at("v1", it - 1))
                nc.gpsimd.tensor_copy(ctx2[:CTX, :], core.ctxT[:CTX, ds(it * 2 * P, 2 * P)]) \
                    .then_inc(G.sem, G.mark("ctx"))
                sm.run_pool(pool, it)

        @block.tensor
        def _(pe):
            pe.sem_inc(T.sem, T.turn())
            pe.wait_ge(*core.w_loaded[tag])
            with pe.Fori(0, PAIRS) as it:
                for half in range(2):
                    pe.wait_ge(V.sem, V.at("pT3", it - 1))
                    for i in range(2):
                        mm = nc.tensor.matmul(ps[half][:, i * 2 * P:(i + 1) * 2 * P],
                                              wq[:, (2 * half + i) * P:(2 * half + i + 1) * P],
                                              core.xnT[:, ds(it * 2 * P, 2 * P)], start=True, stop=True)
                    mm.then_inc(T.sem, T.mark(f"q{half}"))
                for half in range(2):
                    pe.wait_ge(A.sem, A.at(f"oT{half}", it - 1))
                    for i in range(2):
                        mm = nc.tensor.matmul(ps[2 + half][:, i * 2 * P:(i + 1) * 2 * P],
                                              wk[:CTX, (2 * half + i) * P:(2 * half + i + 1) * P],
                                              core.ctxT[:CTX, ds(it * 2 * P, 2 * P)], start=True, stop=True)
                    mm.then_inc(T.sem, T.mark(f"k{half}"))
                pe.wait_ge(G.sem, G.at("ctx", it))
                for u in range(2):
                    pe.wait_ge(V.sem, V.at(f"x{u}", it - 1))
                    nc.tensor.matmul(ps[4 + u][:, :], ctx2[:CTX, u * P:(u + 1) * P], wv[:CTX, :],
                                     start=True, stop=True).then_inc(T.sem, T.mark(f"v{u}"))
                pe.wait_ge(A.sem, A.at("v0", it))
                pe.wait_ge(V.sem, V.at("v1", it))
                sm.run_pe(pe, it)
                for u in range(2):
                    pe.wait_ge(A.sem, A.at(f"oT{u}", it))
                    for i in range(CH):
                        nc.tensor.matmul(ps[4 + u][:, 0:D], oT[:, u, i * P:(i + 1) * P], wo[:, i, :],
                                         start=(i == 0), stop=False)
                    nc.tensor.matmul(ps[4 + u][:, 0:D], core.ones[0:1, 0:P], bo[0:1, :],
                                     start=False, stop=True).then_inc(T.sem, T.mark(f"y{u}"))

        @block.scalar
        def _(act):
            act.sem_inc(A.sem, A.turn())
            with act.Fori(0, PAIRS) as it:
                for half in range(2):
                    act.wait_ge(T.sem, T.at(f"q{half}", it))
                    nc.scalar.mul(qT[:, 2 * half:2 * half + 2, :].rearrange("p a b -> p (a b)"), ps[half][:, :],
                                  K ** -0.5).then_inc(A.sem, A.mark(f"q{half}"))
                act.wait_ge(T.sem, T.at("v0", it))
                nc.scalar.copy(v[:, 0, :], ps[4][:, :]).then_inc(A.sem, A.mark("v0"))
                sm.run_act(act, it)
                for u in range(2):
                    act.wait_ge(T.sem, T.at(f"o{2 * u + 1}", it))
                    nc.scalar.copy(oT[:, u, :], ps[2 + u][:, :]).then_inc(A.sem, A.mark(f"oT{u}"))

        @block.vector
        def _(dve):
            dve.sem_inc(V.sem, V.turn())
            with dve.Fori(0, PAIRS) as it:
                for half in range(2):
                    dve.wait_ge(T.sem, T.at(f"k{half}", it))
                    nc.vector.tensor_copy(kT[:, 2 * half:2 * half + 2, :].rearrange("p a b -> p (a b)"),
                                          ps[2 + half][:, :]).then_inc(V.sem, V.mark(f"k{half}"))
                dve.wait_ge(T.sem, T.at("v1", it))
                nc.vector.tensor_copy(v[:, 1, :], ps[5][:, :]).then_inc(V.sem, V.mark("v1"))
                sm.run_dve(dve, it)
                for u in range(2):
                    dve.wait_ge(T.sem, T.at(f"y{u}", it))
                    xr = core.x[:, ds(it * 2 + u, 1), :].rearrange("p a d -> p (a d)")
                    nc.vector.tensor_tensor(xr, xr, ps[4 + u][:, 0:D], ALU.add).then_inc(V.sem, V.mark(f"x{u}"))


def small_groups(qT, kT, v, ps, o_banks):
    groups = []
    for u in range(2):
        for j in range(4):
            part, tok = slice(32 * j, 32 * j + 8), slice(u * P, u * P + P)
            groups.append(dict(
                q=[qT[part, i, tok] for i in range(4)], k=[kT[part, i, tok] for i in range(4)],
                v=[v[:, u, (4 * i + j) * 32:(4 * i + j + 1) * 32] for i in range(4)],
                o=[ps[o_banks[u]][32 * j:32 * j + 32, i * P:(i + 1) * P] for i in range(4)]))
    return groups


def layer_l2_xattn(core, tag, w):
    nc, ps = core.nc, core.ps
    c = Carve(core.scratch)
    wq, wk, wv, wo = w.take(BANK), w.take(BANK), w.take(BANK), w.take(4, D)
    qT, kT, v = c.take(4, 2 * P), c.take(4, 2 * P), c.take(2, BANK)
    ctx2, bias2, oT = c.take(2 * P), c.take(2, P), c.take(2, BANK)
    vs, as_, gs, ts = names_of(8, True, 4)
    V = core.marks(f"{tag}_dve", ["k0", "k1", "v1"] + vs + ["x0", "x1"])
    A = core.marks(f"{tag}_act", ["q0", "q1", "v0"] + as_ + ["oT0", "oT1"])
    G = core.marks(f"{tag}_pool", ["ctx", "bias"] + gs)
    T = core.marks(f"{tag}_pe", ["q0", "q1", "k0", "k1", "v0", "v1"] + ts + ["y0", "y1"])
    groups = small_groups(qT, kT, v, ps, (2, 3))
    sm = Softmax(core, c, groups, P, V, A, G, T, (6, 7, 4, 5), (0, 1), mask=lambda g: for_heads(bias2[:, g // 4, :]))
    layernorm_all(core, tag)
    with nc.Block(tag, no_gpsimd_drain=True) as block:

        @block.gpsimd
        def _(pool):
            pool.sem_inc(G.sem, G.turn())
            with pool.Fori(0, PAIRS) as it:
                pool.wait_ge(T.sem, T.at("v1", it - 1))
                nc.gpsimd.tensor_copy(ctx2[:CTX, :], core.ctxT[:CTX, ds(it * 2 * P, 2 * P)]) \
                    .then_inc(G.sem, G.mark("ctx"))
                pool.wait_ge(V.sem, V.at("mask7", it - 1))
                nc.gpsimd.tensor_copy(bias2.rearrange("p a b -> p (a b)"),
                                      core.ctx_bias[:, ds(it * 2 * P, 2 * P)]).then_inc(G.sem, G.mark("bias"))
                sm.run_pool(pool, it)

        @block.tensor
        def _(pe):
            pe.sem_inc(T.sem, T.turn())
            pe.wait_ge(*core.w_loaded[tag])
            with pe.Fori(0, PAIRS) as it:
                for half in range(2):
                    pe.wait_ge(V.sem, V.at("pT7", it - 1))
                    for i in range(2):
                        mm = nc.tensor.matmul(ps[half][:, i * 2 * P:(i + 1) * 2 * P],
                                              wq[:, (2 * half + i) * P:(2 * half + i + 1) * P],
                                              core.xnT[:, ds(it * 2 * P, 2 * P)], start=True, stop=True)
                    mm.then_inc(T.sem, T.mark(f"q{half}"))
                for half in range(2):
                    pe.wait_ge(A.sem, A.at(f"oT{half}", it - 1))
                    for i in range(2):
                        mm = nc.tensor.matmul(ps[2 + half][:, i * 2 * P:(i + 1) * 2 * P],
                                              wk[:CTX, (2 * half + i) * P:(2 * half + i + 1) * P],
                                              core.ctxT[:CTX, ds(it * 2 * P, 2 * P)], start=True, stop=True)
                    mm.then_inc(T.sem, T.mark(f"k{half}"))
                pe.wait_ge(G.sem, G.at("ctx", it))
                for u in range(2):
                    pe.wait_ge(V.sem, V.at(f"x{u}", it - 1))
                    nc.tensor.matmul(ps[4 + u][:, :], ctx2[:CTX, u * P:(u + 1) * P], wv[:CTX, :],
                                     start=True, stop=True).then_inc(T.sem, T.mark(f"v{u}"))
                pe.wait_ge(A.sem, A.at("v0", it))
                pe.wait_ge(V.sem, V.at("v1", it))
                sm.run_pe(pe, it)
                for u in range(2):
                    pe.wait_ge(A.sem, A.at(f"oT{u}", it))
                    for i in range(4):
                        mm = nc.tensor.matmul(ps[4 + u][:, 0:D], oT[:, u, i * P:(i + 1) * P], wo[:, i, :],
                                              start=(i == 0), stop=(i == 3))
                    mm.then_inc(T.sem, T.mark(f"y{u}"))

        @block.scalar
        def _(act):
            act.sem_inc(A.sem, A.turn())
            with act.Fori(0, PAIRS) as it:
                for half in range(2):
                    act.wait_ge(T.sem, T.at(f"q{half}", it))
                    nc.scalar.mul(qT[:, 2 * half:2 * half + 2, :].rearrange("p a b -> p (a b)"), ps[half][:, :],
                                  8 ** -0.5).then_inc(A.sem, A.mark(f"q{half}"))
                act.wait_ge(T.sem, T.at("v0", it))
                nc.scalar.copy(v[:, 0, :], ps[4][:, :]).then_inc(A.sem, A.mark("v0"))
                sm.run_act(act, it)
                for u in range(2):
                    act.wait_ge(T.sem, T.at(f"o{4 * u + 3}", it))
                    nc.scalar.copy(oT[:, u, :], ps[2 + u][:, :]).then_inc(A.sem, A.mark(f"oT{u}"))

        @block.vector
        def _(dve):
            dve.sem_inc(V.sem, V.turn())
            with dve.Fori(0, PAIRS) as it:
                for half in range(2):
                    dve.wait_ge(T.sem, T.at(f"k{half}", it))
                    nc.vector.tensor_copy(kT[:, 2 * half:2 * half + 2, :].rearrange("p a b -> p (a b)"),
                                          ps[2 + half][:, :]).then_inc(V.sem, V.mark(f"k{half}"))
                dve.wait_ge(T.sem, T.at("v1", it))
                nc.vector.tensor_copy(v[:, 1, :], ps[5][:, :]).then_inc(V.sem, V.mark("v1"))
                dve.wait_ge(G.sem, G.at("bias", it))
                sm.run_dve(dve, it)
                for u in range(2):
                    dve.wait_ge(T.sem, T.at(f"y{u}", it))
                    xr = core.x[:, ds(it * 2 + u, 1), :].rearrange("p a d -> p (a d)")
                    nc.vector.tensor_tensor(xr, xr, ps[4 + u][:, 0:D], ALU.add).then_inc(V.sem, V.mark(f"x{u}"))


def layer_l3_attn(core, tag, w):
    nc, ps = core.nc, core.ps
    c = Carve(core.scratch)
    down = [w.take(8, P) for _ in range(3)]
    ups = w.take(5, 8)
    wc = w.take(4, D)
    cosq, sinq, cosk, sink, causal = w.take(P), w.take(P), w.take(P), w.take(P), w.take(P)
    eff = [c.take(BANK) for _ in range(5)]
    qT, kT, v = c.take(4, 2 * P), c.take(4, 2 * P), c.take(2, BANK)
    rot = c.take(4, 2 * P)
    xnT2, oT = c.take(2 * P), c.take(2, BANK)
    vs, as_, gs, ts = names_of(8, True, 4)
    PROJ = ["q", "qs", "k", "ks"]
    V = core.marks(f"{tag}_dve", ["qc0", "qc1", "rs0", "rs1", "qsum", "kc0", "kc1", "ks0", "ks1", "ksum"] + vs + ["x0", "x1"])
    A = core.marks(f"{tag}_act", ["v0", "v1"] + as_ + ["oT0", "oT1"])
    G = core.marks(f"{tag}_pool", ["xn"] + gs)
    T = core.marks(f"{tag}_pe", ["q0", "q1", "qs0", "qs1", "k0", "k1", "ks0", "ks1", "v0", "v1"] + ts + ["y0", "y1"])
    W = core.marks(f"{tag}_eff_pe", [f"e{n}" for n in range(5)])
    E = core.marks(f"{tag}_eff_dve", ["zero"] + [f"e{n}" for n in range(5)])
    groups = small_groups(qT, kT, v, ps, (2, 3))
    sm = Softmax(core, c, groups, P, V, A, G, T, (6, 7, 4, 5), (0, 1), mask=lambda g: for_heads(causal))
    layernorm_all(core, tag)
    with nc.Block(f"{tag}_eff", no_gpsimd_drain=True) as block:

        @block.tensor
        def _(pe):
            pe.wait_ge(*core.w_loaded[tag])
            for n in range(5):
                d = down[(0, 0, 1, 1, 2)[n]]
                for h in range(16):
                    part = slice(64 * (h % 2), 64 * (h % 2) + 64)
                    mm = nc.tensor.matmul(ps[h % 2][:, n * 64 + h // 2 * 8:n * 64 + h // 2 * 8 + 8],
                                          d[part, h // 2, :], ups[part, n, :], start=True, stop=True)
                mm.then_inc(W.sem, W.mark(f"e{n}"))

        @block.vector
        def _(dve):
            nc.vector.memset(c.tensor[:, 0:5 * BANK], 0.0).then_inc(E.sem, E.mark("zero"))
            dve.wait_ge(E.sem, E.at("zero", -1))
            for n in range(5):
                dve.wait_ge(W.sem, W.at("e4", -1))
                for par in range(2):
                    e = nc.vector.tensor_copy(
                        eff[n].rearrange("p (h r s) -> p h r s", r=2, s=32)[:, :, par, 0:8],
                        ps[par][:, n * 64:(n + 1) * 64].rearrange("p (h s) -> p h s", s=8))
                e.then_inc(E.sem, E.mark(f"e{n}"))

    with nc.Block(tag, no_gpsimd_drain=True) as block:

        @block.gpsimd
        def _(pool):
            pool.sem_inc(G.sem, G.turn())
            with pool.Fori(0, PAIRS) as it:
                pool.wait_ge(T.sem, T.at("v1", it - 1))
                nc.gpsimd.tensor_copy(xnT2, core.xnT[:, ds(it * 2 * P, 2 * P)]).then_inc(G.sem, G.mark("xn"))
                sm.run_pool(pool, it)

        @block.tensor
        def _(pe):
            pe.sem_inc(T.sem, T.turn())
            with pe.Fori(0, PAIRS) as it:
                for n, name in enumerate(PROJ):
                    for half in range(2):
                        bank = (0, 2, 4, 6)[n] + half
                        if n == 0:
                            pe.wait_ge(V.sem, V.at(f"pT{6 + half}", it - 1))
                        if n == 1:
                            pe.wait_ge(A.sem, A.at(f"oT{half}", it - 1))
                        if n == 2:
                            pe.wait_ge(V.sem, V.at(f"x{half}", it - 1))
                        if n == 3:
                            pe.wait_ge(V.sem, V.at(f"mask{6 + half}", it - 1))
                        for i in range(2):
                            mm = nc.tensor.matmul(ps[bank][:, i * 2 * P:(i + 1) * 2 * P],
                                                  eff[n][:, (2 * half + i) * P:(2 * half + i + 1) * P],
                                                  core.xnT[:, ds(it * 2 * P, 2 * P)], start=True, stop=True)
                        mm.then_inc(T.sem, T.mark(f"{name}{half}"))
                pe.wait_ge(G.sem, G.at("xn", it))
                for u in range(2):
                    pe.wait_ge(V.sem, V.at(f"qc{u}", it))
                    nc.tensor.matmul(ps[u][:, :], xnT2[:, u * P:(u + 1) * P], eff[4],
                                     start=True, stop=True).then_inc(T.sem, T.mark(f"v{u}"))
                pe.wait_ge(V.sem, V.at("ksum", it))
                pe.wait_ge(A.sem, A.at("v1", it))
                sm.run_pe(pe, it)
                for u in range(2):
                    pe.wait_ge(A.sem, A.at(f"oT{u}", it))
                    for i in range(4):
                        mm = nc.tensor.matmul(ps[4 + u][:, 0:D], oT[:, u, i * P:(i + 1) * P], wc[:, i, :],
                                              start=(i == 0), stop=(i == 3))
                    mm.then_inc(T.sem, T.mark(f"y{u}"))

        @block.scalar
        def _(act):
            act.sem_inc(A.sem, A.turn())
            with act.Fori(0, PAIRS) as it:
                for u in range(2):
                    act.wait_ge(T.sem, T.at(f"v{u}", it))
                    nc.scalar.copy(v[:, u, :], ps[u][:, :]).then_inc(A.sem, A.mark(f"v{u}"))
                sm.run_act(act, it)
                for u in range(2):
                    act.wait_ge(T.sem, T.at(f"o{4 * u + 3}", it))
                    nc.scalar.copy(oT[:, u, :], ps[2 + u][:, :]).then_inc(A.sem, A.mark(f"oT{u}"))

        @block.vector
        def _(dve):
            dve.sem_inc(V.sem, V.turn())

            def rotated(it, dst, base, swapped, banks, names, cos, sin):
                for half in range(2):
                    dve.wait_ge(T.sem, T.at(f"{base}{half}", it))
                    nc.vector.tensor_tensor(dst[:, 2 * half:2 * half + 2, :].rearrange("p a (b t) -> p (a b) t", t=P),
                                            ps[banks[0] + half][:, :].rearrange("p (a t) -> p a t", t=P),
                                            cos.unsqueeze(1).broadcast_to([P, 4, P]),
                                            ALU.mult).then_inc(V.sem, V.mark(f"{names[0]}{half}"))
                for half in range(2):
                    dve.wait_ge(T.sem, T.at(f"{swapped}{half}", it))
                    nc.vector.tensor_tensor(rot[:, 2 * half:2 * half + 2, :].rearrange("p a (b t) -> p (a b) t", t=P),
                                            ps[banks[1] + half][:, :].rearrange("p (a t) -> p a t", t=P),
                                            sin.unsqueeze(1).broadcast_to([P, 4, P]),
                                            ALU.mult).then_inc(V.sem, V.mark(f"{names[1]}{half}"))
                dve.wait_ge(V.sem, V.at(f"{names[1]}1", it))
                nc.vector.tensor_tensor(dst, dst, rot, ALU.add).then_inc(V.sem, V.mark(names[2]))

            with dve.Fori(0, PAIRS) as it:
                rotated(it, qT, "q", "qs", (0, 2), ("qc", "rs", "qsum"), cosq, sinq)
                dve.wait_ge(V.sem, V.at("qsum", it))
                rotated(it, kT, "k", "ks", (4, 6), ("kc", "ks", "ksum"), cosk, sink)
                sm.run_dve(dve, it)
                for u in range(2):
                    dve.wait_ge(T.sem, T.at(f"y{u}", it))
                    xr = core.x[:, ds(it * 2 + u, 1), :].rearrange("p a d -> p (a d)")
                    nc.vector.tensor_tensor(xr, xr, ps[4 + u][:, 0:D], ALU.add).then_inc(V.sem, V.mark(f"x{u}"))


class Link:

    def __init__(self, eng, sem):
        self.eng, self.sem, self.n = eng, sem, 0

    def __call__(self, ins):
        self.n += 1
        ins.then_inc(self.sem, 1)
        self.eng.wait_ge(self.sem, self.n)


def unit(m, name, n, it, units):
    return m.at(f"{name}{n % units}", it if n >= 0 else it - 1)


def mixture(core, tag, c, w1, w2, act_func, gates, b1=None):
    nc, ps, x = core.nc, core.ps, core.x
    E, HC = 8, 4
    U = 4
    wa, wb = [c.take(HC * P) for _ in range(2)], [c.take(HC, D) for _ in range(2)]
    hT = [c.take(HC, BANK) for _ in range(2)]
    gate2, bias2 = c.take(2, B), c.take(2, HC)
    V = core.marks(f"{tag}_dve", [f"acc{n}" for n in range(U)])
    G = core.marks(f"{tag}_pool", ["gate"])
    A = core.marks(f"{tag}_act", [f"h{n}" for n in range(U * HC)])
    T = core.marks(f"{tag}_pe", [m for n in range(U) for m in [f"u{n * HC + i}" for i in range(HC)] + [f"y{n}"]])
    loads = [core.sem(f"{tag}_expert_weights{s}") for s in range(2)]
    with nc.Block(tag, no_gpsimd_drain=True) as block:

        @block.sync
        def _(sp):
            with sp.Fori(0, E // 2) as it:
                for s in range(2):
                    sp.wait_ge(T.sem, T.at(f"y{2 * s + 1}", it - 1))
                    sp.dma_start(wa[s], w1[ds(it * 2 + s, 1)].rearrange("e p f -> p (e f)")).then_inc(loads[s], 16)
                    sp.dma_start(wb[s].rearrange("p c d -> p (c d)"),
                                 w2[ds(it * 2 + s, 1)].rearrange("e p f -> p (e f)")).then_inc(loads[s], 16)

        @block.gpsimd
        def _(pool):
            pool.sem_inc(G.sem, G.turn())
            with pool.Fori(0, E // 2) as it:
                pool.wait_ge(V.sem, V.at(f"acc{U - 1}", it - 1))
                pool.wait_ge(A.sem, A.at(f"h{U * HC - 1}", it - 1))
                if b1 is not None:
                    nc.gpsimd.tensor_copy(bias2, b1[:, ds(it * 2, 2), :])
                nc.gpsimd.tensor_copy(gate2, gates[:, ds(it * 2, 2), :]).then_inc(G.sem, G.mark("gate"))

        @block.tensor
        def _(pe):
            pe.sem_inc(T.sem, T.turn())

            def up(it, n):
                s, half = n // 2, n % 2
                if half == 0:
                    pe.wait_ge(loads[s], it * 32 + 32)
                for i in range(HC):
                    m = n * HC + i
                    pe.wait_ge(A.sem, unit(A, "h", m - 4, it, U * HC))
                    nc.tensor.matmul(ps[m % 4][:, :], wa[s][:, i * P:(i + 1) * P],
                                     core.xnT[:, half * BANK:(half + 1) * BANK], start=True, stop=True) \
                        .then_inc(T.sem, T.mark(f"u{m}"))

            def down(it, n):
                s, half = n // 2, n % 2
                pe.wait_ge(A.sem, A.at(f"h{n * HC + HC - 1}", it))
                pe.wait_ge(V.sem, unit(V, "acc", n - 2, it, U))
                for t in range(4):
                    for i in range(HC):
                        mm = nc.tensor.matmul(ps[4 + half][:, t * P:(t + 1) * P], hT[half][:, i, t * P:(t + 1) * P],
                                              wb[s][:, i, :], start=(i == 0), stop=(i == HC - 1))
                mm.then_inc(T.sem, T.mark(f"y{n}"))

            with pe.Fori(0, E // 2) as it:
                for n in range(U):
                    up(it, n)
                    down(it, n)

        @block.scalar
        def _(act):
            act.sem_inc(A.sem, A.turn())
            with act.Fori(0, E // 2) as it:
                act.wait_ge(G.sem, G.at("gate", it))
                for n in range(U):
                    s, half = n // 2, n % 2
                    act.wait_ge(T.sem, unit(T, "y", n - 2, it, U))
                    for i in range(HC):
                        m = n * HC + i
                        act.wait_ge(T.sem, T.at(f"u{m}", it))
                        nc.scalar.activation(hT[half][:, i, :], ps[m % 4][:, :], act_func,
                                             bias=bias2[:, s, i:i + 1] if b1 is not None else 0.0) \
                            .then_inc(A.sem, A.mark(f"h{m}"))

        @block.vector
        def _(dve):
            dve.sem_inc(V.sem, V.turn())
            with dve.Fori(0, E // 2) as it:
                dve.wait_ge(G.sem, G.at("gate", it))
                for n in range(U):
                    s, half = n // 2, n % 2
                    dve.wait_ge(T.sem, T.at(f"y{n}", it))
                    dve.wait_ge(V.sem, unit(V, "acc", n - 2, it, U))
                    for t in range(4):
                        b = half * 4 + t
                        v = nc.vector.scalar_tensor_tensor(
                            out=x[:, b, :], in0=ps[4 + half][:, t * P:(t + 1) * P], scalar=gate2[:, s, b:b + 1],
                            in1=x[:, b, :], op0=ALU.mult, op1=ALU.add)
                    v.then_inc(V.sem, V.mark(f"acc{n}"))


def pe_logits(core, pe, tag, wr, done):
    pe.wait_ge(*core.w_loaded[tag])
    for b in range(B):
        mm = core.nc.tensor.matmul(core.ps[0][:, b * 8:(b + 1) * 8], core.xnT[:, b * P:(b + 1) * P], wr,
                                   start=True, stop=True)
    mm.then_inc(done, 1)


def over_experts(col):
    return col.unsqueeze(2).broadcast_to([P, B, 8])


def dve_softmax(core, dve, link, prob, col, logits_done, shifted, exp_done):
    nc = core.nc
    logits = core.ps[0][:, 0:64].rearrange("p (b e) -> p b e", e=8)
    dve.wait_ge(logits_done, 1)
    link(nc.vector.tensor_reduce(col, logits, AX_X, ALU.max))
    nc.vector.tensor_tensor(prob, logits, over_experts(col), ALU.subtract).then_inc(shifted, 1)
    dve.wait_ge(exp_done, 1)
    link(nc.vector.tensor_reduce(col, prob, AX_X, ALU.add))
    link(nc.vector.reciprocal(col, col))
    link(nc.vector.tensor_tensor(prob, prob, over_experts(col), ALU.mult))


def pick_top(nc, link, values, spare, top, out, k, low):
    link(nc.vector.memset(spare, low))
    link(nc.vector.tensor_copy(spare[:, :, 0:8], values))
    for b in range(B):
        m = nc.vector.max(top[:, b, :], spare[:, b, 0:8])
    link(m)
    link(nc.vector.memset(top[:, :, k:8], low))
    for b in range(B):
        m = nc.vector.match_replace(spare[:, b, :], top[:, b, :], spare[:, b, :], low)
    link(m)
    link(nc.vector.tensor_tensor(out, values, spare[:, :, 0:8], ALU.not_equal))


def layer_l2_ffn(core, tag, w, w1, w2):
    nc = core.nc
    c = Carve(core.scratch)
    wr = w.take(8)
    gates, prob = c.take(8, B), c.take(B, 8)
    spare, top, pick, total, col = c.take(B, 16), c.take(B, 8), c.take(B, 8), c.take(B), c.take(B)
    layernorm_all(core, tag)
    chain, logits_done, shifted, exp_done = (core.sem(f"{tag}_route_{n}")
                                             for n in ("chain", "logits", "shifted", "exp"))
    with nc.Block(f"{tag}_route", no_gpsimd_drain=True) as block:

        @block.tensor
        def _(pe):
            pe_logits(core, pe, tag, wr, logits_done)

        @block.scalar
        def _(act):
            act.wait_ge(shifted, 1)
            nc.scalar.activation(prob, prob, ACT.Exp).then_inc(exp_done, 1)

        @block.vector
        def _(dve):
            link = Link(dve, chain)
            dve_softmax(core, dve, link, prob, col, logits_done, shifted, exp_done)
            pick_top(nc, link, prob, spare, top, pick, 2, -1.0)
            link(nc.vector.tensor_tensor(pick, pick, prob, ALU.mult))
            link(nc.vector.tensor_tensor(total, top[:, :, 0], top[:, :, 1], ALU.add))
            link(nc.vector.reciprocal(total, total))
            link(nc.vector.tensor_tensor(gates.rearrange("p e b -> p b e"), pick, over_experts(total), ALU.mult))

    mixture(core, tag, c, w1, w2, ACT.Gelu_apprx_tanh, gates)


def layer_l3_ffn(core, tag, w, w1, w2):
    nc, ps = core.nc, core.ps
    CAP = int(2 * 1.25 * B * P // 8)
    CAP += CAP % 2
    c = Carve(core.scratch)
    wr, tri = w.take(8), w.take(P)
    gates, val, prob = c.take(8, B), c.take(B, 8), c.take(B, 8)
    spare, top, total = c.take(B, 16), c.take(B, 8), c.take(B)
    picks = [c.take(B, 8), c.take(B, 8)]
    before = [c.take(B, 8), c.take(B, 8)]
    layernorm_all(core, tag)
    chain, logits_done, shifted, exp_done, picked, counted = (
        core.sem(f"{tag}_route_{n}") for n in ("chain", "logits", "shifted", "exp", "picks", "counts"))
    with nc.Block(f"{tag}_route", no_gpsimd_drain=True) as block:

        @block.tensor
        def _(pe):
            pe_logits(core, pe, tag, wr, logits_done)
            pe.wait_ge(picked, 1)
            for k in range(2):
                nc.tensor.matmul(ps[1 + k][:, 0:64], tri, picks[k].rearrange("p b e -> p (b e)"),
                                 start=True, stop=False)
                mm = nc.tensor.matmul(ps[1 + k][:, 0:64], core.ones[:, :], before[k].rearrange("p b e -> p (b e)"),
                                      start=False, stop=True)
            mm.then_inc(counted, 1)

        @block.scalar
        def _(act):
            act.wait_ge(shifted, 1)
            nc.scalar.activation(prob, prob, ACT.Exp).then_inc(exp_done, 1)

        @block.vector
        def _(dve):
            link = Link(dve, chain)
            first, second = picks
            dve.wait_ge(logits_done, 1)
            link(nc.vector.tensor_copy(val, ps[0][:, 0:64].rearrange("p (b e) -> p b e", e=8)))
            pick_top(nc, link, val, spare, top, second, 2, -3.0e38)
            pick_top(nc, link, val, spare, top, first, 1, -3.0e38)
            nc.vector.tensor_tensor(prob, val, top[:, :, 0:1].broadcast_to([P, B, 8]), ALU.subtract) \
                .then_inc(shifted, 1)
            dve.wait_ge(exp_done, 1)
            link(nc.vector.tensor_tensor(prob, prob, second, ALU.mult))
            link(nc.vector.tensor_reduce(total, prob, AX_X, ALU.add))
            link(nc.vector.reciprocal(total, total))
            link(nc.vector.tensor_tensor(prob, prob, over_experts(total), ALU.mult))
            link(nc.vector.tensor_tensor(second, second, first, ALU.subtract))
            link(nc.vector.memset(before[0][:, 0, :], 0.0))
            for b in range(1, B):
                link(nc.vector.tensor_tensor(before[0][:, b, :], before[0][:, b - 1, :], first[:, b - 1, :], ALU.add))
            link(nc.vector.tensor_tensor(before[1][:, 0, :], before[0][:, B - 1, :], first[:, B - 1, :], ALU.add))
            for b in range(1, B):
                v = nc.vector.tensor_tensor(before[1][:, b, :], before[1][:, b - 1, :], second[:, b - 1, :], ALU.add)
                if b < B - 1:
                    link(v)
            v.then_inc(picked, 1)
            dve.wait_ge(counted, 1)
            for k in range(2):
                link(nc.vector.scalar_tensor_tensor(
                    out=picks[k], in0=ps[1 + k][:, 0:64].rearrange("p (b e) -> p b e", e=8), scalar=CAP + 0.5,
                    in1=picks[k], op0=ALU.is_lt, op1=ALU.mult))
            link(nc.vector.tensor_tensor(first, first, second, ALU.add))
            link(nc.vector.tensor_tensor(gates.rearrange("p e b -> p b e"), first, prob, ALU.mult))

    mixture(core, tag, c, w1, w2, ACT.Gelu, gates)


def layer_l0_ffn(core, tag, w, w1, w2):
    nc, ps = core.nc, core.ps
    CAP = int(P * 2.0 / 8) + 1
    c = Carve(core.scratch)
    wr, b1, b2 = w.take(8), w.take(8, 4), w.take(D)
    gates, prob, col = c.take(8, B), c.take(B, 8), c.take(B)
    own, left, top = c.take(P)[0:64, :], c.take(P)[0:64, :], c.take(8)[0:64, :]
    gT = c.take(B * P)[0:8, :]
    layernorm_all(core, tag)
    chain, logits_done, shifted, exp_done, ready, turned, gated, back, given, spread, copied, biased = (
        core.sem(f"{tag}_route_{n}") for n in ("chain", "logits", "shifted", "exp", "by_token", "by_expert",
                                               "chosen", "gates", "gates_out", "gates_T", "gates_T_out", "bias"))
    with nc.Block(f"{tag}_route", no_gpsimd_drain=True) as block:

        @block.tensor
        def _(pe):
            pe_logits(core, pe, tag, wr, logits_done)
            pe.wait_ge(ready, 1)
            nc.tensor.transpose(ps[1][0:64, 0:P], gates.rearrange("p e b -> p (e b)"), core.ident[:, :]) \
                .then_inc(turned, 1)
            pe.wait_ge(gated, 1)
            nc.tensor.transpose(ps[2][:, 0:64], own, core.ident[0:64, 0:64]).then_inc(back, 1)
            pe.wait_ge(given, 1)
            for b in range(B):
                mm = nc.tensor.transpose(ps[3 + b // 4][0:8, b % 4 * P:(b % 4 + 1) * P], gates[:, :, b],
                                         core.ident[:, :])
            mm.then_inc(spread, 1)
            pe.wait_ge(copied, 1)
            for b in range(B):
                mm = nc.tensor.matmul(ps[5 + b // 4][:, b % 4 * P:(b % 4 + 1) * P], gT[:, b * P:(b + 1) * P],
                                      b2[0:8, :], start=True, stop=True)
            mm.then_inc(biased, 1)

        @block.scalar
        def _(act):
            act.wait_ge(shifted, 1)
            nc.scalar.activation(prob, prob, ACT.Exp).then_inc(exp_done, 1)

        @block.vector
        def _(dve):
            link = Link(dve, chain)
            dve_softmax(core, dve, link, prob, col, logits_done, shifted, exp_done)
            nc.vector.tensor_copy(gates.rearrange("p e b -> p b e"), prob).then_inc(ready, 1)
            dve.wait_ge(turned, 1)
            link(nc.vector.tensor_copy(own, ps[1][0:64, 0:P]))
            link(nc.vector.tensor_copy(left, own))
            for r in range(CAP // 8 + 1):
                link(nc.vector.max(top, left))
                if CAP - 8 * r < 8:
                    link(nc.vector.memset(top[:, CAP - 8 * r:8], -1.0))
                link(nc.vector.match_replace(left, top, left, -1.0))
            link(nc.vector.tensor_tensor(left, own, left, ALU.not_equal))
            nc.vector.tensor_tensor(own, own, left, ALU.mult).then_inc(gated, 1)
            dve.wait_ge(back, 1)
            nc.vector.tensor_copy(gates.rearrange("p e b -> p (e b)"), ps[2][:, 0:64]).then_inc(given, 1)
            dve.wait_ge(spread, 1)
            link(nc.vector.tensor_copy(gT[:, 0:BANK], ps[3][0:8, :]))
            nc.vector.tensor_copy(gT[:, BANK:], ps[4][0:8, :]).then_inc(copied, 1)
            dve.wait_ge(biased, 1)
            for half in range(2):
                xs = core.x[:, half * 4:half * 4 + 4, :].rearrange("p b d -> p (b d)")
                link(nc.vector.tensor_tensor(xs, xs, ps[5 + half][:, :], ALU.add))

    mixture(core, tag, c, w1, w2, ACT.Gelu, gates, b1=b1)


def layer_l0_attn(core, tag, w):
    nc, ps = core.nc, core.ps
    CH = 8
    c = Carve(core.scratch)
    wq, wk, wvT, wo = w.take(CH * P), w.take(CH * P), w.take(CH, P), w.take(CH, D)
    xn2, xnT2 = c.take(2, P), c.take(2, P)
    ek = [c.take(CH, P) for _ in range(2)]
    ekT = [c.take(CH * P) for _ in range(2)]
    us = [c.take(CH, P) for _ in range(2)]
    qk = [c.take(CH, P) for _ in range(2)]
    gg = [c.take(CH, P) for _ in range(2)]
    mm_ = [c.take(P) for _ in range(2)]
    top, tot, inv = c.take(2, CH), c.take(2, CH), c.take(2, CH)
    names2 = lambda *n: [f"{a}{u}" for a in n for u in range(2)]
    V = core.marks(f"{tag}_dve", ["maxA0", "maxB0", "maxA1", "maxB1", "inv0", "tA0", "inv1", "tA1", "uA0", "uA1",
                                  "qa0", "qa1", "gA0", "gA1", "gB0", "gB1", "m0", "m1", "x0", "x1"])
    A = core.marks(f"{tag}_act", ["exp0", "exp1", "tB0", "tB1", "uB0", "uB1", "qb0", "qb1"])
    G = core.marks(f"{tag}_pool", ["xn"])
    T = core.marks(f"{tag}_pe", ["k0", "k1", "t0", "t1", "u0", "u1", "q0", "q1", "g0", "g1", "m0", "m1", "y0", "y1"])
    zeroed = core.sem(f"{tag}_zeroed")
    layernorm_all(core, tag)

    def bank(u, n):
        return ps[4 * u + n]

    with nc.Block(tag, no_gpsimd_drain=True) as block:

        @block.gpsimd
        def _(pool):
            pool.sem_inc(G.sem, G.turn())
            for u in range(2):
                z = nc.gpsimd.memset(qk[u], 0.0)
            z.then_inc(zeroed, 1)
            with pool.Fori(0, PAIRS) as it:
                pool.wait_ge(T.sem, T.at("y1", it - 1))
                nc.gpsimd.tensor_copy(xnT2.rearrange("p a b -> p (a b)"), core.xnT[:, ds(it * 2 * P, 2 * P)])
                nc.gpsimd.tensor_copy(xn2, core.xn[:, ds(it * 2, 2), :]).then_inc(G.sem, G.mark("xn"))

        @block.tensor
        def _(pe):
            pe.sem_inc(T.sem, T.turn())
            pe.wait_ge(*core.w_loaded[tag])
            with pe.Fori(0, PAIRS) as it:
                pe.wait_ge(G.sem, G.at("xn", it))
                for u in range(2):
                    pe.wait_ge(V.sem, V.at(f"x{u}", it - 1))
                    for i in range(CH):
                        mm = nc.tensor.matmul(bank(u, i // 4)[:, i % 4 * P:(i % 4 + 1) * P], wk[:, i * P:(i + 1) * P],
                                              xnT2[:, u, :], start=True, stop=True)
                    mm.then_inc(T.sem, T.mark(f"k{u}"))
                for u in range(2):
                    pe.wait_ge(A.sem, A.at(f"exp{u}", it))
                    for i in range(CH):
                        mm = nc.tensor.transpose(bank(u, 2 + i // 4)[:, i % 4 * P:(i % 4 + 1) * P], ek[u][:, i, :],
                                                 core.ident[:, :])
                    mm.then_inc(T.sem, T.mark(f"t{u}"))
                for u in range(2):
                    pe.wait_ge(V.sem, V.at(f"tA{u}", it))
                    pe.wait_ge(A.sem, A.at(f"tB{u}", it))
                    for i in range(2):
                        mm = nc.tensor.matmul(bank(u, i)[:, :], xn2[:, u, :], ekT[u][:, i * BANK:(i + 1) * BANK],
                                              start=True, stop=True)
                    mm.then_inc(T.sem, T.mark(f"u{u}"))
                for u in range(2):
                    pe.wait_ge(V.sem, V.at(f"uA{u}", it))
                    pe.wait_ge(A.sem, A.at(f"uB{u}", it))
                    for i in range(CH):
                        mm = nc.tensor.matmul(bank(u, 2 + i // 4)[:, i % 4 * P:(i % 4 + 1) * P],
                                              wq[:, i * P:(i + 1) * P], us[u][:, i, :], start=True, stop=True)
                    mm.then_inc(T.sem, T.mark(f"q{u}"))
                for u in range(2):
                    pe.wait_ge(V.sem, V.at(f"qa{u}", it))
                    pe.wait_ge(A.sem, A.at(f"qb{u}", it))
                    for i in range(CH):
                        mm = nc.tensor.matmul(bank(u, i // 4)[:, i % 4 * P:(i % 4 + 1) * P], qk[u][:, i, :],
                                              wo[:, i, :], start=True, stop=True)
                    mm.then_inc(T.sem, T.mark(f"g{u}"))
                for u in range(2):
                    pe.wait_ge(V.sem, V.at(f"gB{u}", it))
                    for i in range(CH):
                        mm = nc.tensor.matmul(bank(u, 2)[:, 0:P], wvT[:, i, :], gg[u][:, i, :],
                                              start=(i == 0), stop=(i == CH - 1))
                    mm.then_inc(T.sem, T.mark(f"m{u}"))
                for u in range(2):
                    pe.wait_ge(V.sem, V.at(f"m{u}", it))
                    nc.tensor.matmul(bank(u, 3)[:, 0:P], xnT2[:, u, :], mm_[u], start=True, stop=True) \
                        .then_inc(T.sem, T.mark(f"y{u}"))

        @block.scalar
        def _(act):
            act.sem_inc(A.sem, A.turn())
            act.wait_ge(zeroed, 1)
            with act.Fori(0, PAIRS) as it:
                for u in range(2):
                    act.wait_ge(V.sem, V.at(f"maxB{u}", it))
                    for i in range(CH):
                        e = nc.scalar.activation(ek[u][:, i, :], bank(u, i // 4)[:, i % 4 * P:(i % 4 + 1) * P],
                                                 ACT.Exp, bias=top[:, u, i:i + 1], accum_out=tot[:, u, i:i + 1])
                    e.then_inc(A.sem, A.mark(f"exp{u}"))
                for u in range(2):
                    act.wait_ge(T.sem, T.at(f"t{u}", it))
                    nc.scalar.copy(ekT[u][:, BANK:], bank(u, 3)[:, :]).then_inc(A.sem, A.mark(f"tB{u}"))
                for u in range(2):
                    act.wait_ge(T.sem, T.at(f"u{u}", it))
                    nc.scalar.copy(us[u][:, 4:, :].rearrange("p a b -> p (a b)"), bank(u, 1)[:, :]) \
                        .then_inc(A.sem, A.mark(f"uB{u}"))
                for u in range(2):
                    act.wait_ge(T.sem, T.at(f"q{u}", it))
                    for half in range(2):
                        e = nc.scalar.copy(qk[u][64:, 4 * half:4 * half + 4, 64:],
                                           bank(u, 2 + half)[64:, :].rearrange("p (a b) -> p a b", a=4)[:, :, 64:])
                    e.then_inc(A.sem, A.mark(f"qb{u}"))

        @block.vector
        def _(dve):
            dve.sem_inc(V.sem, V.turn())
            dve.wait_ge(zeroed, 1)
            with dve.Fori(0, PAIRS) as it:
                for u in range(2):
                    dve.wait_ge(T.sem, T.at(f"k{u}", it))
                    for half, m in enumerate(("maxA", "maxB")):
                        nc.vector.tensor_reduce(top[:, u, 4 * half:4 * half + 4],
                                                bank(u, half)[:, :].rearrange("p (a b) -> p a b", a=4), AX_X,
                                                ALU.max, negate=True).then_inc(V.sem, V.mark(f"{m}{u}"))
                for u in range(2):
                    dve.wait_ge(A.sem, A.at(f"exp{u}", it))
                    nc.vector.reciprocal(inv[:, u, :], tot[:, u, :]).then_inc(V.sem, V.mark(f"inv{u}"))
                    dve.wait_ge(T.sem, T.at(f"t{u}", it))
                    nc.vector.tensor_copy(ekT[u][:, 0:BANK], bank(u, 2)[:, :]).then_inc(V.sem, V.mark(f"tA{u}"))
                for u in range(2):
                    dve.wait_ge(T.sem, T.at(f"u{u}", it))
                    nc.vector.tensor_copy(us[u][:, 0:4, :].rearrange("p a b -> p (a b)"), bank(u, 0)[:, :]) \
                        .then_inc(V.sem, V.mark(f"uA{u}"))
                for u in range(2):
                    dve.wait_ge(T.sem, T.at(f"q{u}", it))
                    for half in range(2):
                        v = nc.vector.tensor_copy(qk[u][0:64, 4 * half:4 * half + 4, 0:64],
                                                  bank(u, 2 + half)[0:64, :].rearrange("p (a b) -> p a b", a=4)[:, :, 0:64])
                    v.then_inc(V.sem, V.mark(f"qa{u}"))
                for u in range(2):
                    dve.wait_ge(T.sem, T.at(f"g{u}", it))
                    nc.vector.tensor_tensor(gg[u][:, 0:4, :], bank(u, 0)[:, :].rearrange("p (a b) -> p a b", a=4),
                                            inv[:, u, 0:4].unsqueeze(2).broadcast_to([P, 4, P]),
                                            ALU.mult).then_inc(V.sem, V.mark(f"gA{u}"))
                for u in range(2):
                    nc.vector.tensor_tensor(gg[u][:, 4:8, :], bank(u, 1)[:, :].rearrange("p (a b) -> p a b", a=4),
                                            inv[:, u, 4:8].unsqueeze(2).broadcast_to([P, 4, P]),
                                            ALU.mult).then_inc(V.sem, V.mark(f"gB{u}"))
                for u in range(2):
                    dve.wait_ge(T.sem, T.at(f"m{u}", it))
                    nc.vector.tensor_copy(mm_[u], bank(u, 2)[:, 0:P]).then_inc(V.sem, V.mark(f"m{u}"))
                for u in range(2):
                    dve.wait_ge(T.sem, T.at(f"y{u}", it))
                    xr = core.x[:, ds(it * 2 + u, 1), :].rearrange("p a d -> p (a d)")
                    nc.vector.tensor_tensor(xr, xr, bank(u, 3)[:, 0:D], ALU.add).then_inc(V.sem, V.mark(f"x{u}"))


def layer_l1_attn(core, tag, w):
    nc, ps = core.nc, core.ps
    H, K, TG = 16, 64, 8
    SEQ = P // TG
    c = Carve(core.scratch)
    wq, wk, wv = w.take(H * K), w.take(H * K), w.take(H * K)
    wp, bp, bias = w.take(H, D), w.take(D), w.take(P)
    q, k, vT = (c.take(SEQ, H, TG)[0:K] for _ in range(3))
    v = c.take(SEQ, K)
    oT = c.take(H, P)[0:K]
    groups = [dict(q=[q[:, 4 * g + i].rearrange("p a b -> p (a b)") for i in range(4)],
                   k=[k[:, 4 * g + i].rearrange("p a b -> p (a b)") for i in range(4)],
                   v=[v[:, 4 * g + i, :] for i in range(4)],
                   o=[ps[2 + g % 2][0:K, i * P:(i + 1) * P] for i in range(4)]) for g in range(4)]
    vs, as_, gs, ts = names_of(4, True, 4)
    a_names = ["exp0", "v0", "exp1", "v1", "exp2", "exp3"] + [f"oT{g}" for g in range(4)]
    V = core.marks(f"{tag}_dve", [f"{n}{h}" for h in range(2) for n in ("qo", "ko", "vo")] + vs + ["x"])
    A = core.marks(f"{tag}_act", [f"{n}{h}" for h in range(2) for n in ("qe", "ke", "ve")] + a_names)
    G = core.marks(f"{tag}_pool", gs)
    T = core.marks(f"{tag}_pe", [f"{n}{h}" for h in range(2) for n in "qkv"] + ts[:4] + ["vt0", "vt1"] + ts[4:] + ["y"])
    sm = Softmax(core, c, groups, P, V, A, G, T, (6, 7, 4, 5), (0, 1), mask=lambda g: for_heads(bias))
    layernorm_all(core, tag)

    def halves(dst, half, par):
        return dst[:, :, 8 * half + par:8 * half + 8:2, :].rearrange("p s c t -> p c s t")

    def source(bank, par):
        return ps[bank][64 * par:64 * par + 64, :].rearrange("p (c s t) -> p c s t", c=4, t=TG)

    with nc.Block(tag, no_gpsimd_drain=True) as block:

        @block.gpsimd
        def _(pool):
            pool.sem_inc(G.sem, G.turn())
            with pool.Fori(0, B) as it:
                sm.run_pool(pool, it)

        @block.tensor
        def _(pe):
            pe.sem_inc(T.sem, T.turn())
            pe.wait_ge(*core.w_loaded[tag])
            with pe.Fori(0, B) as it:
                pe.wait_ge(V.sem, V.at("x", it - 1))
                pe.wait_ge(A.sem, A.at("oT3", it - 1))
                for half in range(2):
                    for n, wt in enumerate((wq, wk, wv)):
                        bank = 3 * half + n
                        for i in range(4):
                            ch = 4 * half + i
                            mm = nc.tensor.matmul(ps[bank][:, i * P:(i + 1) * P], wt[:, ch * P:(ch + 1) * P],
                                                  core.xnT[:, ds(it * P, P)], start=True, stop=True)
                        mm.then_inc(T.sem, T.mark("qkv"[n] + str(half)))
                pe.wait_ge(V.sem, V.at("vo1", it))
                pe.wait_ge(A.sem, A.at("ve1", it))

                def turn_values():
                    for half in range(2):
                        for s in range(8):
                            mm = nc.tensor.transpose(ps[half][:, s * K:(s + 1) * K],
                                                     vT[:, 8 * half + s].rearrange("p a b -> p (a b)"),
                                                     core.ident[0:K, 0:K])
                        mm.then_inc(T.sem, T.mark(f"vt{half}"))
                    pe.wait_ge(A.sem, A.at("v1", it))

                def free_output(g):
                    if g >= 2:
                        pe.wait_ge(A.sem, A.at(f"oT{g - 2}", it))

                sm.run_pe(pe, it, turn_values, free_output)
                pe.wait_ge(A.sem, A.at("oT3", it))
                for h in range(H):
                    nc.tensor.matmul(ps[4][:, 0:D], oT[:, h, :], wp[0:K, h, :], start=(h == 0), stop=False)
                nc.tensor.matmul(ps[4][:, 0:D], core.ones[0:1, 0:P], bp[0:1, :], start=False, stop=True) \
                    .then_inc(T.sem, T.mark("y"))

        @block.scalar
        def _(act):
            act.sem_inc(A.sem, A.turn())

            def out(it, g):
                act.wait_ge(T.sem, T.at(f"o{g}", it))
                if g == 0:
                    act.wait_ge(T.sem, T.at("y", it - 1))
                nc.scalar.copy(oT.rearrange("p h (s t) -> p s h t", t=TG)[:, 4 * g:4 * g + 4],
                               ps[2 + g % 2][0:K, :].rearrange("p (s h t) -> p s h t", s=4, t=TG)) \
                    .then_inc(A.sem, A.mark(f"oT{g}"))

            with act.Fori(0, B) as it:
                for half in range(2):
                    for n, (dst, nm) in enumerate(((q, "qe"), (k, "ke"), (vT, "ve"))):
                        act.wait_ge(T.sem, T.at("qkv"[n] + str(half), it))
                        nc.scalar.mul(halves(dst, half, 0), source(3 * half + n, 0), K ** -0.5 if n == 0 else 1.0) \
                            .then_inc(A.sem, A.mark(f"{nm}{half}"))
                for g in range(4):
                    sm.act_exp(act, it, g)
                    if g < 2:
                        act.wait_ge(T.sem, T.at(f"vt{g}", it))
                        nc.scalar.copy(v[:, 8 * g:8 * g + 8, :].rearrange("p a b -> p (a b)"), ps[g][:, :]) \
                            .then_inc(A.sem, A.mark(f"v{g}"))
                for g in range(4):
                    out(it, g)

        @block.vector
        def _(dve):
            dve.sem_inc(V.sem, V.turn())
            with dve.Fori(0, B) as it:
                for half in range(2):
                    for n, (dst, nm) in enumerate(((q, "qo"), (k, "ko"), (vT, "vo"))):
                        dve.wait_ge(A.sem, A.at(("qe", "ke", "ve")[n] + str(half), it))
                        nc.vector.tensor_scalar(halves(dst, half, 1), source(3 * half + n, 1),
                                                K ** -0.5 if n == 0 else 1.0, None, ALU.mult) \
                            .then_inc(V.sem, V.mark(f"{nm}{half}"))
                sm.run_dve(dve, it)
                dve.wait_ge(T.sem, T.at("y", it))
                xr = core.x[:, ds(it, 1), :].rearrange("p a d -> p (a d)")
                nc.vector.tensor_tensor(xr, xr, ps[4][:, 0:D], ALU.add).then_inc(V.sem, V.mark("x"))


def layer_l3_xattn(core, tag, w):
    nc, ps = core.nc, core.ps
    H, K = 2, 64
    c = Carve(core.scratch)
    wqk, wvl = w.take(2 * P), w.take(P)
    wkc, wvc = w.take(P), w.take(P)
    wo, bo = w.take(D), w.take(D)
    gx, bx, gl, bl, gq, gk = (w.take(1) for _ in range(6))
    cn, cnT = c.take(B, CTX), c.take(B * P)
    lat, latT = c.take(B, D), c.take(B * P)
    latT2, cnT2, bias2 = c.take(2 * P), c.take(2 * P), c.take(2, 2 * P)
    sq, qkn = c.take(2, 3 * P), c.take(2, 3 * P)
    ss, rn, half = c.take(2, 6), c.take(2, 6), c.take(2, 6)
    qT, kT, v = c.take(2, P), c.take(2, 2 * P), c.take(2, 2 * P)
    oT = c.take(2, P)
    vs, as_, gs, ts = names_of(2, True, 2)
    V = core.marks(f"{tag}_dve", ["ss0", "ss1", "rn0", "rn1", "inv0n", "inv1n", "qkn0", "qkn1", "kT0", "kT1"]
                   + vs + ["x0", "x1"])
    A = core.marks(f"{tag}_act", ["sq0", "sq1", "v", "qT0", "qT1"] + as_ + ["oT"])
    G = core.marks(f"{tag}_pool", ["copies", "root0", "root1"] + gs)
    T = core.marks(f"{tag}_pe", ["p0", "p1", "v", "tq0", "tq1"] + ts + ["y0", "y1"])
    groups = []
    for h in range(H):
        r = slice(K * h, K * h + K)
        groups.append(dict(q=[qT[r, u, :] for u in range(2)], k=[kT[r, u, :] for u in range(2)],
                           v=[v[:, u, kb * P + h * K:kb * P + (h + 1) * K] for u in range(2) for kb in range(2)],
                           o=[ps[5][r, u * P:(u + 1) * P] for u in range(2)]))
    sm = Softmax(core, c, groups, 2 * P, V, A, G, T, (6, 7), (0, 1), mask=lambda g: bias2)
    layernorm_all(core, tag)
    with nc.Block(f"{tag}_weights", no_gpsimd_drain=True) as block:

        @block.scalar
        def _(act):
            act.wait_ge(*core.w_loaded[tag])

        @block.vector
        def _(dve):
            dve.wait_ge(*core.w_loaded[tag])

    layernorm_all(core, f"{tag}_latents", src=core.xn, out=lat, outT=latT, gain=gl, bias=bl)
    layernorm_all(core, f"{tag}_context", src=core.ctxk, out=cn, outT=cnT, gain=gx[0:CTX], bias=bx[0:CTX], width=CTX)
    ready = core.sem(f"{tag}_constants")
    with nc.Block(tag, no_gpsimd_drain=True) as block:

        @block.gpsimd
        def _(pool):
            pool.sem_inc(G.sem, G.turn())
            nc.gpsimd.memset(half, 0.5).then_inc(ready, 1)
            nc.gpsimd.memset(bias2, 0.0).then_inc(ready, 1)
            pool.wait_ge(ready, 2)
            with pool.Fori(0, PAIRS) as it:
                pool.wait_ge(T.sem, T.at("v", it - 1))
                pool.wait_ge(V.sem, V.at("mask1", it - 1))
                nc.gpsimd.tensor_copy(latT2, latT[:, ds(it * 2 * P, 2 * P)])
                nc.gpsimd.tensor_copy(bias2[:, :, 0:P], core.lat_bias[:, ds(it * 2 * P, 2 * P)]
                                      .rearrange("p (a b) -> p a b", a=2))
                nc.gpsimd.tensor_copy(cnT2[0:CTX, :], cnT[0:CTX, ds(it * 2 * P, 2 * P)]) \
                    .then_inc(G.sem, G.mark("copies"))
                for u in range(2):
                    pool.wait_ge(V.sem, V.at(f"ss{u}", it))
                    nc.gpsimd.tensor_tensor(rn[:, u, :], ss[:, u, :], half[:, u, :], ALU.pow) \
                        .then_inc(G.sem, G.mark(f"root{u}"))
                sm.run_pool(pool, it)

        @block.tensor
        def _(pe):
            pe.sem_inc(T.sem, T.turn())
            with pe.Fori(0, PAIRS) as it:
                pe.wait_ge(G.sem, G.at("copies", it))
                pe.wait_ge(V.sem, V.at("x1", it - 1))
                for u in range(2):
                    lt, ct = latT2[:, u * P:(u + 1) * P], cnT2[0:CTX, u * P:(u + 1) * P]
                    nc.tensor.matmul(ps[u][:, 0:2 * P], lt, wqk, start=True, stop=True)
                    nc.tensor.matmul(ps[u][:, 2 * P:3 * P], ct, wkc[0:CTX, :], start=True, stop=True) \
                        .then_inc(T.sem, T.mark(f"p{u}"))
                for u in range(2):
                    lt, ct = latT2[:, u * P:(u + 1) * P], cnT2[0:CTX, u * P:(u + 1) * P]
                    nc.tensor.matmul(ps[2][:, u * 2 * P:u * 2 * P + P], ct, wvc[0:CTX, :], start=True, stop=True)
                    mm = nc.tensor.matmul(ps[2][:, u * 2 * P + P:(u + 1) * 2 * P], lt, wvl, start=True, stop=True)
                mm.then_inc(T.sem, T.mark("v"))
                for u in range(2):
                    pe.wait_ge(V.sem, V.at(f"qkn{u}", it))
                    for n in range(3):
                        mm = nc.tensor.transpose(ps[3 + u][:, n * P:(n + 1) * P], qkn[:, u, n * P:(n + 1) * P],
                                                 core.ident[:, :])
                    mm.then_inc(T.sem, T.mark(f"tq{u}"))
                pe.wait_ge(A.sem, A.at("qT1", it))
                pe.wait_ge(V.sem, V.at("kT1", it))
                sm.run_pe(pe, it)
                pe.wait_ge(A.sem, A.at("oT", it))
                for u in range(2):
                    nc.tensor.matmul(ps[3 + u][:, 0:D], oT[:, u, :], wo, start=True, stop=False)
                    nc.tensor.matmul(ps[3 + u][:, 0:D], core.ones[0:1, 0:P], bo[0:1, :], start=False, stop=True) \
                        .then_inc(T.sem, T.mark(f"y{u}"))

        @block.scalar
        def _(act):
            act.sem_inc(A.sem, A.turn())
            with act.Fori(0, PAIRS) as it:
                for u in range(2):
                    act.wait_ge(T.sem, T.at(f"p{u}", it))
                    nc.scalar.activation(sq[:, u, :], ps[u][:, 0:3 * P], ACT.Square).then_inc(A.sem, A.mark(f"sq{u}"))
                act.wait_ge(T.sem, T.at("v", it))
                nc.scalar.copy(v.rearrange("p a b -> p (a b)"), ps[2][:, :]).then_inc(A.sem, A.mark("v"))
                for u in range(2):
                    act.wait_ge(T.sem, T.at(f"tq{u}", it))
                    nc.scalar.activation(qT[:, u, :], ps[3 + u][:, 0:P], ACT.Copy, scale=gq) \
                        .then_inc(A.sem, A.mark(f"qT{u}"))
                sm.run_act(act, it)
                act.wait_ge(T.sem, T.at("o1", it))
                nc.scalar.copy(oT.rearrange("p a b -> p (a b)"), ps[5][:, 0:2 * P]).then_inc(A.sem, A.mark("oT"))

        @block.vector
        def _(dve):
            dve.sem_inc(V.sem, V.turn())
            dve.wait_ge(ready, 2)
            with dve.Fori(0, PAIRS) as it:
                for u in range(2):
                    dve.wait_ge(A.sem, A.at(f"sq{u}", it))
                    nc.vector.tensor_reduce(ss[:, u, :], sq[:, u, :].rearrange("p (n k) -> p n k", k=K), AX_X,
                                            ALU.add).then_inc(V.sem, V.mark(f"ss{u}"))
                for u in range(2):
                    dve.wait_ge(G.sem, G.at(f"root{u}", it))
                    nc.vector.tensor_scalar(rn[:, u, :], rn[:, u, :], K ** -0.5, 1e-8, ALU.mult, ALU.max) \
                        .then_inc(V.sem, V.mark(f"rn{u}"))
                for u in range(2):
                    dve.wait_ge(V.sem, V.at(f"rn{u}", it))
                    nc.vector.reciprocal(rn[:, u, :], rn[:, u, :]).then_inc(V.sem, V.mark(f"inv{u}n"))
                for u in range(2):
                    dve.wait_ge(V.sem, V.at(f"inv{u}n", it))
                    nc.vector.tensor_tensor(qkn[:, u, :].rearrange("p (n k) -> p n k", k=K),
                                            ps[u][:, 0:3 * P].rearrange("p (n k) -> p n k", k=K),
                                            rn[:, u, :].unsqueeze(2).broadcast_to([P, 6, K]), ALU.mult) \
                        .then_inc(V.sem, V.mark(f"qkn{u}"))
                for u in range(2):
                    dve.wait_ge(A.sem, A.at(f"qT{u}", it))
                    nc.vector.tensor_scalar(kT[:, u, 0:P], ps[3 + u][:, 2 * P:3 * P], gk, K ** -0.5, ALU.mult, ALU.mult)
                    nc.vector.tensor_scalar(kT[:, u, P:], ps[3 + u][:, P:2 * P], gk, K ** -0.5, ALU.mult, ALU.mult) \
                        .then_inc(V.sem, V.mark(f"kT{u}"))
                dve.wait_ge(G.sem, G.at("copies", it))
                sm.run_dve(dve, it)
                for u in range(2):
                    dve.wait_ge(T.sem, T.at(f"y{u}", it))
                    xr = core.x[:, ds(it * 2 + u, 1), :].rearrange("p a d -> p (a d)")
                    nc.vector.tensor_tensor(xr, xr, ps[3 + u][:, 0:D], ALU.add).then_inc(V.sem, V.mark(f"x{u}"))


class RelativeSoftmax(Softmax):

    def __init__(self, core, c, groups, V, A, G, T, banks_a, banks_s, banks_t, rel, rel_at):
        super().__init__(core, c, groups, P, V, A, G, T, banks_s, banks_t)
        self.banks_a, self.rel, self.rel_at = banks_a, rel, rel_at
        self.summed = c.take(2, BANK)

    def slots(self, it, g):
        return self.rel[:, ds(self.rel_at(it, g), 8 * P)].rearrange("p (c y t) -> p c y t", c=4, y=2)[:, :, 0, :]

    def pe_scores(self, pe, it, g):
        grp = self.groups[g]
        pe.wait_ge(self.V.sem, self.before(self.V, "add", g - 2, it))
        for j, (q, k) in enumerate(zip(grp["q"], grp["k"])):
            mm = self.nc.tensor.matmul(self.core.ps[self.banks_a[g % 2]][:, j * P:(j + 1) * P], k, q,
                                       start=True, stop=True)
        mm.then_inc(self.T.sem, self.T.mark(f"a{g}"))

    def dve_add(self, dve, it, g):
        dve.wait_ge(self.T.sem, self.T.at(f"a{g}", it))
        dve.wait_ge(self.T.sem, self.before(self.T, "s", g - 2, it))
        four = lambda a: a.rearrange("p (c t) -> p c t", c=4)
        self.nc.vector.tensor_tensor(four(self.summed[:, g % 2, :]), four(self.core.ps[self.banks_a[g % 2]][:, :]),
                                     self.slots(it, g), ALU.add).then_inc(self.V.sem, self.V.mark(f"add{g}"))

    def pe_sums(self, pe, it, g):
        pe.wait_ge(self.V.sem, self.V.at(f"add{g}", it))
        pe.wait_ge(self.A.sem, self.before(self.A, "exp", g - 2, it))
        for j in range(4):
            mm = self.nc.tensor.transpose(self.core.ps[self.banks_s[g % 2]][:, j * P:(j + 1) * P],
                                          self.summed[:, g % 2, j * P:(j + 1) * P], self.core.ident[:, :])
        mm.then_inc(self.T.sem, self.T.mark(f"s{g}"))

    def dve_copy(self, dve, it, g):
        dve.wait_ge(self.G.sem, self.before(self.G, "keep", g - 2, it))
        super().dve_copy(dve, it, g)

    def pool_keep(self, pool, it, g):
        pool.wait_ge(self.V.sem, self.V.at(f"pT{g}", it))
        self.nc.gpsimd.tensor_copy(self.slots(it, g), self.probT[:, g % 2, :].rearrange("p (c t) -> p c t", c=4)) \
            .then_inc(self.G.sem, self.G.mark(f"keep{g}"))

    def run_pool(self, pool, it):
        n = len(self.groups)
        for g in range(n):
            self.pool_norm(pool, it, g)
            if g > 0:
                self.pool_keep(pool, it, g - 1)
        self.pool_keep(pool, it, n - 1)

    def names(self):
        n, ahead = len(self.groups), self.ahead
        t = [f"a{g}" for g in range(ahead)] + [f"s{g}" for g in range(ahead)]
        v = [f"add{g}" for g in range(ahead)] + [f"max{g}" for g in range(ahead)]
        p = []
        for g in range(n):
            more, last = g + ahead < n, g > 0
            t += ([f"a{g + ahead}"] if more else []) + [f"t{g}"] + ([f"s{g + ahead}"] if more else []) \
                + ([f"o{g - 1}"] if last else [])
            v += ([f"add{g + ahead}"] if more else []) + [f"inv{g}"] + ([f"max{g + ahead}"] if more else []) \
                + ([f"pT{g - 1}"] if last else [])
            p += [f"norm{g}"] + ([f"keep{g - 1}"] if last else [])
        return v + [f"pT{n - 1}"], [f"exp{g}" for g in range(n)], p + [f"keep{n - 1}"], t + [f"o{n - 1}"]

    def run_pe(self, pe, it):
        n, ahead = len(self.groups), self.ahead
        for g in range(ahead):
            self.pe_scores(pe, it, g)
        for g in range(ahead):
            self.pe_sums(pe, it, g)
        for g in range(n + 1):
            if g + ahead < n:
                self.pe_scores(pe, it, g + ahead)
            if g < n:
                self.pe_turn(pe, it, g)
            if g + ahead < n:
                self.pe_sums(pe, it, g + ahead)
            if g > 0:
                self.pe_values(pe, it, g - 1)

    def run_dve(self, dve, it):
        n, ahead = len(self.groups), self.ahead
        for g in range(ahead):
            self.dve_add(dve, it, g)
        for g in range(ahead):
            self.dve_max(dve, it, g)
        for g in range(n + 1):
            if g + ahead < n:
                self.dve_add(dve, it, g + ahead)
            if g < n:
                self.dve_recip(dve, it, g)
            if g + ahead < n:
                self.dve_max(dve, it, g + ahead)
            if g > 0:
                self.dve_copy(dve, it, g - 1)


def layer_l2_attn(core, tag, w):
    nc, ps = core.nc, core.ps
    SC = 8 ** -0.5
    TCH = 32
    c = Carve(core.scratch)
    wq, wk, wv, wo = w.take(BANK), w.take(BANK), w.take(BANK), w.take(4, D)
    bq, bk, bv, bo = w.take(4), w.take(4), w.take(BANK), w.take(D)
    relv, relk = w.take(P, 8), w.take(2 * P)
    rel = c.take(P * P + P)
    rel3 = rel[:, 0:P * P].rearrange("p (n t) -> p n t", t=P)
    start = c.at
    layernorm_all(core, tag)

    qTall, q8, window = c.take(4, B * P), c.take(2, 16 * B, TCH // 2), c.take(P + TCH - 1)
    T = core.marks(f"{tag}_qall_pe", [f"q{n}" for n in range(8)])
    V = core.marks(f"{tag}_qall_dve", [f"q{n}" for n in range(8)])
    with nc.Block(f"{tag}_qall", no_gpsimd_drain=True) as block:

        @block.tensor
        def _(pe):
            pe.wait_ge(*core.w_loaded[tag])
            for n in range(8):
                nc.tensor.matmul(ps[n][:, :], wq[:, n // 2 * P:(n // 2 + 1) * P],
                                 core.xnT[:, n % 2 * BANK:(n % 2 + 1) * BANK], start=True, stop=True) \
                    .then_inc(T.sem, T.mark(f"q{n}"))

        @block.vector
        def _(dve):
            dve.wait_ge(*core.w_loaded[tag])
            for n in range(8):
                dve.wait_ge(T.sem, T.at(f"q{n}", -1))
                nc.vector.tensor_scalar(qTall[:, n // 2, n % 2 * BANK:(n % 2 + 1) * BANK], ps[n][:, :],
                                        bq[:, n // 2:n // 2 + 1], SC, ALU.add, ALU.mult) \
                    .then_inc(V.sem, V.mark(f"q{n}"))

    QB = TCH // 4
    T = core.marks(f"{tag}_rel_pe", [f"r{n}" for n in range(QB)])
    V = core.marks(f"{tag}_rel_dve", [f"r{n}" for n in range(0, QB, 2)])
    A = core.marks(f"{tag}_rel_act", [f"r{n}" for n in range(1, QB, 2)])
    G = core.marks(f"{tag}_rel_pool", ["window"])
    q8_loaded = [core.sem(f"{tag}_q8_loaded{half}") for half in range(2)]

    def out_of_bank(eng, copy, marks, it, n):
        eng.wait_ge(T.sem, T.at(f"r{n}", it))
        copy(rel3[:, :, ds(it * TCH + 4 * n, 4)], ps[n][:, :].rearrange("p (t n) -> p n t", t=4)) \
            .then_inc(marks.sem, marks.mark(f"r{n}"))

    with nc.Block(f"{tag}_rel", no_gpsimd_drain=True) as block:

        @block.sync
        def _(sp):
            with sp.Fori(0, P // TCH) as it:
                for half in range(2):
                    sp.wait_ge(T.sem, T.at(f"r{QB // 2 * (half + 1) - 1}", it - 1))
                    for j in range(4):
                        sp.dma_start(q8[0:8, half, 32 * j:32 * j + 32], qTall[32 * j:32 * j + 8, :, :]
                                     .rearrange("p i (b t) -> p (i b) t", t=P)
                                     [:, :, ds(it * TCH + half * (TCH // 2), TCH // 2)]) \
                            .then_inc(q8_loaded[half], 16)

        @block.gpsimd
        def _(pool):
            pool.sem_inc(G.sem, G.turn())
            with pool.Fori(0, P // TCH) as it:
                pool.wait_ge(T.sem, T.at(f"r{QB - 1}", it - 1))
                nc.gpsimd.tensor_copy(window[0:8, :], relk[0:8, ds(it * (-TCH) + (P - TCH), P + TCH - 1)]) \
                    .then_inc(G.sem, G.mark("window"))

        @block.tensor
        def _(pe):
            pe.sem_inc(T.sem, T.turn())
            with pe.Fori(0, P // TCH) as it:
                pe.wait_ge(G.sem, G.at("window", it))
                for n in range(QB):
                    half = n // (QB // 2)
                    if n % (QB // 2) == 0:
                        pe.wait_ge(q8_loaded[half], it * 64 + 64)
                    m = A if n % 2 else V
                    pe.wait_ge(m.sem, m.at(f"r{n}", it - 1))
                    for i in range(4):
                        t = 4 * n + i
                        mm = nc.tensor.matmul(ps[n][:, i * P:(i + 1) * P], window[0:8, TCH - 1 - t:TCH - 1 - t + P],
                                              q8[0:8, half, :, t % (TCH // 2)]
                                              .rearrange("p (j i b) -> p i j b", j=4, i=4), start=True, stop=True)
                    mm.then_inc(T.sem, T.mark(f"r{n}"))

        @block.vector
        def _(dve):
            dve.sem_inc(V.sem, V.turn())
            with dve.Fori(0, P // TCH) as it:
                for n in range(0, QB, 2):
                    out_of_bank(dve, nc.vector.tensor_copy, V, it, n)

        @block.scalar
        def _(act):
            act.sem_inc(A.sem, A.turn())
            with act.Fori(0, P // TCH) as it:
                for n in range(1, QB, 2):
                    out_of_bank(act, nc.scalar.copy, A, it, n)

    c.at = start
    qT, kT, v = c.take(4, 2 * P), c.take(4, 2 * P), c.take(2, BANK)
    xnT2, oT = c.take(2 * P), c.take(2, BANK)
    groups = small_groups(qT, kT, v, ps, (2, 3))
    probe = RelativeSoftmax.__new__(RelativeSoftmax)
    probe.groups, probe.ahead = groups, 2
    vs, as_, gs, ts = probe.names()
    V = core.marks(f"{tag}_dve", [f"q{n}" for n in range(4)] + vs + ["x0", "x1"])
    A = core.marks(f"{tag}_act", [f"k{n}" for n in range(4)] + ["v0", "v1"] + as_ + ["oT0", "oT1"])
    G = core.marks(f"{tag}_pool", ["xn"] + gs)
    T = core.marks(f"{tag}_pe", ["q0", "q1", "k0", "k1", "v0", "v1"] + ts + ["y0", "y1"])

    def rel_at(it, g):
        u, j = g // 4, g % 4
        return it * (2 * 8 * P) + ((j % 2) * 64 + u * 8 + j // 2) * P

    sm = RelativeSoftmax(core, c, groups, V, A, G, T, (4, 5), (6, 7), (0, 1), rel, rel_at)
    with nc.Block(tag, no_gpsimd_drain=True) as block:

        @block.gpsimd
        def _(pool):
            pool.sem_inc(G.sem, G.turn())
            with pool.Fori(0, PAIRS) as it:
                pool.wait_ge(T.sem, T.at("v1", it - 1))
                nc.gpsimd.tensor_copy(xnT2, core.xnT[:, ds(it * 2 * P, 2 * P)]).then_inc(G.sem, G.mark("xn"))
                sm.run_pool(pool, it)

        @block.tensor
        def _(pe):
            pe.sem_inc(T.sem, T.turn())
            with pe.Fori(0, PAIRS) as it:
                pe.wait_ge(V.sem, V.at("x1", it - 1))
                for n, wt in enumerate((wq, wk)):
                    for half in range(2):
                        for i in range(2):
                            mm = nc.tensor.matmul(ps[2 * n + half][:, i * 2 * P:(i + 1) * 2 * P],
                                                  wt[:, (2 * half + i) * P:(2 * half + i + 1) * P],
                                                  core.xnT[:, ds(it * 2 * P, 2 * P)], start=True, stop=True)
                        mm.then_inc(T.sem, T.mark("qk"[n] + str(half)))
                pe.wait_ge(G.sem, G.at("xn", it))
                for u in range(2):
                    nc.tensor.matmul(ps[4 + u][:, :], xnT2[:, u * P:(u + 1) * P], wv, start=True, stop=False)
                    nc.tensor.matmul(ps[4 + u][:, :], core.ones[0:1, 0:P], bv[0:1, :], start=False, stop=True) \
                        .then_inc(T.sem, T.mark(f"v{u}"))
                pe.wait_ge(V.sem, V.at("q3", it))
                pe.wait_ge(A.sem, A.at("v1", it))
                sm.run_pe(pe, it)
                for u in range(2):
                    pe.wait_ge(A.sem, A.at(f"oT{u}", it))
                    for i in range(4):
                        nc.tensor.matmul(ps[4 + u][:, 0:D], oT[:, u, i * P:(i + 1) * P], wo[:, i, :],
                                         start=(i == 0), stop=False)
                    nc.tensor.matmul(ps[4 + u][:, 0:D], core.ones[0:1, 0:P], bo[0:1, :], start=False, stop=True) \
                        .then_inc(T.sem, T.mark(f"y{u}"))

        @block.scalar
        def _(act):
            act.sem_inc(A.sem, A.turn())
            with act.Fori(0, PAIRS) as it:
                for n in range(4):
                    act.wait_ge(T.sem, T.at(f"k{n // 2}", it))
                    nc.scalar.activation(kT[:, n, :], ps[2 + n // 2][:, n % 2 * 2 * P:(n % 2 + 1) * 2 * P],
                                         ACT.Identity, bias=bk[:, n:n + 1]).then_inc(A.sem, A.mark(f"k{n}"))
                for u in range(2):
                    act.wait_ge(T.sem, T.at(f"v{u}", it))
                    nc.scalar.copy(v[:, u, :], ps[4 + u][:, :]).then_inc(A.sem, A.mark(f"v{u}"))
                sm.run_act(act, it)
                for u in range(2):
                    act.wait_ge(T.sem, T.at(f"o{4 * u + 3}", it))
                    nc.scalar.copy(oT[:, u, :], ps[2 + u][:, :]).then_inc(A.sem, A.mark(f"oT{u}"))

        @block.vector
        def _(dve):
            dve.sem_inc(V.sem, V.turn())
            with dve.Fori(0, PAIRS) as it:
                for n in range(4):
                    dve.wait_ge(T.sem, T.at(f"q{n // 2}", it))
                    nc.vector.tensor_scalar(qT[:, n, :], ps[n // 2][:, n % 2 * 2 * P:(n % 2 + 1) * 2 * P],
                                            bq[:, n:n + 1], SC, ALU.add, ALU.mult).then_inc(V.sem, V.mark(f"q{n}"))
                sm.run_dve(dve, it)
                for u in range(2):
                    dve.wait_ge(T.sem, T.at(f"y{u}", it))
                    xr = core.x[:, ds(it * 2 + u, 1), :].rearrange("p a d -> p (a d)")
                    nc.vector.tensor_tensor(xr, xr, ps[4 + u][:, 0:D], ALU.add).then_inc(V.sem, V.mark(f"x{u}"))

    kept = (G.sem, G.at(f"keep{len(groups) - 1}", PAIRS - 1))
    c.at = start
    VCH = 16
    HALF = VCH // 2
    out2, vecs = c.take(32, P), c.take(VCH, 32)
    turned = c.take(2, P, HALF)
    T = core.marks(f"{tag}_relv_pe", ["w0", "w1"])
    V = core.marks(f"{tag}_relv_dve", ["w0", "w1"])
    A = core.marks(f"{tag}_relv_act", ["p0", "p1"])
    G = core.marks(f"{tag}_relv_pool", ["vecs"])
    zeroed = core.sem(f"{tag}_relv_zeroed")
    with nc.Block(f"{tag}_relv", no_gpsimd_drain=True) as block:

        @block.gpsimd
        def _(pool):
            pool.sem_inc(G.sem, G.turn())
            nc.gpsimd.memset(vecs, 0.0).then_inc(zeroed, 1)
            pool.wait_ge(zeroed, 1)
            with pool.Fori(0, P // VCH) as it:
                pool.wait_ge(T.sem, T.at("w1", it - 1))
                nc.gpsimd.tensor_copy(vecs[:, :, 0:8], relv[:, ds(it * VCH, VCH), :]).then_inc(G.sem, G.mark("vecs"))

        @block.scalar
        def _(act):
            act.sem_inc(A.sem, A.turn())
            act.wait_ge(*kept)
            with act.Fori(0, P // VCH) as it:
                for n in range(2):
                    act.wait_ge(T.sem, T.at(f"w{n}", it - 1))
                    nc.scalar.copy(turned[:, n, :, :], rel3[:, :, ds(it * VCH + HALF * n, HALF)]) \
                        .then_inc(A.sem, A.mark(f"p{n}"))

        @block.tensor
        def _(pe):
            pe.sem_inc(T.sem, T.turn())
            with pe.Fori(0, P // VCH) as it:
                pe.wait_ge(G.sem, G.at("vecs", it))
                for n in range(2):
                    pe.wait_ge(A.sem, A.at(f"p{n}", it))
                    pe.wait_ge(V.sem, V.at(f"w{n}", it - 1))
                    probs = turned[:, n, :, :].rearrange("p (a c y z) t -> p a c y z t", a=2, c=4, y=2)
                    for i in range(HALF):
                        for j in range(4):
                            z = (j % 2) * 4
                            mm = nc.tensor.matmul(ps[n][32 * j:32 * j + 32, i * 32:(i + 1) * 32],
                                                  vecs[:, HALF * n + i, :], probs[:, :, :, j // 2, z:z + 4, i],
                                                  start=True, stop=True)
                    mm.then_inc(T.sem, T.mark(f"w{n}"))

        @block.vector
        def _(dve):
            dve.sem_inc(V.sem, V.turn())
            with dve.Fori(0, P // VCH) as it:
                for n in range(2):
                    dve.wait_ge(T.sem, T.at(f"w{n}", it))
                    nc.vector.tensor_copy(out2[:, :, ds(it * VCH + HALF * n, HALF)],
                                          ps[n][:, 0:32 * HALF].rearrange("p (t n) -> p n t", n=32)) \
                        .then_inc(V.sem, V.mark(f"w{n}"))

    done, added = core.sem(f"{tag}_relv_out"), core.sem(f"{tag}_relv_added")
    out4 = out2.rearrange("p (a c z) t -> p a c z t", a=2, c=4)
    with nc.Block(f"{tag}_relv_proj", no_gpsimd_drain=True) as block:

        @block.tensor
        def _(pe):
            for b in range(B):
                for i in range(4):
                    mm = nc.tensor.matmul(ps[b // 4][:, b % 4 * P:(b % 4 + 1) * P], out4[:, b % 2, i, b // 2, :],
                                          wo[:, i, :], start=(i == 0), stop=(i == 3))
                if b % 4 == 3:
                    mm.then_inc(done, 1)

        @block.vector
        def _(dve):
            for half in range(2):
                dve.wait_ge(done, half + 1)
                xs = core.x[:, half * 4:half * 4 + 4, :].rearrange("p b d -> p (b d)")
                nc.vector.tensor_tensor(xs, xs, ps[half][:, :], ALU.add).then_inc(added, 1)


def shift_tokens(core, tag, src, out, shift, outT=None, extra=None):
    nc, ps = core.nc, core.ps
    s_pe, s_dve, s_act = core.sem(f"{tag}_pe"), core.sem(f"{tag}_dve"), core.sem(f"{tag}_act")
    HF = D // 2
    with nc.Block(tag, no_gpsimd_drain=True) as block:

        @block.tensor
        def _(pe):
            nc.tensor.matmul(ps[0][:, :].rearrange("p (b d) -> p b d", d=HF), shift, src[:, :, HF:],
                             start=True, stop=True).then_inc(s_pe, 1)
            if outT is not None:
                pe.wait_ge(s_dve, 2)
                for b in range(B):
                    nc.tensor.transpose(ps[1 + b // 4][:, b % 4 * P:(b % 4 + 1) * P], out[:, b, :],
                                        core.ident[:, :]).then_inc(s_pe, 1)

        @block.vector
        def _(dve):
            nc.vector.tensor_copy(out[:, :, 0:HF], src[:, :, 0:HF]).then_inc(s_dve, 1)
            dve.wait_ge(s_pe, 1)
            nc.vector.tensor_copy(out[:, :, HF:], ps[0][:, :].rearrange("p (b d) -> p b d", d=HF)).then_inc(s_dve, 1)
            if extra is not None:
                extra(dve)
            if outT is not None:
                dve.wait_ge(s_pe, 1 + B)
                nc.vector.tensor_copy(outT[:, BANK:], ps[2][:, :]).then_inc(s_dve, 1)

        @block.scalar
        def _(act):
            if outT is not None:
                act.wait_ge(s_pe, 5)
                nc.scalar.copy(outT[:, 0:BANK], ps[1][:, :]).then_inc(s_act, 1)


def local_attention(core, tag, c, res, wqkv, wo, tables, bias):
    nc, ps = core.nc, core.ps
    H, K = 8, 64
    hT2 = c.take(2, P)
    sq = c.take(2 * BANK)
    ss, rn, half = c.take(2, 2 * H), c.take(2, 2 * H), c.take(2, 2 * H)
    unit_ = [c.take(H, K) for _ in range(4)]
    turned = [c.take(H, K) for _ in range(4)]
    qT, kT, v, oT = c.take(2, 4, P), c.take(2, 4, P), c.take(2, BANK), c.take(2, BANK)
    vs, as_, gs, ts = names_of(4, True, 4)
    QK = [(u, n) for u in range(2) for n in range(2)]
    V = core.marks(f"{tag}_dve", ["ss0", "ss1", "rn0", "rn1", "inv0n", "inv1n"] + [f"unit{u}{n}" for u, n in QK]
                   + [f"{a}{u}{n}" for u, n in QK for a in ("cos", "rot")] + ["kT0", "kT1"] + vs + ["x0", "x1"])
    A = core.marks(f"{tag}_act", ["sq0", "sq1", "v0", "v1", "qT0", "qT1"] + as_ + ["oT0", "oT1"])
    G = core.marks(f"{tag}_pool", ["copy", "root0", "root1"] + [f"sin{u}{n}" for u, n in QK] + gs)
    T = core.marks(f"{tag}_pe", [f"{n}{u}" for u in range(2) for n in "qkv"]
                   + ["tq0", "tk0", "tq1", "tk1"] + ts + ["y0", "y1"])
    groups = []
    for u in range(2):
        for par in range(2):
            r = slice(K * par, K * par + K)
            groups.append(dict(q=[qT[r, u, i, :] for i in range(4)], k=[kT[r, u, i, :] for i in range(4)],
                               v=[v[:, u, (2 * i + par) * K:(2 * i + par + 1) * K] for i in range(4)],
                               o=[ps[2 + u][r, i * P:(i + 1) * P] for i in range(4)]))
    sm = Softmax(core, c, groups, P, V, A, G, T, (6, 7, 4, 5), (0, 1), mask=lambda g: for_heads(bias))
    ready = core.sem(f"{tag}_constants")
    with nc.Block(tag, no_gpsimd_drain=True) as block:

        @block.gpsimd
        def _(pool):
            pool.sem_inc(G.sem, G.turn())
            nc.gpsimd.memset(half, 0.5).then_inc(ready, 1)
            pool.wait_ge(ready, 1)
            with pool.Fori(0, PAIRS) as it:
                pool.wait_ge(T.sem, T.at("v1", it - 1))
                nc.gpsimd.tensor_copy(hT2.rearrange("p a b -> p (a b)"), core.xnT[:, ds(it * 2 * P, 2 * P)]) \
                    .then_inc(G.sem, G.mark("copy"))
                for u in range(2):
                    pool.wait_ge(V.sem, V.at(f"ss{u}", it))
                    nc.gpsimd.tensor_tensor(rn[:, u, :], ss[:, u, :], half[:, u, :], ALU.pow) \
                        .then_inc(G.sem, G.mark(f"root{u}"))
                for u, n in QK:
                    pool.wait_ge(V.sem, V.at(f"unit{u}{n}", it))
                    src, dst, sin = unit_[2 * u + n], turned[2 * u + n], tables[2 * n + 1]
                    nc.gpsimd.tensor_tensor(dst[:, :, 0:32], src[:, :, 32:], for_heads(sin[:, 0:32], H), ALU.mult)
                    nc.gpsimd.tensor_tensor(dst[:, :, 32:], src[:, :, 0:32], for_heads(sin[:, 32:], H), ALU.mult) \
                        .then_inc(G.sem, G.mark(f"sin{u}{n}"))
                sm.run_pool(pool, it)

        @block.tensor
        def _(pe):
            pe.sem_inc(T.sem, T.turn())
            with pe.Fori(0, PAIRS) as it:
                pe.wait_ge(G.sem, G.at("copy", it))
                pe.wait_ge(V.sem, V.at("x1", it - 1))
                for u in range(2):
                    for n in range(3):
                        nc.tensor.matmul(ps[2 * n + u][:, :], hT2[:, u, :], wqkv[:, n * BANK:(n + 1) * BANK],
                                         start=True, stop=True).then_inc(T.sem, T.mark("qkv"[n] + str(u)))
                for u, n in QK:
                    pe.wait_ge(V.sem, V.at(f"rot{u}{n}", it))
                    for i in range(4):
                        mm = nc.tensor.transpose(ps[2 * n + u][:, i * P:(i + 1) * P],
                                                 unit_[2 * u + n].rearrange("p h k -> p (h k)")[:, i * P:(i + 1) * P],
                                                 core.ident[:, :])
                    mm.then_inc(T.sem, T.mark("t" + "qk"[n] + str(u)))
                pe.wait_ge(A.sem, A.at("qT1", it))
                pe.wait_ge(V.sem, V.at("kT1", it))
                sm.run_pe(pe, it)
                for u in range(2):
                    pe.wait_ge(A.sem, A.at(f"oT{u}", it))
                    for i in range(4):
                        mm = nc.tensor.matmul(ps[4 + u][:, 0:D], oT[:, u, i * P:(i + 1) * P], wo[:, i, :],
                                              start=(i == 0), stop=(i == 3))
                    mm.then_inc(T.sem, T.mark(f"y{u}"))

        @block.scalar
        def _(act):
            act.sem_inc(A.sem, A.turn())
            with act.Fori(0, PAIRS) as it:
                for u in range(2):
                    act.wait_ge(T.sem, T.at(f"k{u}", it))
                    if u == 1:
                        act.wait_ge(V.sem, V.at("ss0", it))
                    nc.scalar.activation(sq[:, 0:BANK], ps[u][:, :], ACT.Square)
                    nc.scalar.activation(sq[:, BANK:], ps[2 + u][:, :], ACT.Square).then_inc(A.sem, A.mark(f"sq{u}"))
                for u in range(2):
                    act.wait_ge(T.sem, T.at(f"v{u}", it))
                    nc.scalar.copy(v[:, u, :], ps[4 + u][:, :]).then_inc(A.sem, A.mark(f"v{u}"))
                for u in range(2):
                    act.wait_ge(T.sem, T.at(f"tq{u}", it))
                    nc.scalar.copy(qT[:, u].rearrange("p a b -> p (a b)"), ps[u][:, :]).then_inc(A.sem, A.mark(f"qT{u}"))
                sm.run_act(act, it)
                for u in range(2):
                    act.wait_ge(T.sem, T.at(f"o{2 * u + 1}", it))
                    nc.scalar.copy(oT[:, u, :], ps[2 + u][:, :]).then_inc(A.sem, A.mark(f"oT{u}"))

        @block.vector
        def _(dve):
            dve.sem_inc(V.sem, V.turn())
            dve.wait_ge(ready, 1)
            with dve.Fori(0, PAIRS) as it:
                for u in range(2):
                    dve.wait_ge(A.sem, A.at(f"sq{u}", it))
                    nc.vector.tensor_reduce(ss[:, u, :], sq.rearrange("p (n k) -> p n k", k=K), AX_X, ALU.add) \
                        .then_inc(V.sem, V.mark(f"ss{u}"))
                for u in range(2):
                    dve.wait_ge(G.sem, G.at(f"root{u}", it))
                    nc.vector.tensor_scalar(rn[:, u, :], rn[:, u, :], 1e-12, None, ALU.max) \
                        .then_inc(V.sem, V.mark(f"rn{u}"))
                for u in range(2):
                    dve.wait_ge(V.sem, V.at(f"rn{u}", it))
                    nc.vector.reciprocal(rn[:, u, :], rn[:, u, :]).then_inc(V.sem, V.mark(f"inv{u}n"))
                dve.wait_ge(V.sem, V.at("inv1n", it))
                for u, n in QK:
                    nc.vector.tensor_tensor(unit_[2 * u + n], ps[2 * n + u][:, :].rearrange("p (h k) -> p h k", k=K),
                                            rn[:, u, n * H:(n + 1) * H].unsqueeze(2).broadcast_to([P, H, K]),
                                            ALU.mult).then_inc(V.sem, V.mark(f"unit{u}{n}"))
                for u, n in QK:
                    dve.wait_ge(G.sem, G.at(f"sin{u}{n}", it))
                    nc.vector.tensor_tensor(unit_[2 * u + n], unit_[2 * u + n], for_heads(tables[2 * n], H),
                                            ALU.mult).then_inc(V.sem, V.mark(f"cos{u}{n}"))
                    dve.wait_ge(V.sem, V.at(f"cos{u}{n}", it))
                    nc.vector.tensor_tensor(unit_[2 * u + n], unit_[2 * u + n], turned[2 * u + n], ALU.add) \
                        .then_inc(V.sem, V.mark(f"rot{u}{n}"))
                for u in range(2):
                    dve.wait_ge(T.sem, T.at(f"tk{u}", it))
                    nc.vector.tensor_copy(kT[:, u].rearrange("p a b -> p (a b)"), ps[2 + u][:, :]) \
                        .then_inc(V.sem, V.mark(f"kT{u}"))
                sm.run_dve(dve, it)
                for u in range(2):
                    dve.wait_ge(T.sem, T.at(f"y{u}", it))
                    xr = res[:, ds(it * 2 + u, 1), :].rearrange("p a d -> p (a d)")
                    nc.vector.tensor_tensor(xr, xr, ps[4 + u][:, 0:D], ALU.add).then_inc(V.sem, V.mark(f"x{u}"))


def gated_ffn(core, tag, c, res, w1, ba, bg, w2, b2, widths):
    nc, ps = core.nc, core.ps
    HID, N = sum(widths), len(widths)
    gl, hT = c.take(2, BANK), [c.take(N, BANK) for _ in range(2)]
    pe_up, act_gelu, dve_gate, pe_down, dve_add = (core.sem(f"{tag}_{n}") for n in ("up", "gelu", "gate", "down", "add"))
    with nc.Block(tag, no_gpsimd_drain=True) as block:

        @block.tensor
        def _(pe):
            for half in range(2):
                for i, m in enumerate(widths):
                    n = half * N + i
                    if n >= 2:
                        pe.wait_ge(dve_gate, n - 1)
                    for part in range(2):
                        mm = nc.tensor.matmul(ps[2 * (n % 2) + part][0:m, :],
                                              w1[:, part * HID + i * P:part * HID + i * P + m],
                                              core.xnT[:, half * BANK:(half + 1) * BANK], start=True, stop=True)
                    mm.then_inc(pe_up, 1)
            for half in range(2):
                pe.wait_ge(dve_gate, N * (half + 1))
                for t in range(4):
                    for i, m in enumerate(widths):
                        nc.tensor.matmul(ps[4 + half][:, t * P:(t + 1) * P], hT[half][0:m, i, t * P:(t + 1) * P],
                                         w2[0:m, i, :], start=(i == 0), stop=False)
                    mm = nc.tensor.matmul(ps[4 + half][:, t * P:(t + 1) * P], core.ones[0:1, 0:P], b2[0:1, :],
                                          start=False, stop=True)
                mm.then_inc(pe_down, 1)

        @block.scalar
        def _(act):
            for n in range(2 * N):
                i, m = n % N, widths[n % N]
                act.wait_ge(pe_up, n + 1)
                if n >= 2:
                    act.wait_ge(dve_gate, n - 1)
                nc.scalar.activation(gl[0:m, n % 2, :], ps[2 * (n % 2) + 1][0:m, :], ACT.Gelu, bias=bg[0:m, i:i + 1]) \
                    .then_inc(act_gelu, 1)

        @block.vector
        def _(dve):
            for n in range(2 * N):
                i, m = n % N, widths[n % N]
                dve.wait_ge(act_gelu, n + 1)
                nc.vector.scalar_tensor_tensor(out=hT[n // N][0:m, i, :], in0=ps[2 * (n % 2)][0:m, :],
                                               scalar=ba[0:m, i:i + 1], in1=gl[0:m, n % 2, :],
                                               op0=ALU.add, op1=ALU.mult).then_inc(dve_gate, 1)
            for half in range(2):
                dve.wait_ge(pe_down, half + 1)
                xs = res[:, half * 4:half * 4 + 4, :].rearrange("p b d -> p (b d)")
                nc.vector.tensor_tensor(xs, xs, ps[4 + half][:, :], ALU.add).then_inc(dve_add, 1)


def layer_l1_ffn(core, tag, w):
    nc = core.nc
    DEPTH, HID, K = 2, 341, 64
    widths = [P, P, HID - 2 * P]
    c = Carve(core.scratch)
    res, shifted = c.take(B, D), c.take(B, D)
    tables = [c.take(K) for _ in range(4)]
    base = [w.take(K) for _ in range(4)]
    bias, shift = w.take(P), w.take(P)
    start = c.at
    layernorm_all(core, tag, out=res)
    for d in range(DEPTH):
        wqkv, wo, w1, w2 = w.take(3 * BANK), w.take(4, D), w.take(2 * HID), w.take(3, D)
        ba, bg, b2, lg, lb = w.take(3), w.take(3), w.take(D), w.take(1), w.take(1)
        gains = [w.take(K) for _ in range(4)]
        made = core.sem(f"{tag}{d}_tables")
        if d == 0:
            with nc.Block(f"{tag}_weights", no_gpsimd_drain=True) as block:

                @block.tensor
                def _(pe):
                    pe.wait_ge(*core.w_loaded[tag])

                @block.vector
                def _(dve):
                    dve.wait_ge(*core.w_loaded[tag])

        def make_tables(dve):
            for n in range(4):
                nc.vector.tensor_tensor(tables[n], base[n], gains[n], ALU.mult).then_inc(made, 1)

        shift_tokens(core, f"{tag}{d}_shift", res, shifted, shift, outT=core.xnT, extra=make_tables)
        c.at = start
        local_attention(core, f"{tag}{d}_attn", c, res, wqkv, wo, tables, bias)
        shift_tokens(core, f"{tag}{d}_shift2", res, shifted, shift)
        layernorm_all(core, f"{tag}{d}_norm", src=shifted, out=shifted, gain=lg, bias=lb)
        c.at = start
        gated_ffn(core, f"{tag}{d}_ffn", c, res, w1, ba, bg, w2, b2, widths)
    added = core.sem(f"{tag}_added")
    with nc.Block(f"{tag}_add", no_gpsimd_drain=True) as block:

        @block.vector
        def _(dve):
            nc.vector.tensor_tensor(core.x[:, :, :], core.x[:, :, :], res, ALU.add).then_inc(added, 1)


def conv_kernels(core, tag, c, log_dt, a_re, a_im, c_re, c_im, skip):
    nc = core.nc
    N, R, S = 64, 16, P // 16
    PI = float(np.pi)
    ROUND = 1.5 * 2 ** 23
    TAU_HI = 6.28125
    TAU_LO = 2 * PI - TAU_HI
    dt, ar, ai, er = c.take(1), c.take(N), c.take(N), c.take(N)
    ang, turns = c.take(2, N), c.take(2, N)
    t = [c.take(R // 2, N) for _ in range(4)]
    z = c.take(R, 2 * N)
    wa = c.take(S, 2 * N)
    pw = c.take(2, 2 * N)
    den, kp = c.take(N), c.take(2 * P)
    prod = [c.take(R, 2 * N) for _ in range(2)]
    chain, scaled, exped, sined, made, summed, stored = (
        core.sem(f"{tag}_{n}") for n in ("chain", "angles", "exp", "sin", "products", "sums", "stored"))
    with nc.Block(tag, no_gpsimd_drain=True) as block:

        @block.scalar
        def _(act):
            act.wait_ge(*core.w_loaded["l1_xattn"])
            nc.scalar.activation(dt, log_dt, ACT.Exp).then_inc(exped, 1)
            act.wait_ge(scaled, 1)
            nc.scalar.activation(er, ar, ACT.Exp).then_inc(exped, 1)
            act.wait_ge(scaled, 2)
            nc.scalar.activation(ang, ang, ACT.Sin).then_inc(sined, 1)

        @block.vector
        def _(dve):
            link = Link(dve, chain)
            tt, ts, stt = nc.vector.tensor_tensor, nc.vector.tensor_scalar, nc.vector.scalar_tensor_tensor

            def cmul(out, a, b):
                sh = out[0].shape
                u = [x[:, 0:sh[1]] if len(sh) == 3 else x[:, 0] for x in t]
                link(tt(u[0], a[0], b[0], ALU.mult))
                link(tt(u[1], a[1], b[1], ALU.mult))
                link(tt(u[2], a[0], b[1], ALU.mult))
                link(tt(u[3], a[1], b[0], ALU.mult))
                link(tt(out[0], u[0], u[1], ALU.subtract))
                link(tt(out[1], u[2], u[3], ALU.add))

            def pair(v):
                return v[:, 0:N], v[:, N:2 * N]

            dve.wait_ge(exped, 1)
            ts(ar, a_re, dt, None, ALU.mult).then_inc(scaled, 1)
            link(ts(ai, a_im, dt, None, ALU.mult))
            link(ts(ang[:, 0], ai, 0.0, None, ALU.add))
            link(ts(ang[:, 1], ai, PI / 2, None, ALU.add))
            link(ts(turns, ang, 1 / (2 * PI), None, ALU.mult))
            link(ts(turns, turns, ROUND, None, ALU.add))
            link(ts(turns, turns, ROUND, None, ALU.subtract))
            link(stt(ang, turns, -TAU_HI, ang, ALU.mult, ALU.add))
            link(stt(ang, turns, -TAU_LO, ang, ALU.mult, ALU.add))
            ts(ang, ang, -3.1415925, 3.1415925, ALU.max, ALU.min).then_inc(scaled, 1)
            dve.wait_ge(exped, 2)
            dve.wait_ge(sined, 1)
            one = pair(z[:, 1])
            link(tt(one[0], er, ang[:, 1], ALU.mult))
            link(tt(one[1], er, ang[:, 0], ALU.mult))
            link(ts(ar, one[0], -1.0, None, ALU.add))
            w0 = pair(wa[:, 0])
            cmul(w0, (c_re, c_im), (ar, one[1]))
            link(tt(den, a_re, a_re, ALU.mult))
            link(tt(er, a_im, a_im, ALU.mult))
            link(tt(den, den, er, ALU.add))
            link(nc.vector.reciprocal(den, den))
            link(ts(den, den, 2.0, None, ALU.mult))
            link(ts(ai, a_im, -1.0, None, ALU.mult))
            cmul((ang[:, 0], ang[:, 1]), w0, (a_re, ai))
            link(tt(w0[0], ang[:, 0], den, ALU.mult))
            link(tt(ang[:, 1], ang[:, 1], den, ALU.mult))
            link(ts(w0[1], ang[:, 1], -1.0, None, ALU.mult))
            link(nc.vector.memset(z[:, 0, 0:N], 1.0))
            link(nc.vector.memset(z[:, 0, N:], 0.0))
            cmul(pair(pw[:, 0]), one, one)
            k, at = 2, 0
            while k < R:
                lo, hi = z[:, 0:k], z[:, k:2 * k]
                p = [x.unsqueeze(1).broadcast_to([P, k, N]) for x in pair(pw[:, at])]
                cmul((hi[:, :, 0:N], hi[:, :, N:]), (lo[:, :, 0:N], lo[:, :, N:]), p)
                cmul(pair(pw[:, 1 - at]), pair(pw[:, at]), pair(pw[:, at]))
                k, at = 2 * k, 1 - at
            q = pair(pw[:, at])
            link(ts(q[1], q[1], -1.0, None, ALU.mult))
            for a in range(1, S):
                cmul(pair(wa[:, a]), pair(wa[:, a - 1]), q)
            link(nc.vector.memset(kp, 0.0))
            for a in range(S):
                dst = prod[a % 2]
                link(tt(dst, z, wa[:, a].unsqueeze(1).broadcast_to([P, R, 2 * N]), ALU.mult))
                link(nc.vector.tensor_reduce(kp[:, P - 1 + R * a:P - 1 + R * (a + 1)], dst, AX_X, ALU.add))
            tt(kp[:, P - 1:P], kp[:, P - 1:P], skip, ALU.add).then_inc(summed, 1)

        @block.sync
        def _(sp):
            sp.wait_ge(summed, 1)
            sp.dma_start(core.conv_dram.ap(), kp).then_inc(stored, 16)
            sp.wait_ge(stored, 16)


def top_attention(core, tag, c, wq, wk, wv, wfi, bfi, wfo, bfo, gate, ln, u_all, film_out):
    nc, ps = core.nc, core.ps
    H, K, TOP = 4, 32, 32
    ctx2, bias2 = c.take(2 * P), c.take(2, P)
    qT, kT, v = c.take(2 * P), c.take(2 * P), c.take(2, P)
    s, e, left = c.take(H, 2, P), c.take(H, 2, P), c.take(H, 2, P)
    best, best0 = c.take(2 * H, 8), c.take(2 * H, 8)
    nmax, tot = c.take(2 * H), c.take(2 * H)
    mean, meanT, ctT = c.take(2, P), c.take(2, P), c.take(2, P)
    carrier = c.take(1)
    HU = [(h, u) for h in range(H) for u in range(2)]
    V = core.marks(f"{tag}_dve", ["k"] + [f"s{h}" for h in range(H)]
                   + [f"{n}{i}" for r in range(TOP // 8) for n in ("top", "out") for i in (r,)] + ["nmax", "kept", "prob"]
                   + ["tot", "inv", "quarter", "coef"] + [f"mean{h}" for h in range(H)] + ["meanT"]
                   + [f"{n}{u}" for u in range(2) for n in ("sc", "mod", "u")])
    A = core.marks(f"{tag}_act", ["q", "v", "exp", "ctT", "fo0", "fo1", "fo2", "fo3"])
    G = core.marks(f"{tag}_pool", ["copies"])
    T = core.marks(f"{tag}_pe", ["qk", "v", "s", "meanT", "ct", "film0", "film1"])
    with nc.Block(tag, no_gpsimd_drain=True) as block:

        @block.gpsimd
        def _(pool):
            pool.sem_inc(G.sem, G.turn())
            with pool.Fori(0, PAIRS) as it:
                pool.wait_ge(T.sem, T.at("v", it - 1))
                pool.wait_ge(V.sem, V.at(f"s{H - 1}", it - 1))
                nc.gpsimd.tensor_copy(ctx2[:CTX, :], core.ctxT[:CTX, ds(it * 2 * P, 2 * P)])
                nc.gpsimd.tensor_copy(bias2.rearrange("p a b -> p (a b)"),
                                      core.ctx_bias[:, ds(it * 2 * P, 2 * P)]).then_inc(G.sem, G.mark("copies"))

        @block.tensor
        def _(pe):
            pe.sem_inc(T.sem, T.turn())
            with pe.Fori(0, PAIRS) as it:
                pe.wait_ge(A.sem, A.at("fo3", it - 1))
                pe.wait_ge(V.sem, V.at("u1", it - 1))
                nc.tensor.matmul(ps[0][:, 0:2 * P], wq, core.xnT[:, ds(it * 2 * P, 2 * P)], start=True, stop=True)
                nc.tensor.matmul(ps[0][:, 2 * P:], wk[:CTX, :], core.ctxT[:CTX, ds(it * 2 * P, 2 * P)],
                                 start=True, stop=True).then_inc(T.sem, T.mark("qk"))
                pe.wait_ge(G.sem, G.at("copies", it))
                for u in range(2):
                    mm = nc.tensor.matmul(ps[1][:, u * P:(u + 1) * P], ctx2[:CTX, u * P:(u + 1) * P], wv[:CTX, :],
                                          start=True, stop=True)
                mm.then_inc(T.sem, T.mark("v"))
                pe.wait_ge(A.sem, A.at("q", it))
                pe.wait_ge(V.sem, V.at("k", it))
                for h, u in HU:
                    r, tok = slice(K * h, K * h + K), slice(u * P, (u + 1) * P)
                    mm = nc.tensor.matmul(ps[2 + h][:, tok], qT[r, tok], kT[r, tok], start=True, stop=True)
                mm.then_inc(T.sem, T.mark("s"))
                pe.wait_ge(V.sem, V.at(f"mean{H - 1}", it))
                for u in range(2):
                    mm = nc.tensor.transpose(ps[6][:, u * P:(u + 1) * P], mean[:, u, :], core.ident[:, :])
                mm.then_inc(T.sem, T.mark("meanT"))
                pe.wait_ge(V.sem, V.at("meanT", it))
                for u in range(2):
                    mm = nc.tensor.matmul(ps[7][:, u * P:(u + 1) * P], v[:, u, :], meanT[:, u, :],
                                          start=True, stop=True)
                mm.then_inc(T.sem, T.mark("ct"))
                pe.wait_ge(A.sem, A.at("ctT", it))
                for n, (wf, bf) in enumerate(((wfi, bfi), (wfo, bfo))):
                    for u in range(2):
                        bank = ps[2 * n + u][:, 0:2 * P]
                        nc.tensor.matmul(bank, ctT[:, u, :], wf, start=True, stop=False)
                        mm = nc.tensor.matmul(bank, core.ones[0:1, 0:P], bf[0:1, :], start=False, stop=True)
                    mm.then_inc(T.sem, T.mark(f"film{n}"))

        @block.scalar
        def _(act):
            act.sem_inc(A.sem, A.turn())
            with act.Fori(0, PAIRS) as it:
                act.wait_ge(T.sem, T.at("qk", it))
                nc.scalar.mul(qT, ps[0][:, 0:2 * P], K ** -0.5).then_inc(A.sem, A.mark("q"))
                act.wait_ge(T.sem, T.at("v", it))
                nc.scalar.copy(v.rearrange("p a b -> p (a b)"), ps[1][:, 0:2 * P]).then_inc(A.sem, A.mark("v"))
                act.wait_ge(V.sem, V.at("nmax", it))
                for i, (h, u) in enumerate(HU):
                    a = nc.scalar.activation(e[:, h, u, :], s[:, h, u, :], ACT.Exp, bias=nmax[:, i:i + 1])
                a.then_inc(A.sem, A.mark("exp"))
                act.wait_ge(T.sem, T.at("ct", it))
                nc.scalar.copy(ctT.rearrange("p a b -> p (a b)"), ps[7][:, 0:2 * P]).then_inc(A.sem, A.mark("ctT"))
                act.wait_ge(T.sem, T.at("film1", it))
                for u in range(2):
                    dst = film_out[:, ds(it * 2 + u, 1), :].rearrange("p a d -> p (a d)")
                    nc.scalar.activation(dst[:, 0:P], ps[2 + u][:, 0:P], ACT.Identity, scale=gate, bias=core.ones[:, 0:1]) \
                        .then_inc(A.sem, A.mark(f"fo{2 * u}"))
                    nc.scalar.activation(dst[:, P:], ps[2 + u][:, P:2 * P], ACT.Copy, scale=gate) \
                        .then_inc(A.sem, A.mark(f"fo{2 * u + 1}"))

        @block.vector
        def _(dve):
            dve.sem_inc(V.sem, V.turn())
            with dve.Fori(0, PAIRS) as it:
                dve.wait_ge(A.sem, A.at("q", it))
                nc.vector.tensor_copy(kT, ps[0][:, 2 * P:]).then_inc(V.sem, V.mark("k"))
                dve.wait_ge(T.sem, T.at("s", it))
                dve.wait_ge(G.sem, G.at("copies", it))
                for h in range(H):
                    nc.vector.tensor_tensor(s[:, h], ps[2 + h][:, 0:2 * P].rearrange("p (a b) -> p a b", a=2), bias2,
                                            ALU.add).then_inc(V.sem, V.mark(f"s{h}"))
                dve.wait_ge(V.sem, V.at(f"s{H - 1}", it))
                nc.vector.memset(carrier, 0.0)
                for r in range(TOP // 8):
                    src, top = (s, best0) if r == 0 else (left, best)
                    for i, (h, u) in enumerate(HU):
                        m = nc.vector.max(top[:, i, :], src[:, h, u, :])
                    m.then_inc(V.sem, V.mark(f"top{r}"))
                    dve.wait_ge(V.sem, V.at(f"top{r}", it))
                    nc.vector.memset(carrier, 0.0)
                    for i, (h, u) in enumerate(HU):
                        m = nc.vector.match_replace(left[:, h, u, :], top[:, i, :], src[:, h, u, :], -FLT_MAX)
                    m.then_inc(V.sem, V.mark(f"out{r}"))
                    dve.wait_ge(V.sem, V.at(f"out{r}", it))
                    nc.vector.memset(carrier, 0.0)
                nc.vector.tensor_scalar(nmax, best0[:, :, 0], -1.0, None, ALU.mult).then_inc(V.sem, V.mark("nmax"))
                nc.vector.tensor_tensor(left, s, left, ALU.not_equal).then_inc(V.sem, V.mark("kept"))
                dve.wait_ge(A.sem, A.at("exp", it))
                dve.wait_ge(V.sem, V.at("kept", it))
                nc.vector.tensor_tensor(e, e, left, ALU.mult).then_inc(V.sem, V.mark("prob"))
                dve.wait_ge(V.sem, V.at("prob", it))
                nc.vector.tensor_reduce(tot, e.rearrange("p h u k -> p (h u) k"), AX_X, ALU.add) \
                    .then_inc(V.sem, V.mark("tot"))
                dve.wait_ge(V.sem, V.at("tot", it))
                nc.vector.reciprocal(tot, tot).then_inc(V.sem, V.mark("inv"))
                dve.wait_ge(V.sem, V.at("inv", it))
                nc.vector.tensor_scalar(tot, tot, 1.0 / H, None, ALU.mult).then_inc(V.sem, V.mark("quarter"))
                dve.wait_ge(V.sem, V.at("quarter", it))
                hu = tot.rearrange("p (h u) -> p h u", u=2)
                nc.vector.tensor_tensor(hu, hu, core.text_on[:, ds(it * 2, 2)].unsqueeze(1).broadcast_to([P, H, 2]),
                                        ALU.mult).then_inc(V.sem, V.mark("coef"))
                dve.wait_ge(V.sem, V.at("coef", it))
                for h in range(H):
                    for u in range(2):
                        w = tot[:, 2 * h + u:2 * h + u + 1]
                        if h == 0:
                            m = nc.vector.tensor_scalar(mean[:, u, :], e[:, h, u, :], w, None, ALU.mult)
                        else:
                            m = nc.vector.scalar_tensor_tensor(out=mean[:, u, :], in0=e[:, h, u, :], scalar=w,
                                                               in1=mean[:, u, :], op0=ALU.mult, op1=ALU.add)
                    m.then_inc(V.sem, V.mark(f"mean{h}"))
                    dve.wait_ge(V.sem, V.at(f"mean{h}", it))
                dve.wait_ge(T.sem, T.at("meanT", it))
                nc.vector.tensor_copy(meanT.rearrange("p a b -> p (a b)"), ps[6][:, 0:2 * P]) \
                    .then_inc(V.sem, V.mark("meanT"))
                dve.wait_ge(T.sem, T.at("film0", it))
                for u in range(2):
                    sc = s[:, 0, u, :]
                    dst = u_all[:, ds(it * 2 + u, 1), :].rearrange("p a d -> p (a d)")
                    row = ln[:, ds(it * 2 + u, 1), :].rearrange("p a d -> p (a d)")
                    nc.vector.tensor_scalar(sc, ps[u][:, 0:P], gate, 1.0, ALU.mult, ALU.add) \
                        .then_inc(V.sem, V.mark(f"sc{u}"))
                    dve.wait_ge(V.sem, V.at(f"sc{u}", it))
                    nc.vector.tensor_tensor(sc, sc, row, ALU.mult).then_inc(V.sem, V.mark(f"mod{u}"))
                    dve.wait_ge(V.sem, V.at(f"mod{u}", it))
                    nc.vector.scalar_tensor_tensor(out=dst, in0=ps[u][:, P:2 * P], scalar=gate, in1=sc,
                                                   op0=ALU.mult, op1=ALU.add).then_inc(V.sem, V.mark(f"u{u}"))


def causal_conv(core, tag, c, u, y, flip):
    nc, ps = core.nc, core.ps
    CHN = 16
    BUFS = 4
    rev = c.take(B, D)
    toe = [c.take(CHN, P) for _ in range(BUFS)]
    loads = [core.sem(f"{tag}_toeplitz{s}") for s in range(BUFS)]
    turned, copied = core.sem(f"{tag}_reversed"), core.sem(f"{tag}_reversed_out")
    T = core.marks(f"{tag}_pe", [f"y{s}" for s in range(BUFS)])
    V = core.marks(f"{tag}_dve", [f"y{s}" for s in range(BUFS)])
    TURNS = D // (CHN * BUFS)
    with nc.Block(tag, no_gpsimd_drain=True) as block:

        @block.sync
        def _(sp):
            for it in range(TURNS):
                for s in range(BUFS):
                    if it:
                        sp.wait_ge(T.sem, T.at(f"y{s}", it - 1))
                    src = bass.AP(tensor=core.conv_dram.ap().tensor, offset=(it * BUFS + s) * CHN * 2 * P,
                                  ap=[[1, P], [2 * P, CHN], [1, P]])
                    sp.dma_start(toe[s], src).then_inc(loads[s], 16)

        @block.tensor
        def _(pe):
            pe.sem_inc(T.sem, T.turn())
            for half in range(2):
                mm = nc.tensor.matmul(ps[4 + half][:, :], flip,
                                      u[:, 4 * half:4 * half + 4, :].rearrange("p b d -> p (b d)"),
                                      start=True, stop=True)
            mm.then_inc(turned, 1)
            pe.wait_ge(copied, 2)
            with pe.Fori(0, TURNS) as it:
                for s in range(BUFS):
                    pe.wait_ge(loads[s], it * 16 + 16)
                    pe.wait_ge(V.sem, V.at(f"y{s}", it - 1))
                    for i in range(CHN):
                        mm = nc.tensor.matmul(ps[s][:, i * B:(i + 1) * B], toe[s][:, i, :],
                                              rev[:, :, ds(it * (BUFS * CHN) + (s * CHN + i), 1)]
                                              .rearrange("p b a -> p (b a)"), start=True, stop=True)
                    mm.then_inc(T.sem, T.mark(f"y{s}"))

        @block.vector
        def _(dve):
            dve.sem_inc(V.sem, V.turn())
            dve.wait_ge(turned, 1)
            for half in range(2):
                nc.vector.tensor_copy(rev[:, 4 * half:4 * half + 4, :].rearrange("p b d -> p (b d)"),
                                      ps[4 + half][:, :]).then_inc(copied, 1)
            with dve.Fori(0, TURNS) as it:
                for s in range(BUFS):
                    dve.wait_ge(T.sem, T.at(f"y{s}", it))
                    nc.vector.tensor_copy(y[:, :, ds(it * (BUFS * CHN) + s * CHN, CHN)],
                                          ps[s][:, 0:CHN * B].rearrange("p (d b) -> p b d", b=B)) \
                        .then_inc(V.sem, V.mark(f"y{s}"))


def plain_ffn(core, tag, c, res, w1, b1, w2, b2):
    nc, ps = core.nc, core.ps
    HC = 4
    hT = [c.take(HC, BANK) for _ in range(2)]
    up, gelu, down, add = (core.sem(f"{tag}_{n}") for n in ("up", "gelu", "down", "add"))
    with nc.Block(tag, no_gpsimd_drain=True) as block:

        @block.tensor
        def _(pe):
            for n in range(2 * HC):
                half, i = n // HC, n % HC
                if n >= 4:
                    pe.wait_ge(gelu, n - 3)
                nc.tensor.matmul(ps[n % 4][:, :], w1[:, i * P:(i + 1) * P],
                                 core.xnT[:, half * BANK:(half + 1) * BANK], start=True, stop=True).then_inc(up, 1)
            for half in range(2):
                pe.wait_ge(gelu, HC * (half + 1))
                for t in range(4):
                    bank = ps[4 + half][:, t * P:(t + 1) * P]
                    for i in range(HC):
                        nc.tensor.matmul(bank, hT[half][:, i, t * P:(t + 1) * P], w2[:, i, :],
                                         start=(i == 0), stop=False)
                    mm = nc.tensor.matmul(bank, core.ones[0:1, 0:P], b2[0:1, :], start=False, stop=True)
                mm.then_inc(down, 1)

        @block.scalar
        def _(act):
            for n in range(2 * HC):
                act.wait_ge(up, n + 1)
                nc.scalar.activation(hT[n // HC][:, n % HC, :], ps[n % 4][:, :], ACT.Gelu,
                                     bias=b1[:, n % HC:n % HC + 1]).then_inc(gelu, 1)

        @block.vector
        def _(dve):
            for half in range(2):
                dve.wait_ge(down, half + 1)
                xs = res[:, half * 4:half * 4 + 4, :].rearrange("p b d -> p (b d)")
                nc.vector.tensor_tensor(xs, xs, ps[4 + half][:, :], ALU.add).then_inc(add, 1)


def layer_l1_xattn(core, tag, w):
    nc = core.nc
    c = Carve(core.scratch)
    wq, wk, wv = w.take(P), w.take(P), w.take(P)
    wfi, bfi, wfo, bfo = w.take(2 * P), w.take(2 * P), w.take(2 * P), w.take(2 * P)
    w1, w2, b1, b2, gf, bf = w.take(4 * P), w.take(4, D), w.take(4), w.take(D), w.take(1), w.take(1)
    g_in, b_in, g_out, b_out = (w.take(D) for _ in range(4))
    gate, log_dt = w.take(1), w.take(1)
    ssm = [w.take(64) for _ in range(4)]
    skip, flip = w.take(1), w.take(P)
    ln, u, y, film_out = c.take(B, D), c.take(B, D), c.take(B, D), c.take(B, 2 * D)
    start = c.at
    every = lambda a: a.unsqueeze(1).broadcast_to([P, B, D])
    layernorm_all(core, tag)
    layernorm_all(core, f"{tag}_in", src=core.xn, out=ln, turn=False)
    conv_kernels(core, f"{tag}_kernels", c, log_dt, *ssm, skip)
    c.at = start
    affine = core.sem(f"{tag}_affine")
    with nc.Block(f"{tag}_affine", no_gpsimd_drain=True) as block:

        @block.vector
        def _(dve):
            link = Link(dve, affine)
            link(nc.vector.tensor_tensor(ln, ln, every(g_in), ALU.mult))
            link(nc.vector.tensor_tensor(ln, ln, every(b_in), ALU.add))

    top_attention(core, f"{tag}_top", c, wq, wk, wv, wfi, bfi, wfo, bfo, gate, ln, u, film_out)
    c.at = start
    causal_conv(core, f"{tag}_conv", c, u, y, flip)
    modulated = core.sem(f"{tag}_modulated")
    with nc.Block(f"{tag}_mod", no_gpsimd_drain=True) as block:

        @block.vector
        def _(dve):
            link = Link(dve, modulated)
            link(nc.vector.tensor_tensor(y, y, film_out[:, :, 0:D], ALU.mult))
            link(nc.vector.tensor_tensor(y, y, film_out[:, :, D:], ALU.add))
            link(nc.vector.tensor_tensor(y, y, core.xn[:, :, :], ALU.add))

    layernorm_all(core, f"{tag}_mid", src=y, out=ln, gain=gf, bias=bf)
    c.at = start
    plain_ffn(core, f"{tag}_ffn", c, y, w1, b1, w2, b2)
    layernorm_all(core, f"{tag}_out", src=y, out=ln, turn=False)
    added = core.sem(f"{tag}_added")
    with nc.Block(f"{tag}_add", no_gpsimd_drain=True) as block:

        @block.vector
        def _(dve):
            link = Link(dve, added)
            link(nc.vector.tensor_tensor(ln, ln, every(g_out), ALU.mult))
            link(nc.vector.tensor_tensor(ln, ln, every(b_out), ALU.add))
            link(nc.vector.tensor_tensor(core.x[:, :, :], core.x[:, :, :], ln, ALU.add))


def wide(*parts):
    out = []
    for a in parts:
        a = np.asarray(a)
        a = a.reshape(a.shape[0], -1)
        out.append(np.pad(a, ((0, P - a.shape[0]), (0, 0))))
    return np.ascontiguousarray(np.concatenate(out, 1))


def rows(a):
    a = np.asarray(a)
    return a.reshape(-1, P, a.shape[-1]).transpose(1, 0, 2).reshape(P, -1)


def lay_weights(i):
    g = {k: np.asarray(v) for k, v in i.items()}
    lay = {}
    lay["l0_xattn"] = wide(g["L0_xattn_Wq"], g["L0_xattn_Wk"], g["L0_xattn_Wv"],
                           rows(g["L0_xattn_Wout"]), g["L0_xattn_bout"][None])
    lay["l2_xattn"] = wide(cols32(g["L2_xattn_Wq"]), cols32(g["L2_xattn_Wk"]), cols32(g["L2_xattn_Wv"]),
                           rows(cols32(g["L2_xattn_Wo"].T).T))
    lay["l2_ffn"] = wide(g["L2_ffn_gate_w"])
    tri = np.triu(np.ones((P, P), np.float32))
    lay["l3_ffn"] = wide(g["L3_ffn_w_g"], tri)
    lay["l0_ffn"] = wide(g["L0_ffn_router_w"].T, g["L0_ffn_b1"].reshape(8, 4, P).transpose(2, 0, 1), g["L0_ffn_b2"])
    lay["l0_attn"] = wide(g["L0_attn_Wq"], g["L0_attn_Wk"], rows(g["L0_attn_Wv"].T), rows(g["L0_attn_Wo"]))
    heads = lambda a: a.transpose(1, 0, 2).reshape(D, 16 * 64)
    pos = np.arange(P) % 8 * 16 + np.arange(P) // 8
    interleaved = np.where(pos[:, None] >= pos[None, :], 0.0, -FLT_MAX).astype(np.float32)
    lay["l1_attn"] = wide(*[heads(g[f"L1_attn_W{n}"]) for n in "qkv"],
                          g["L1_attn_proj_w"].T.reshape(16, 64, D).transpose(1, 0, 2),
                          g["L1_attn_proj_b"][None], interleaved)
    twice = lambda a: np.concatenate([a, a])[:, None]
    lkv = g["L3_xattn_Wlkv"].T
    lay["l3_xattn"] = wide(g["L3_xattn_Wq"].T, lkv, g["L3_xattn_Wkv"].T, g["L3_xattn_Wo"].T, g["L3_xattn_bo"][None],
                           *[g[f"L3_xattn_ln_{n}"][:, None] for n in ("x_g", "x_b", "l_g", "l_b")],
                           twice(g["L3_xattn_qn_g"]), twice(g["L3_xattn_kn_g"]))
    t = np.arange(P)
    seen = (t[:, None] >= t[None, :]) & (t[:, None] <= t[None, :] + 64)
    parts = [*xpos_tables(), np.where(seen, 0.0, -FLT_MAX).astype(np.float32), np.eye(P, k=1, dtype=np.float32)]
    swapped = lambda a: np.concatenate([a[32:], a[:32]])
    every = lambda a: np.broadcast_to(a[None], (P, a.shape[0]))
    for d in range(2):
        b1 = np.pad(g["L1_ffn_b1"][d].reshape(2, 341), ((0, 0), (0, 43))).reshape(2, 3, P)
        qs, ks = g["L1_ffn_q_scale"][d], g["L1_ffn_k_scale"][d]
        parts += [g["L1_ffn_wqkv"][d], rows(g["L1_ffn_wo"][d]), g["L1_ffn_w1"][d],
                  rows(np.pad(g["L1_ffn_w2"][d], ((0, 43), (0, 0)))), b1[0].T, b1[1].T, g["L1_ffn_b2"][d][None],
                  g["L1_ffn_ln_g"][d][:, None], g["L1_ffn_ln_b"][d][:, None],
                  every(qs), every(swapped(qs)), every(ks), every(swapped(ks))]
    lay["l1_ffn"] = wide(*parts)
    n = "L1_xattn_"
    lay["l1_xattn"] = wide(
        g[n + "Wq"], g[n + "Wk"], g[n + "Wv"], g[n + "W_film_in"], g[n + "b_film_in"][None],
        g[n + "W_film_out"], g[n + "b_film_out"][None], g[n + "W1"], rows(g[n + "W2"]),
        g[n + "b1"].reshape(4, P).T, g[n + "b2"][None], g[n + "g_ffn"][:, None], g[n + "b_ffn"][:, None],
        *[every(g[n + m]) for m in ("g_norm_in", "b_norm_in", "g_norm_out", "b_norm_out")],
        every(g[n + "mod_gate"].reshape(1)), g[n + "log_dt"][:, None],
        *[g[n + m] for m in ("A_re", "A_im", "C_re", "C_im")], g[n + "D_skip"][:, None],
        np.eye(P, dtype=np.float32)[::-1])
    n = "L2_attn_"
    by_part = lambda a: cols32(a[None]).reshape(4, P).T
    at = np.arange(P)[None, :] - np.arange(P)[:, None] + 128
    lay["l2_attn"] = wide(cols32(g[n + "Wq"].T), cols32(g[n + "Wk"].T), cols32(g[n + "Wv"].T),
                          rows(cols32(g[n + "Wo"]).T), by_part(g[n + "bq"]), by_part(g[n + "bk"]),
                          cols32(g[n + "bv"][None]), g[n + "bo"][None], g[n + "rel_v_emb"][at],
                          g[n + "rel_k_emb"][255::-1].T)
    half = lambda a: np.concatenate([a, a], 0)
    swap = [1, 0, 3, 2]
    ups = []
    for n in "qk":
        cc, ee = g[f"L3_attn_W{n}_up_c"], g[f"L3_attn_W{n}_up_e"]
        ups += [half(np.concatenate([cc, ee], 1)), half(np.concatenate([cc, ee[:, swap]], 1))]
    ups.append(half(g["L3_attn_Wv_up"]))
    lay["l3_attn"] = wide(*[rows(g[f"L3_attn_W{n}_down"].T) for n in "qkv"], *ups,
                          rows(cols32(g["L3_attn_Wc"].T).T), *rope_tables(), causal_bias())
    return lay


def cols32(a):
    a = np.asarray(a)
    return np.pad(a.reshape(a.shape[0], 16, 8), ((0, 0), (0, 0), (0, 24))).reshape(a.shape[0], 512)


FLT_MAX = float(np.finfo(np.float32).max)


def causal_bias():
    t = np.arange(P)
    return np.where(t[:, None] >= t[None, :], 0.0, -FLT_MAX).astype(np.float32)


def rope_tables():
    inv = 1.0 / 10000.0 ** (np.arange(0, 4, 2, dtype=np.float32) / 4)
    fr = np.arange(P, dtype=np.float32)[:, None] * inv[None, :]
    emb = np.concatenate((fr, fr), -1)
    cos, sin = np.zeros((4, 32, P), np.float32), np.zeros((4, 32, P), np.float32)
    cos[:, 0:4] = 1.0
    cos[:, 4:8] = np.cos(emb).T
    sin[:, 4:8] = (np.sin(emb) * np.array([-1, 1, -1, 1])).T
    cos, sin = cos.reshape(P, P), sin.reshape(P, P)
    return [(a * s).astype(np.float32) for s in (8 ** -0.5, 1.0) for a in (cos, sin)]


def xpos_tables():
    half = np.arange(0, 64, 2, dtype=np.float32)
    t = np.arange(P, dtype=np.float32)
    fr = t[:, None] * (1.0 / 10000.0 ** (half / 64))[None, :]
    scale = ((half + 0.4 * 64) / (1.4 * 64))[None, :] ** ((t - P // 2) / 32.0)[:, None]
    cos, sin = np.tile(np.cos(fr), 2), np.concatenate([-np.sin(fr), np.sin(fr)], -1)
    scale = np.tile(scale, 2)
    return [a.astype(np.float32) for a in (cos * scale * 8, sin * scale * 8, cos / scale, sin / scale)]


LAYER_NAMES = ["l0_attn", "l0_xattn", "l0_ffn", "l1_attn", "l1_xattn", "l1_ffn",
               "l2_attn", "l2_xattn", "l2_ffn", "l3_attn", "l3_xattn", "l3_ffn"]
WEIGHTS = 7680
SCRATCH = 25088


def build(nc, x_in, ctx_in, ctxk_in, masks_in, text_in, out, weights, experts):
    names = [LAYER_NAMES[n] for n in LAYERS]
    with ExitStack() as ctx:
        core = Core(nc, ctx)
        core.x = core.sbuf("x_res", [P, B, D])
        core.xn = core.sbuf("xn", [P, B, D])
        core.xnT = core.sbuf("xnT", [P, B * P])
        core.ctxT = core.sbuf("ctxT_sb", [P, B * P])
        core.ident = core.sbuf("ident", [P, P])
        core.ones = core.sbuf("ones", [P, P])
        core.ln_st = core.sbuf("ln_st", [P, B, 6])
        core.ln_mv = core.sbuf("ln_mv", [P, B, 2])
        core.ln_rstd = core.sbuf("ln_rstd", [P, B])
        core.ln_ve = core.sbuf("ln_ve", [P, 2 * B])
        core.ctxk = core.sbuf("ctx_tokens", [P, B, CTX])
        core.ctx_bias = core.sbuf("ctx_bias", [P, B * P])
        core.lat_bias = core.sbuf("lat_bias", [P, B * P])
        core.text_on = core.sbuf("text_on", [P, B])
        mask_b = core.sbuf("mask_bytes", [P, 2 * B * P], mybir.dt.uint8)
        text_b = core.sbuf("text_bytes", [P, B], mybir.dt.uint8)
        core.scratch = core.sbuf("scratch", [P, SCRATCH])
        wbuf = [core.sbuf(f"weights{n}", [P, WEIGHTS]) for n in range(2)]
        core.ps = [ctx.enter_context(nc.psum_tensor(f"bank{n}", [P, BANK], F32)) for n in range(8)]
        buffer_loaded = [core.sem(f"weights{n}_loaded") for n in range(2)]
        core.w_loaded = {name: (buffer_loaded[n % 2], 16 * (n // 2 + 1)) for n, name in enumerate(names)}
        core.conv_dram = nc.dram_tensor("conv_kernels", (P, 2 * P), F32, kind="Internal")
        loaded, prepared, stored = core.sem("inputs_loaded"), core.sem("constants_ready"), core.sem("out_stored")

        def load_weights(eng, n):
            name = names[n]
            width = weights[name].shape[1]
            eng.dma_start(wbuf[n % 2][:, 0:width], weights[name]).then_inc(buffer_loaded[n % 2], 16)

        with nc.Block("start", no_gpsimd_drain=True) as block:

            @block.sync
            def _(sp):
                sp.dma_start(core.x[:, :, :], x_in.rearrange("b s d -> s b d")).then_inc(loaded, 16)
                sp.dma_start(core.ctxT[:CTX, :], ctx_in).then_inc(loaded, 16)
                sp.dma_start(mask_b[:, :], masks_in.broadcast_to([P, 2 * B * P])).then_inc(loaded, 16)
                sp.dma_start(text_b[:, :], text_in).then_inc(loaded, 16)
                load_weights(sp, 0)
                sp.dma_start(core.ctxk[:, :, :], ctxk_in.rearrange("b s d -> s b d")).then_inc(loaded, 16)
                sp.wait_ge(loaded, 80)

            @block.vector
            def _(dve):
                dve.wait_ge(loaded, 80)
                nc.vector.tensor_copy(core.text_on[:, :], text_b[:, :])
                for n, bias in enumerate((core.ctx_bias, core.lat_bias)):
                    nc.vector.tensor_scalar(bias[:, :], mask_b[:, n * B * P:(n + 1) * B * P], 1.0, FLT_MAX,
                                            ALU.subtract, ALU.mult)

            @block.gpsimd
            def _(pool):
                nc.gpsimd.memset(core.ident[:, :], 0.0).then_inc(prepared, 1)
                nc.gpsimd.memset(core.ones[:, :], 1.0).then_inc(prepared, 1)
                pool.wait_ge(prepared, 2)
                nc.gpsimd.affine_select(out=core.ident[:, :], in_=core.ident[:, :], compare_op=ALU.not_equal,
                                        fill=1.0, base=0, pattern=[[-1, P]], channel_multiplier=1) \
                    .then_inc(prepared, 1)
                pool.wait_ge(prepared, 3)

        for n, name in enumerate(names):
            if n + 1 < len(names):
                with nc.Block(f"{name}_prefetch", no_gpsimd_drain=True) as block:

                    @block.sync
                    def _(sp):
                        load_weights(sp, n + 1)

            if name.endswith("_ffn") and name != "l1_ffn":
                LAYER_FUNCS[name](core, name, Carve(wbuf[n % 2]), experts[name + "_w1"], experts[name + "_w2"])
            else:
                LAYER_FUNCS[name](core, name, Carve(wbuf[n % 2]))

        with nc.Block("finish", no_gpsimd_drain=True) as block:

            @block.sync
            def _(sp):
                sp.dma_start(out.rearrange("b s d -> s b d"), core.x[:, :, :]).then_inc(stored, 16)
                sp.wait_ge(stored, 16)


LAYER_FUNCS = {
    "l0_attn": layer_l0_attn, "l0_xattn": layer_l0_xattn, "l0_ffn": layer_l0_ffn,
    "l1_attn": layer_l1_attn, "l1_xattn": layer_l1_xattn, "l1_ffn": layer_l1_ffn,
    "l2_attn": layer_l2_attn, "l2_xattn": layer_l2_xattn, "l2_ffn": layer_l2_ffn,
    "l3_attn": layer_l3_attn, "l3_xattn": layer_l3_xattn, "l3_ffn": layer_l3_ffn}


def kernel(**inputs):
    import concourse.bacc as _bacc
    from concourse.bass_utils import run_bass_kernel_spmd as _run

    nc = _bacc.Bacc("TRN2", target_bir_lowering=False, num_devices=1)
    g = {k: np.asarray(v) for k, v in inputs.items()}
    arrays = {"x": np.ascontiguousarray(g["x"]),
              "ctxT": np.ascontiguousarray(g["ctx_768"].transpose(2, 0, 1).reshape(CTX, B * P)),
              "ctxk": np.ascontiguousarray(g["ctx_768"]),
              "masks": np.stack([g["mask_BxS2_bf1"], g["mask_BxS2_bk0"]]).reshape(1, 2 * B * P),
              "text_mask": np.ascontiguousarray(g["mask_BxS_bf1"].T)}
    lay = lay_weights(g)
    for n in LAYERS:
        arrays["w_" + LAYER_NAMES[n]] = lay[LAYER_NAMES[n]]
        key = {2: ("L0_ffn_w1", "L0_ffn_w2"), 8: ("L2_ffn_w1", "L2_ffn_w2"), 11: ("L3_ffn_c_fc", "L3_ffn_c_proj")}.get(n)
        if key:
            arrays["e_" + LAYER_NAMES[n] + "_w1"] = np.ascontiguousarray(g[key[0]])
            arrays["e_" + LAYER_NAMES[n] + "_w2"] = np.stack([rows(a) for a in g[key[1]]])
    aps = {k: nc.dram_tensor(k, a.shape, mybir.dt.from_np(a.dtype), kind="ExternalInput").ap()
           for k, a in arrays.items()}
    out = nc.dram_tensor("out", (B, P, D), F32, kind="ExternalOutput").ap()
    build(nc, aps["x"], aps["ctxT"], aps["ctxk"], aps["masks"], aps["text_mask"], out,
          {k[2:]: a for k, a in aps.items() if k.startswith("w_")},
          {k[2:]: a for k, a in aps.items() if k.startswith("e_")})
    return _run(nc, [arrays], core_ids=[0]).results[0]["out"]
```

```python
from contextlib import ExitStack

import numpy as np

import concourse.bass as bass
from concourse import mybir

LAYERS = (0, 1, 2, 3, 4, 5, 6, 7, 8, 9, 10, 11)

ALU = mybir.AluOpType
ACT = mybir.ActivationFunctionType
F32 = mybir.dt.float32
AX_X = mybir.AxisListType.X
ds = bass.ds

P = 128
B = 8
PAIRS = B // 2
D = 128
CTX = 96
BANK = 512
BIG = 3.0e38


class Marks:

    def __init__(self, sem, names, base=0):
        self.sem, self.names, self.now, self.base = sem, list(names), 0, base
        self.last_turn, self.left_out = None, []
        assert len(set(self.names)) == len(self.names)

    def leave_out(self, turn, names):
        self.last_turn, self.left_out = turn, [n for n in names if n in self.names]

    def turn(self):
        return len(self.names)

    def credit(self, eng, upto=None):
        until = len(self.names) if upto is None else self.names.index(upto)
        if until > self.now:
            if self.now:
                eng.wait_ge(self.sem, self.now)
            eng.sem_inc(self.sem, until - self.now)
        self.now = until

    def mark(self, name):
        while self.now >= 2 * len(self.names) and self.names[self.now % len(self.names)] in self.left_out:
            self.now += 1
        assert self.names[self.now % len(self.names)] == name, (self.names[self.now % len(self.names)], name)
        self.now += 1
        return 1

    def at(self, name, it=0):
        place = self.names.index(name)
        if isinstance(it, int) and it == self.last_turn:
            place -= sum(n in self.left_out for n in self.names[:place])
        return (it + 1) * len(self.names) + (self.base + place + 1)


class Core:

    def __init__(self, nc, ctx):
        self.nc, self.ctx = nc, ctx
        self.ln_sem = {n: self.sem(f"ln_{n}") for n in ("dve", "pool", "pe", "act")}
        self.ln_passed = dict.fromkeys(self.ln_sem, 0)

    def sbuf(self, name, shape, dt=F32):
        return self.ctx.enter_context(self.nc.sbuf_tensor(name, shape, dt))

    def sem(self, name):
        return self.ctx.enter_context(self.nc.semaphore(name))

    def marks(self, name, names):
        return Marks(self.sem(name), names)

    def load_table(self, func):
        self.nc.scalar.activation(self.unused[:, :], self.ones[:, 0:1], func)

    def ln_marks(self, engine, names):
        m = Marks(self.ln_sem[engine], names, self.ln_passed[engine])
        self.ln_passed[engine] += len(m.names)
        return m


class Carve:

    def __init__(self, tensor):
        self.tensor, self.at = tensor, 0

    def take(self, *shape):
        n = int(np.prod(shape))
        ap = self.tensor[:, self.at:self.at + n]
        self.at += n
        assert self.at <= self.tensor.shape[1], self.at
        if len(shape) == 2:
            ap = ap.rearrange("p (a b) -> p a b", a=shape[0])
        if len(shape) == 3:
            ap = ap.rearrange("p (a b c) -> p a b c", a=shape[0], b=shape[1])
        return ap


def layernorm_all(core, tag, src=None, out=None, outT=None, gain=None, bias=None, width=D,
                  turn=True):
    nc = core.nc
    src = core.x if src is None else src
    out = core.xn if out is None else out
    outT = core.xnT if outT is None else outT
    HALVES = [range(0, B // 2), range(B // 2, B)]
    stats = lambda n: [f"stat{b}" for b in HALVES[n]] + [f"aggr{b}" for b in HALVES[n]] + [f"eps{n}"]
    V = core.ln_marks("dve", ["half"] + stats(0) + stats(1) + [f"xn{b}" for b in range(B)]
                      + (["out1"] if turn else []))
    G = core.ln_marks("pool", ["rstd0", "rstd1"])
    T = core.ln_marks("pe", [f"t{b}" for b in range(B)] if turn else [])
    A = core.ln_marks("act", ["out0"] if turn else [])
    st, mv, rstd, ve = core.ln_st, core.ln_mv, core.ln_rstd, core.ln_ve
    with nc.Block(f"{tag}_ln", no_gpsimd_drain=True) as block:

        @block.vector
        def _(dve):
            nc.vector.memset(ve[:, B:], -0.5).then_inc(V.sem, V.mark("half"))
            for n, half in enumerate(HALVES):
                for b in half:
                    nc.vector.bn_stats(st[:, b, :], src[:, b, 0:width]).then_inc(V.sem, V.mark(f"stat{b}"))
                for b in half:
                    dve.wait_ge(V.sem, V.at(f"stat{b}", -1))
                    nc.vector.bn_aggr(mv[:, b, :], st[:, b, :]).then_inc(V.sem, V.mark(f"aggr{b}"))
                dve.wait_ge(V.sem, V.at(f"aggr{half[-1]}", -1))
                nc.vector.tensor_scalar(ve[:, half[0]:half[-1] + 1], mv[:, half[0]:half[-1] + 1, 1], 1e-5, None,
                                        ALU.add).then_inc(V.sem, V.mark(f"eps{n}"))
            for n, half in enumerate(HALVES):
                dve.wait_ge(G.sem, G.at(f"rstd{n}", -1))
                for b in half:
                    nc.vector.tensor_scalar(out[:, b, 0:width], src[:, b, 0:width], mv[:, b, 0:1], rstd[:, b:b + 1],
                                            ALU.subtract, ALU.mult).then_inc(V.sem, V.mark(f"xn{b}"))
            if not turn:
                return
            dve.wait_ge(T.sem, T.at(f"t{B - 1}", -1))
            if gain is None:
                v = nc.vector.tensor_copy(outT[0:width, BANK:], core.ps[1][0:width, :])
            else:
                v = nc.vector.tensor_scalar(outT[0:width, BANK:], core.ps[1][0:width, :], gain, bias,
                                            ALU.mult, ALU.add)
            v.then_inc(V.sem, V.mark("out1"))

        @block.gpsimd
        def _(pool):
            for n, half in enumerate(HALVES):
                pool.wait_ge(V.sem, V.at(f"eps{n}", -1))
                rows = slice(half[0], half[-1] + 1)
                nc.gpsimd.tensor_tensor(rstd[:, rows], ve[:, rows], ve[:, B:B + len(half)], ALU.pow) \
                    .then_inc(G.sem, G.mark(f"rstd{n}"))

        @block.tensor
        def _(pe):
            for b in range(B if turn else 0):
                pe.wait_ge(V.sem, V.at(f"xn{b}", -1))
                nc.tensor.transpose(core.ps[b // 4][0:width, (b % 4) * P:(b % 4 + 1) * P], out[:, b, 0:width],
                                    core.ident[:, :]).then_inc(T.sem, T.mark(f"t{b}"))

        @block.scalar
        def _(act):
            if not turn:
                return
            act.wait_ge(T.sem, T.at("t3", -1))
            if gain is None:
                a = nc.scalar.copy(outT[0:width, 0:BANK], core.ps[0][0:width, :])
            else:
                a = nc.scalar.activation(outT[0:width, 0:BANK], core.ps[0][0:width, :], ACT.Identity,
                                         bias=bias, scale=gain)
            a.then_inc(A.sem, A.mark("out0"))


class Softmax:

    def __init__(self, core, c, groups, keys, V, A, G, T, banks_s, banks_t, mask=None):
        self.core, self.nc, self.groups, self.keys = core, core.nc, groups, keys
        self.V, self.A, self.G, self.T = V, A, G, T
        self.banks_s, self.banks_t, self.mask = banks_s, banks_t, mask
        self.ahead = len(banks_s)
        self.hd = BANK // keys
        self.prob = c.take(self.ahead, BANK)
        self.probT = c.take(2, BANK)
        self.masked = c.take(self.ahead, BANK) if mask is not None else None
        self.top = c.take(self.ahead, self.hd)
        self.total = c.take(self.ahead, self.hd)
        self.inv = c.take(self.ahead, self.hd)

    def marks_dve(self, g):
        return ([f"mask{g}"] if self.mask is not None else []) + [f"max{g}"]

    def before(self, m, name, g, it):
        return m.at(f"{name}{g % len(self.groups)}", it if g >= 0 else it - 1)

    def pe_scores(self, pe, it, g):
        nc, grp, u = self.nc, self.groups[g], g % self.ahead
        if self.mask is not None:
            pe.wait_ge(self.V.sem, self.before(self.V, "mask", g - self.ahead, it))
        else:
            pe.wait_ge(self.A.sem, self.before(self.A, "exp", g - self.ahead, it))
        bank = self.core.ps[self.banks_s[u]]
        for j, (q, k) in enumerate(zip(grp["q"], grp["k"])):
            mm = nc.tensor.matmul(bank[:, j * self.keys:(j + 1) * self.keys], q, k, start=True, stop=True)
        mm.then_inc(self.T.sem, self.T.mark(f"s{g}"))

    def pe_scores_read(self, pe, it):
        m, name = (self.V, "mask") if self.mask is not None else (self.A, "exp")
        pe.wait_ge(m.sem, m.at(f"{name}{len(self.groups) - 1}", it))

    def dve_max(self, dve, it, g):
        nc, u = self.nc, g % self.ahead
        dve.wait_ge(self.T.sem, self.T.at(f"s{g}", it))
        src = self.core.ps[self.banks_s[u]][:, :]
        dve.wait_ge(self.A.sem, self.before(self.A, "exp", g - self.ahead, it))
        if self.mask is not None:
            nc.vector.tensor_tensor(self.masked[:, u, :].rearrange("p (h k) -> p h k", h=self.hd),
                                    src.rearrange("p (h k) -> p h k", h=self.hd),
                                    self.mask(g),
                                    ALU.add).then_inc(self.V.sem, self.V.mark(f"mask{g}"))
            dve.wait_ge(self.V.sem, self.V.at(f"mask{g}", it))
            src = self.masked[:, u, :]
        nc.vector.tensor_reduce(self.top[:, u, :], src.rearrange("p (h k) -> p h k", h=self.hd), AX_X,
                                ALU.max, negate=True).then_inc(self.V.sem, self.V.mark(f"max{g}"))

    def act_exp(self, act, it, g):
        nc, u = self.nc, g % self.ahead
        act.wait_ge(self.V.sem, self.V.at(f"max{g}", it))
        act.wait_ge(self.T.sem, self.before(self.T, "t", g - self.ahead, it))
        src = self.masked[:, u, :] if self.mask is not None else self.core.ps[self.banks_s[u]][:, :]
        for j in range(self.hd):
            sl = slice(j * self.keys, (j + 1) * self.keys)
            e = nc.scalar.activation(self.prob[:, u, sl], src[:, sl], ACT.Exp, bias=self.top[:, u, j:j + 1],
                                     accum_out=self.total[:, u, j:j + 1])
        e.then_inc(self.A.sem, self.A.mark(f"exp{g}"))

    def dve_recip(self, dve, it, g):
        u = g % self.ahead
        dve.wait_ge(self.A.sem, self.A.at(f"exp{g}", it))
        dve.wait_ge(self.G.sem, self.before(self.G, "norm", g - self.ahead, it))
        self.nc.vector.reciprocal(self.inv[:, u, :], self.total[:, u, :]) \
            .then_inc(self.V.sem, self.V.mark(f"inv{g}"))

    def pool_norm(self, pool, it, g):
        u = g % self.ahead
        pool.wait_ge(self.V.sem, self.V.at(f"inv{g}", it))
        v = self.prob[:, u, :].rearrange("p (h k) -> p h k", h=self.hd)
        self.nc.gpsimd.tensor_tensor(v, v, self.inv[:, u, :].unsqueeze(2).broadcast_to([P, self.hd, self.keys]),
                                     ALU.mult).then_inc(self.G.sem, self.G.mark(f"norm{g}"))

    def pe_turn(self, pe, it, g):
        pe.wait_ge(self.G.sem, self.G.at(f"norm{g}", it))
        pe.wait_ge(self.V.sem, self.before(self.V, "pT", g - 2, it))
        bank = self.core.ps[self.banks_t[g % 2]]
        for j in range(BANK // P):
            mm = self.nc.tensor.transpose(bank[:, j * P:(j + 1) * P], self.prob[:, g % self.ahead, j * P:(j + 1) * P],
                                          self.core.ident[:, :])
        mm.then_inc(self.T.sem, self.T.mark(f"t{g}"))

    def dve_copy(self, dve, it, g):
        u = g % 2
        dve.wait_ge(self.T.sem, self.T.at(f"t{g}", it))
        dve.wait_ge(self.T.sem, self.before(self.T, "o", g - 2, it))
        self.nc.vector.tensor_copy(self.probT[:, u, :], self.core.ps[self.banks_t[u]][:, :]) \
            .then_inc(self.V.sem, self.V.mark(f"pT{g}"))

    def pe_values(self, pe, it, g):
        u, grp = g % 2, self.groups[g]
        pe.wait_ge(self.V.sem, self.V.at(f"pT{g}", it))
        blocks = self.keys // P
        for j in range(self.hd):
            for kb in range(blocks):
                i = j * blocks + kb
                mm = self.nc.tensor.matmul(grp["o"][j], grp["v"][i], self.probT[:, u, i * P:(i + 1) * P],
                                           start=(kb == 0), stop=(kb == blocks - 1))
        mm.then_inc(self.T.sem, self.T.mark(f"o{g}"))

    def names(self):
        n, ahead = len(self.groups), self.ahead
        t, v = [f"s{g}" for g in range(ahead)], []
        for g in range(ahead):
            v += self.marks_dve(g)
        for g in range(n):
            t += ([f"s{g + ahead}"] if g + ahead < n else []) + [f"t{g}"] + ([f"o{g - 1}"] if g > 0 else [])
            v += [f"inv{g}"] + (self.marks_dve(g + ahead) if g + ahead < n else []) + ([f"pT{g - 1}"] if g > 0 else [])
        return (v + [f"pT{n - 1}"], [f"exp{g}" for g in range(n)], [f"norm{g}" for g in range(n)],
                t + [f"o{n - 1}"])

    def run_pe(self, pe, it, before_turns=None, before_values=None):
        n = len(self.groups)
        for g in range(self.ahead):
            self.pe_scores(pe, it, g)
        if before_turns is not None:
            before_turns()
        for g in range(n + 1):
            if g + self.ahead < n:
                self.pe_scores(pe, it, g + self.ahead)
            if g < n:
                self.pe_turn(pe, it, g)
            if g > 0:
                if before_values is not None:
                    before_values(g - 1)
                self.pe_values(pe, it, g - 1)

    def run_dve(self, dve, it):
        n = len(self.groups)
        for g in range(self.ahead):
            self.dve_max(dve, it, g)
        for g in range(n + 1):
            if g < n:
                self.dve_recip(dve, it, g)
            if g + self.ahead < n:
                self.dve_max(dve, it, g + self.ahead)
            if g > 0:
                self.dve_copy(dve, it, g - 1)

    def run_act(self, act, it):
        for g in range(len(self.groups)):
            self.act_exp(act, it, g)

    def run_pool(self, pool, it):
        for g in range(len(self.groups)):
            self.pool_norm(pool, it, g)


def for_heads(bias, n=4):
    return bias.unsqueeze(1).broadcast_to([bias.shape[0], n, bias.shape[1]])


def names_of(groups, masked, ahead):
    probe = Softmax.__new__(Softmax)
    probe.groups, probe.mask, probe.ahead = [None] * groups, (True if masked else None), ahead
    return probe.names()


def attention_by_pairs(core, tag, c, names, heads, make, wq, wk, wv, wo, src, rows, scale,
                       bq=None, bk=None, bv=None, bo=None, key_bias=None):
    nc, ps = core.nc, core.ps
    CH = 4
    Q_BANKS, K_BANKS, V_BANKS, Y_BANKS = (4, 5), (6, 7), (0, 1), (2, 3)
    qT, kT, v = c.take(CH, 2 * P), c.take(CH, 2 * P), c.take(2, BANK)
    src2, oT = c.take(2 * P), c.take(2, BANK)
    pair_bias = c.take(2, P) if key_bias is not None else None
    vs, as_, gs, ts = names
    n = len(as_)
    per_row = n // 2
    cut = ts.index(f"o{n - 2}")
    V = core.marks(f"{tag}_dve", vs + ["q0", "q1", "v1", "x0", "x1"])
    A = core.marks(f"{tag}_act", as_ + ["k0", "k1", "oT0", "oT1", "v0"])
    G = core.marks(f"{tag}_pool", gs + ["src"] + (["bias"] if key_bias is not None else []))
    T = core.marks(f"{tag}_pe", ts[:cut] + ["q0", "q1", "k0", "k1"] + ts[cut:] + ["v0", "v1", "y0", "y1"])
    for m in (V, A, G, T):
        m.leave_out(PAIRS - 1, ["q0", "q1", "k0", "k1", "v0", "v1", "src", "bias"])
    sm = make(heads(qT, kT, v), V, A, G, T, pair_bias)

    def pair(a, it):
        return a[:, ds(it * (2 * P) + 2 * P, 2 * P)]

    def turns(eng, turn):
        with eng.Fori(0, PAIRS - 1) as it:
            turn(it, True)
        turn(PAIRS - 1, False)

    with nc.Block(tag, no_gpsimd_drain=True) as block:

        @block.gpsimd
        def _(pool):

            def next_pair(it, first=False):
                if not first:
                    pool.wait_ge(T.sem, T.at("v1", it - 1))
                nc.gpsimd.tensor_copy(src2[:rows, :], pair(src[:rows], it)).then_inc(G.sem, G.mark("src"))
                if key_bias is not None:
                    if not first:
                        pool.wait_ge(V.sem, V.at(f"mask{n - 1}", it))
                    nc.gpsimd.tensor_copy(pair_bias.rearrange("p a b -> p (a b)"), pair(key_bias, it)) \
                        .then_inc(G.sem, G.mark("bias"))

            def turn(it, more):
                sm.run_pool(pool, it)
                if more:
                    next_pair(it)

            G.credit(pool, "src")
            next_pair(-1, True)
            turns(pool, turn)

        @block.tensor
        def _(pe):

            def project_qk(it):
                for name, banks, wt, xT in (("q", Q_BANKS, wq, core.xnT), ("k", K_BANKS, wk[:rows], src[:rows])):
                    for half in range(2):
                        for i in range(2):
                            mm = nc.tensor.matmul(ps[banks[half]][:, i * 2 * P:(i + 1) * 2 * P],
                                                  wt[:, (2 * half + i) * P:(2 * half + i + 1) * P],
                                                  pair(xT, it), start=True, stop=True)
                        mm.then_inc(T.sem, T.mark(f"{name}{half}"))

            def project_v(it):
                pe.wait_ge(G.sem, G.at("src", it))
                for u in range(2):
                    mm = nc.tensor.matmul(ps[V_BANKS[u]][:, :], src2[:rows, u * P:(u + 1) * P], wv[:rows, :],
                                          start=True, stop=bv is None)
                    if bv is not None:
                        mm = nc.tensor.matmul(ps[V_BANKS[u]][:, :], core.ones[0:1, 0:P], bv[0:1, :],
                                              start=False, stop=True)
                    mm.then_inc(T.sem, T.mark(f"v{u}"))

            def turn(it, more):
                def before_turns():
                    pe.wait_ge(A.sem, A.at("v0", it - 1))
                    pe.wait_ge(V.sem, V.at("v1", it - 1))

                def before_values(g):
                    if g == 0:
                        pe.wait_ge(V.sem, V.at("x1", it - 1))
                    if g == n - 2 and more:
                        sm.pe_scores_read(pe, it)
                        project_qk(it)

                pe.wait_ge(V.sem, V.at("q1", it - 1))
                pe.wait_ge(A.sem, A.at("k1", it - 1))
                sm.run_pe(pe, it, before_turns, before_values)
                if more:
                    project_v(it)
                for u in range(2):
                    pe.wait_ge(A.sem, A.at(f"oT{u}", it))
                    for i in range(CH):
                        mm = nc.tensor.matmul(ps[Y_BANKS[u]][:, 0:D], oT[:, u, i * P:(i + 1) * P], wo[:, i, :],
                                              start=(i == 0), stop=(bo is None and i == CH - 1))
                    if bo is not None:
                        mm = nc.tensor.matmul(ps[Y_BANKS[u]][:, 0:D], core.ones[0:1, 0:P], bo[0:1, :],
                                              start=False, stop=True)
                    mm.then_inc(T.sem, T.mark(f"y{u}"))

            T.credit(pe, "q0")
            pe.wait_ge(*core.w_loaded[tag])
            project_qk(-1)
            T.credit(pe, "v0")
            project_v(-1)
            T.credit(pe)
            turns(pe, turn)

        @block.scalar
        def _(act):

            def keys_out(it):
                for half in range(2):
                    act.wait_ge(T.sem, T.at(f"k{half}", it))
                    if bk is None:
                        a = nc.scalar.copy(kT[:, 2 * half:2 * half + 2, :].rearrange("p a b -> p (a b)"),
                                           ps[K_BANKS[half]][:, :])
                    else:
                        for i in range(2):
                            a = nc.scalar.activation(kT[:, 2 * half + i, :],
                                                     ps[K_BANKS[half]][:, i * 2 * P:(i + 1) * 2 * P], ACT.Identity,
                                                     bias=bk[:, 2 * half + i:2 * half + i + 1])
                    a.then_inc(A.sem, A.mark(f"k{half}"))

            def values_out(it):
                act.wait_ge(T.sem, T.at("v0", it))
                nc.scalar.copy(v[:, 0, :], ps[V_BANKS[0]][:, :]).then_inc(A.sem, A.mark("v0"))

            def turn(it, more):
                sm.run_act(act, it)
                if more:
                    keys_out(it)
                for u in range(2):
                    act.wait_ge(T.sem, T.at(f"o{per_row * (u + 1) - 1}", it))
                    nc.scalar.copy(oT[:, u, :], ps[Y_BANKS[u]][:, :]).then_inc(A.sem, A.mark(f"oT{u}"))
                if more:
                    values_out(it)

            A.credit(act, "k0")
            core.load_table(ACT.Exp)
            act.wait_ge(*core.w_loaded[tag])
            keys_out(-1)
            A.credit(act, "v0")
            values_out(-1)
            turns(act, turn)

        @block.vector
        def _(dve):

            def queries_out(it):
                for half in range(2):
                    dve.wait_ge(T.sem, T.at(f"q{half}", it))
                    if bq is None:
                        d = nc.vector.tensor_scalar(qT[:, 2 * half:2 * half + 2, :].rearrange("p a b -> p (a b)"),
                                                    ps[Q_BANKS[half]][:, :], scale, None, ALU.mult)
                    else:
                        for i in range(2):
                            d = nc.vector.tensor_scalar(qT[:, 2 * half + i, :],
                                                        ps[Q_BANKS[half]][:, i * 2 * P:(i + 1) * 2 * P],
                                                        bq[:, 2 * half + i:2 * half + i + 1], scale, ALU.add, ALU.mult)
                    d.then_inc(V.sem, V.mark(f"q{half}"))

            def values_out(it):
                dve.wait_ge(T.sem, T.at("v1", it))
                nc.vector.tensor_copy(v[:, 1, :], ps[V_BANKS[1]][:, :]).then_inc(V.sem, V.mark("v1"))

            def turn(it, more):
                if key_bias is not None:
                    dve.wait_ge(G.sem, G.at("bias", it - 1))
                sm.run_dve(dve, it)
                if more:
                    queries_out(it)
                    values_out(it)
                for u in range(2):
                    dve.wait_ge(T.sem, T.at(f"y{u}", it))
                    xr = core.x[:, ds(it * 2 + u, 1), :].rearrange("p a d -> p (a d)")
                    nc.vector.tensor_tensor(xr, xr, ps[Y_BANKS[u]][:, 0:D], ALU.add).then_inc(V.sem, V.mark(f"x{u}"))

            V.credit(dve, "q0")
            dve.wait_ge(*core.w_loaded[tag])
            queries_out(-1)
            values_out(-1)
            V.credit(dve)
            turns(dve, turn)


def layer_l0_xattn(core, tag, w):
    ps = core.ps
    H, K = 8, 64
    CH = H * K // P
    c = Carve(core.scratch)
    wq, wk, wv = w.take(H * K), w.take(H * K), w.take(H * K)
    wo, bo = w.take(CH, D), w.take(D)

    def heads(qT, kT, v):
        groups = []
        for u in range(2):
            for par in range(2):
                rows, tok = slice(K * par, K * par + K), slice(u * P, u * P + P)
                groups.append(dict(
                    q=[qT[rows, i, tok] for i in range(CH)], k=[kT[rows, i, tok] for i in range(CH)],
                    v=[v[:, u, (2 * i + par) * K:(2 * i + par + 1) * K] for i in range(CH)],
                    o=[ps[2 + u][rows, i * P:(i + 1) * P] for i in range(CH)]))
        return groups

    def make(groups, V, A, G, T, _):
        return Softmax(core, c, groups, P, V, A, G, T, (6, 7, 4, 5), (0, 1))

    layernorm_all(core, tag)
    attention_by_pairs(core, tag, c, names_of(4, False, 4), heads, make, wq, wk, wv, wo, core.ctxT, CTX,
                       K ** -0.5, bo=bo)


def small_groups(qT, kT, v, ps, o_banks):
    groups = []
    for u in range(2):
        for j in range(4):
            part, tok = slice(32 * j, 32 * j + 8), slice(u * P, u * P + P)
            groups.append(dict(
                q=[qT[part, i, tok] for i in range(4)], k=[kT[part, i, tok] for i in range(4)],
                v=[v[:, u, (4 * i + j) * 32:(4 * i + j + 1) * 32] for i in range(4)],
                o=[ps[o_banks[u]][32 * j:32 * j + 32, i * P:(i + 1) * P] for i in range(4)]))
    return groups


def layer_l2_xattn(core, tag, w):
    c = Carve(core.scratch)
    wq, wk, wv, wo = w.take(BANK), w.take(BANK), w.take(BANK), w.take(4, D)

    def make(groups, V, A, G, T, pair_bias):
        return Softmax(core, c, groups, P, V, A, G, T, (6, 7, 4, 5), (0, 1),
                       mask=lambda g: for_heads(pair_bias[:, g // 4, :]))

    layernorm_all(core, tag)
    attention_by_pairs(core, tag, c, names_of(8, True, 4), lambda qT, kT, v: small_groups(qT, kT, v, core.ps, (2, 3)),
                       make, wq, wk, wv, wo, core.ctxT, CTX, 8 ** -0.5, key_bias=core.ctx_bias)


def layer_l3_attn(core, tag, w):
    nc, ps = core.nc, core.ps
    c = Carve(core.scratch)
    down = [w.take(8, P) for _ in range(3)]
    ups = w.take(5, 8)
    wc = w.take(4, D)
    cosq, sinq, cosk, sink, causal = w.take(P), w.take(P), w.take(P), w.take(P), w.take(P)
    eff = [c.take(BANK) for _ in range(5)]
    qT, kT, v = c.take(4, 2 * P), c.take(4, 2 * P), c.take(2, BANK)
    rot = c.take(4, 2 * P)
    xnT2, oT = c.take(2 * P), c.take(2, BANK)
    vs, as_, gs, ts = names_of(8, True, 4)
    PROJ = ["q", "qs", "k", "ks"]
    V = core.marks(f"{tag}_dve", ["qc0", "qc1", "rs0", "rs1", "qsum", "kc0", "kc1", "ks0", "ks1", "ksum"] + vs + ["x0", "x1"])
    A = core.marks(f"{tag}_act", ["v0", "v1"] + as_ + ["oT0", "oT1"])
    G = core.marks(f"{tag}_pool", ["xn"] + gs)
    T = core.marks(f"{tag}_pe", ["q0", "q1", "qs0", "qs1", "k0", "k1", "ks0", "ks1", "v0", "v1"] + ts + ["y0", "y1"])
    W = core.marks(f"{tag}_eff_pe", [f"e{n}" for n in range(5)])
    E = core.marks(f"{tag}_eff_dve", ["zero"] + [f"e{n}" for n in range(5)])
    groups = small_groups(qT, kT, v, ps, (2, 3))
    sm = Softmax(core, c, groups, P, V, A, G, T, (6, 7, 4, 5), (0, 1), mask=lambda g: for_heads(causal))
    layernorm_all(core, tag)
    with nc.Block(f"{tag}_eff", no_gpsimd_drain=True) as block:

        @block.tensor
        def _(pe):
            pe.wait_ge(*core.w_loaded[tag])
            for n in range(5):
                d = down[(0, 0, 1, 1, 2)[n]]
                for h in range(16):
                    part = slice(64 * (h % 2), 64 * (h % 2) + 64)
                    mm = nc.tensor.matmul(ps[h % 2][:, n * 64 + h // 2 * 8:n * 64 + h // 2 * 8 + 8],
                                          d[part, h // 2, :], ups[part, n, :], start=True, stop=True)
                mm.then_inc(W.sem, W.mark(f"e{n}"))

        @block.vector
        def _(dve):
            nc.vector.memset(c.tensor[:, 0:5 * BANK], 0.0).then_inc(E.sem, E.mark("zero"))
            dve.wait_ge(E.sem, E.at("zero", -1))
            for n in range(5):
                dve.wait_ge(W.sem, W.at("e4", -1))
                for par in range(2):
                    e = nc.vector.tensor_copy(
                        eff[n].rearrange("p (h r s) -> p h r s", r=2, s=32)[:, :, par, 0:8],
                        ps[par][:, n * 64:(n + 1) * 64].rearrange("p (h s) -> p h s", s=8))
                e.then_inc(E.sem, E.mark(f"e{n}"))

    with nc.Block(tag, no_gpsimd_drain=True) as block:

        @block.gpsimd
        def _(pool):
            pool.sem_inc(G.sem, G.turn())
            with pool.Fori(0, PAIRS) as it:
                pool.wait_ge(T.sem, T.at("v1", it - 1))
                nc.gpsimd.tensor_copy(xnT2, core.xnT[:, ds(it * 2 * P, 2 * P)]).then_inc(G.sem, G.mark("xn"))
                sm.run_pool(pool, it)

        @block.tensor
        def _(pe):
            pe.sem_inc(T.sem, T.turn())
            with pe.Fori(0, PAIRS) as it:
                for n, name in enumerate(PROJ):
                    for half in range(2):
                        bank = (0, 2, 4, 6)[n] + half
                        if n == 0:
                            pe.wait_ge(V.sem, V.at(f"pT{6 + half}", it - 1))
                        if n == 1:
                            pe.wait_ge(A.sem, A.at(f"oT{half}", it - 1))
                        if n == 2:
                            pe.wait_ge(V.sem, V.at(f"x{half}", it - 1))
                        if n == 3:
                            pe.wait_ge(V.sem, V.at(f"mask{6 + half}", it - 1))
                        for i in range(2):
                            mm = nc.tensor.matmul(ps[bank][:, i * 2 * P:(i + 1) * 2 * P],
                                                  eff[n][:, (2 * half + i) * P:(2 * half + i + 1) * P],
                                                  core.xnT[:, ds(it * 2 * P, 2 * P)], start=True, stop=True)
                        mm.then_inc(T.sem, T.mark(f"{name}{half}"))
                pe.wait_ge(G.sem, G.at("xn", it))
                for u in range(2):
                    pe.wait_ge(V.sem, V.at(f"qc{u}", it))
                    nc.tensor.matmul(ps[u][:, :], xnT2[:, u * P:(u + 1) * P], eff[4],
                                     start=True, stop=True).then_inc(T.sem, T.mark(f"v{u}"))
                pe.wait_ge(V.sem, V.at("ksum", it))
                pe.wait_ge(A.sem, A.at("v1", it))
                sm.run_pe(pe, it)
                for u in range(2):
                    pe.wait_ge(A.sem, A.at(f"oT{u}", it))
                    for i in range(4):
                        mm = nc.tensor.matmul(ps[4 + u][:, 0:D], oT[:, u, i * P:(i + 1) * P], wc[:, i, :],
                                              start=(i == 0), stop=(i == 3))
                    mm.then_inc(T.sem, T.mark(f"y{u}"))

        @block.scalar
        def _(act):
            act.sem_inc(A.sem, A.turn())
            core.load_table(ACT.Exp)
            with act.Fori(0, PAIRS) as it:
                for u in range(2):
                    act.wait_ge(T.sem, T.at(f"v{u}", it))
                    nc.scalar.copy(v[:, u, :], ps[u][:, :]).then_inc(A.sem, A.mark(f"v{u}"))
                sm.run_act(act, it)
                for u in range(2):
                    act.wait_ge(T.sem, T.at(f"o{4 * u + 3}", it))
                    nc.scalar.copy(oT[:, u, :], ps[2 + u][:, :]).then_inc(A.sem, A.mark(f"oT{u}"))

        @block.vector
        def _(dve):
            dve.sem_inc(V.sem, V.turn())

            def rotated(it, dst, base, swapped, banks, names, cos, sin):
                for half in range(2):
                    dve.wait_ge(T.sem, T.at(f"{base}{half}", it))
                    nc.vector.tensor_tensor(dst[:, 2 * half:2 * half + 2, :].rearrange("p a (b t) -> p (a b) t", t=P),
                                            ps[banks[0] + half][:, :].rearrange("p (a t) -> p a t", t=P),
                                            cos.unsqueeze(1).broadcast_to([P, 4, P]),
                                            ALU.mult).then_inc(V.sem, V.mark(f"{names[0]}{half}"))
                for half in range(2):
                    dve.wait_ge(T.sem, T.at(f"{swapped}{half}", it))
                    nc.vector.tensor_tensor(rot[:, 2 * half:2 * half + 2, :].rearrange("p a (b t) -> p (a b) t", t=P),
                                            ps[banks[1] + half][:, :].rearrange("p (a t) -> p a t", t=P),
                                            sin.unsqueeze(1).broadcast_to([P, 4, P]),
                                            ALU.mult).then_inc(V.sem, V.mark(f"{names[1]}{half}"))
                dve.wait_ge(V.sem, V.at(f"{names[1]}1", it))
                nc.vector.tensor_tensor(dst, dst, rot, ALU.add).then_inc(V.sem, V.mark(names[2]))

            with dve.Fori(0, PAIRS) as it:
                rotated(it, qT, "q", "qs", (0, 2), ("qc", "rs", "qsum"), cosq, sinq)
                dve.wait_ge(V.sem, V.at("qsum", it))
                rotated(it, kT, "k", "ks", (4, 6), ("kc", "ks", "ksum"), cosk, sink)
                sm.run_dve(dve, it)
                for u in range(2):
                    dve.wait_ge(T.sem, T.at(f"y{u}", it))
                    xr = core.x[:, ds(it * 2 + u, 1), :].rearrange("p a d -> p (a d)")
                    nc.vector.tensor_tensor(xr, xr, ps[4 + u][:, 0:D], ALU.add).then_inc(V.sem, V.mark(f"x{u}"))


class Link:

    def __init__(self, eng, sem):
        self.eng, self.sem, self.n = eng, sem, 0

    def __call__(self, *instructions):
        for ins in instructions:
            self.n += 1
            ins.then_inc(self.sem, 1)
        self.eng.wait_ge(self.sem, self.n)


def unit(m, name, n, it, units):
    return m.at(f"{name}{n % units}", it if n >= 0 else it - 1)


def mixture(core, tag, c, w1, w2, act_func, gates, b1=None, aside=None):
    nc, ps, x = core.nc, core.ps, core.x
    E, HC = 8, 4
    U = 4
    wa, wb = [c.take(HC * P) for _ in range(2)], [c.take(HC, D) for _ in range(2)]
    hT = [c.take(HC, BANK) for _ in range(2)]
    gate2, bias2 = c.take(2, B), c.take(2, HC)
    V = core.marks(f"{tag}_dve", ["gate"] + [f"acc{n}" for n in range(U)])
    A = core.marks(f"{tag}_act", (["bias"] if b1 is not None else []) + [f"h{n}" for n in range(U * HC)])
    T = core.marks(f"{tag}_pe", [m for n in range(U) for m in [f"u{n * HC + i}" for i in range(HC)]
                                 + ([f"y{n - 1}"] if n else [])] + [f"y{U - 1}"])
    loads = [core.sem(f"{tag}_expert_weights{s}") for s in range(2)]
    with nc.Block(tag, no_gpsimd_drain=True) as block:

        @block.sync
        def _(sp):
            with sp.Fori(0, E // 2) as it:
                for s in range(2):
                    sp.wait_ge(T.sem, T.at(f"y{2 * s + 1}", it - 1))
                    sp.dma_start(wa[s], w1[ds(it * 2 + s, 1)].rearrange("e p f -> p (e f)")).then_inc(loads[s], 16)
                    sp.dma_start(wb[s].rearrange("p c d -> p (c d)"),
                                 w2[ds(it * 2 + s, 1)].rearrange("e p f -> p (e f)")).then_inc(loads[s], 16)

        @block.gpsimd
        def _(pool):
            if aside is not None:
                aside(pool)

        @block.tensor
        def _(pe):
            pe.sem_inc(T.sem, T.turn())

            def up(it, n):
                s, half = n // 2, n % 2
                if half == 0:
                    pe.wait_ge(loads[s], it * 32 + 32)
                for i in range(HC):
                    m = n * HC + i
                    pe.wait_ge(A.sem, unit(A, "h", m - 4, it, U * HC))
                    nc.tensor.matmul(ps[m % 4][:, :], wa[s][:, i * P:(i + 1) * P],
                                     core.xnT[:, half * BANK:(half + 1) * BANK], start=True, stop=True) \
                        .then_inc(T.sem, T.mark(f"u{m}"))

            def down(it, n):
                s, half = n // 2, n % 2
                pe.wait_ge(A.sem, A.at(f"h{n * HC + HC - 1}", it))
                pe.wait_ge(V.sem, unit(V, "acc", n - 2, it, U))
                for t in range(4):
                    for i in range(HC):
                        mm = nc.tensor.matmul(ps[4 + half][:, t * P:(t + 1) * P], hT[half][:, i, t * P:(t + 1) * P],
                                              wb[s][:, i, :], start=(i == 0), stop=(i == HC - 1))
                mm.then_inc(T.sem, T.mark(f"y{n}"))

            with pe.Fori(0, E // 2) as it:
                for n in range(U + 1):
                    if n < U:
                        up(it, n)
                    if n > 0:
                        down(it, n - 1)

        @block.scalar
        def _(act):
            act.sem_inc(A.sem, A.turn())
            core.load_table(act_func)
            with act.Fori(0, E // 2) as it:
                if b1 is not None:
                    act.wait_ge(A.sem, A.at(f"h{U * HC - 1}", it - 1))
                    nc.scalar.copy(bias2, b1[:, ds(it * 2, 2), :]).then_inc(A.sem, A.mark("bias"))
                    act.wait_ge(A.sem, A.at("bias", it))
                for n in range(U):
                    s, half = n // 2, n % 2
                    act.wait_ge(T.sem, unit(T, "y", n - 2, it, U))
                    for i in range(HC):
                        m = n * HC + i
                        act.wait_ge(T.sem, T.at(f"u{m}", it))
                        nc.scalar.activation(hT[half][:, i, :], ps[m % 4][:, :], act_func,
                                             bias=bias2[:, s, i:i + 1] if b1 is not None else 0.0) \
                            .then_inc(A.sem, A.mark(f"h{m}"))

        @block.vector
        def _(dve):
            dve.sem_inc(V.sem, V.turn())
            with dve.Fori(0, E // 2) as it:
                dve.wait_ge(V.sem, V.at(f"acc{U - 1}", it - 1))
                nc.vector.tensor_copy(gate2, gates[:, ds(it * 2, 2), :]).then_inc(V.sem, V.mark("gate"))
                dve.wait_ge(V.sem, V.at("gate", it))
                for n in range(U):
                    s, half = n // 2, n % 2
                    dve.wait_ge(T.sem, T.at(f"y{n}", it))
                    dve.wait_ge(V.sem, unit(V, "acc", n - 2, it, U))
                    for t in range(4):
                        b = half * 4 + t
                        v = nc.vector.scalar_tensor_tensor(
                            out=x[:, b, :], in0=ps[4 + half][:, t * P:(t + 1) * P], scalar=gate2[:, s, b:b + 1],
                            in1=x[:, b, :], op0=ALU.mult, op1=ALU.add)
                    v.then_inc(V.sem, V.mark(f"acc{n}"))


def pe_logits(core, pe, tag, wr, done):
    pe.wait_ge(*core.w_loaded[tag])
    for b in range(B):
        mm = core.nc.tensor.matmul(core.ps[0][:, b * 8:(b + 1) * 8], core.xnT[:, b * P:(b + 1) * P], wr,
                                   start=True, stop=True)
    mm.then_inc(done, 1)


def over_experts(col):
    return col.unsqueeze(2).broadcast_to([P, B, 8])


def dve_softmax(core, dve, link, prob, col, logits_done, shifted, exp_done):
    nc = core.nc
    logits = core.ps[0][:, 0:64].rearrange("p (b e) -> p b e", e=8)
    dve.wait_ge(logits_done, 1)
    link(nc.vector.tensor_reduce(col, logits, AX_X, ALU.max))
    nc.vector.tensor_tensor(prob, logits, over_experts(col), ALU.subtract).then_inc(shifted, 1)
    dve.wait_ge(exp_done, 1)
    link(nc.vector.tensor_reduce(col, prob, AX_X, ALU.add))
    link(nc.vector.reciprocal(col, col))
    link(nc.vector.tensor_tensor(prob, prob, over_experts(col), ALU.mult))


def pick_top(nc, link, values, spare, top, out, k, low):
    link(nc.vector.memset(spare, low))
    link(nc.vector.tensor_copy(spare[:, :, 0:8], values))
    for b in range(B):
        m = nc.vector.max(top[:, b, :], spare[:, b, 0:8])
    link(m)
    link(nc.vector.memset(top[:, :, k:8], low))
    for b in range(B):
        m = nc.vector.match_replace(spare[:, b, :], top[:, b, :], spare[:, b, :], low)
    link(m)
    link(nc.vector.tensor_tensor(out, values, spare[:, :, 0:8], ALU.not_equal))


def layer_l2_ffn(core, tag, w, w1, w2):
    nc = core.nc
    c = Carve(core.scratch)
    wr = w.take(8)
    gates, prob = c.take(8, B), c.take(B, 8)
    spare, top, pick, total, col = c.take(B, 16), c.take(B, 8), c.take(B, 8), c.take(B), c.take(B)
    layernorm_all(core, tag)
    chain, logits_done, shifted, exp_done = (core.sem(f"{tag}_route_{n}")
                                             for n in ("chain", "logits", "shifted", "exp"))
    with nc.Block(f"{tag}_route", no_gpsimd_drain=True) as block:

        @block.tensor
        def _(pe):
            pe_logits(core, pe, tag, wr, logits_done)

        @block.scalar
        def _(act):
            act.wait_ge(shifted, 1)
            nc.scalar.activation(prob, prob, ACT.Exp).then_inc(exp_done, 1)

        @block.vector
        def _(dve):
            link = Link(dve, chain)
            dve_softmax(core, dve, link, prob, col, logits_done, shifted, exp_done)
            pick_top(nc, link, prob, spare, top, pick, 2, -1.0)
            link(nc.vector.tensor_tensor(pick, pick, prob, ALU.mult))
            link(nc.vector.tensor_tensor(total, top[:, :, 0], top[:, :, 1], ALU.add))
            link(nc.vector.reciprocal(total, total))
            link(nc.vector.tensor_tensor(gates.rearrange("p e b -> p b e"), pick, over_experts(total), ALU.mult))

    mixture(core, tag, c, w1, w2, ACT.Gelu_apprx_tanh, gates)


def layer_l3_ffn(core, tag, w, w1, w2):
    nc, ps = core.nc, core.ps
    CAP = int(2 * 1.25 * B * P // 8)
    CAP += CAP % 2
    c = Carve(core.scratch)
    wr, tri = w.take(8), w.take(P)
    gates, val, prob = c.take(8, B), c.take(B, 8), c.take(B, 8)
    spare, top, total = c.take(B, 16), c.take(B, 8), c.take(B)
    picks = [c.take(B, 8), c.take(B, 8)]
    before = [c.take(B, 8), c.take(B, 8)]
    layernorm_all(core, tag)
    chain, logits_done, shifted, exp_done, picked, counted = (
        core.sem(f"{tag}_route_{n}") for n in ("chain", "logits", "shifted", "exp", "picks", "counts"))
    with nc.Block(f"{tag}_route", no_gpsimd_drain=True) as block:

        @block.tensor
        def _(pe):
            pe_logits(core, pe, tag, wr, logits_done)
            pe.wait_ge(picked, 1)
            for k in range(2):
                nc.tensor.matmul(ps[1 + k][:, 0:64], tri, picks[k].rearrange("p b e -> p (b e)"),
                                 start=True, stop=False)
                mm = nc.tensor.matmul(ps[1 + k][:, 0:64], core.ones[:, :], before[k].rearrange("p b e -> p (b e)"),
                                      start=False, stop=True)
            mm.then_inc(counted, 1)

        @block.scalar
        def _(act):
            act.wait_ge(shifted, 1)
            nc.scalar.activation(prob, prob, ACT.Exp).then_inc(exp_done, 1)

        @block.vector
        def _(dve):
            link = Link(dve, chain)
            first, second = picks
            dve.wait_ge(logits_done, 1)
            link(nc.vector.tensor_copy(val, ps[0][:, 0:64].rearrange("p (b e) -> p b e", e=8)))
            pick_top(nc, link, val, spare, top, second, 2, -3.0e38)
            pick_top(nc, link, val, spare, top, first, 1, -3.0e38)
            nc.vector.tensor_tensor(prob, val, top[:, :, 0:1].broadcast_to([P, B, 8]), ALU.subtract) \
                .then_inc(shifted, 1)
            dve.wait_ge(exp_done, 1)
            link(nc.vector.tensor_tensor(prob, prob, second, ALU.mult))
            link(nc.vector.tensor_reduce(total, prob, AX_X, ALU.add))
            link(nc.vector.reciprocal(total, total))
            link(nc.vector.tensor_tensor(prob, prob, over_experts(total), ALU.mult))
            link(nc.vector.tensor_tensor(second, second, first, ALU.subtract))
            link(nc.vector.memset(before[0][:, 0, :], 0.0))
            for b in range(1, B):
                link(nc.vector.tensor_tensor(before[0][:, b, :], before[0][:, b - 1, :], first[:, b - 1, :], ALU.add))
            link(nc.vector.tensor_tensor(before[1][:, 0, :], before[0][:, B - 1, :], first[:, B - 1, :], ALU.add))
            for b in range(1, B):
                v = nc.vector.tensor_tensor(before[1][:, b, :], before[1][:, b - 1, :], second[:, b - 1, :], ALU.add)
                if b < B - 1:
                    link(v)
            v.then_inc(picked, 1)
            dve.wait_ge(counted, 1)
            for k in range(2):
                link(nc.vector.scalar_tensor_tensor(
                    out=picks[k], in0=ps[1 + k][:, 0:64].rearrange("p (b e) -> p b e", e=8), scalar=CAP + 0.5,
                    in1=picks[k], op0=ALU.is_lt, op1=ALU.mult))
            link(nc.vector.tensor_tensor(first, first, second, ALU.add))
            link(nc.vector.tensor_tensor(gates.rearrange("p e b -> p b e"), first, prob, ALU.mult))

    mixture(core, tag, c, w1, w2, ACT.Gelu, gates)


def layer_l0_ffn(core, tag, w, w1, w2):
    nc, ps = core.nc, core.ps
    CAP = int(P * 2.0 / 8) + 1
    c = Carve(core.scratch)
    wr, b1, b2 = w.take(8), w.take(8, 4), w.take(D)
    gates, prob, col = c.take(8, B), c.take(B, 8), c.take(B)
    own, left, top = c.take(P)[0:64, :], c.take(P)[0:64, :], c.take(8)[0:64, :]
    gT = c.take(B * P)[0:8, :]
    layernorm_all(core, tag)
    chain, logits_done, shifted, exp_done, ready, turned, gated, back, given, spread, copied, biased = (
        core.sem(f"{tag}_route_{n}") for n in ("chain", "logits", "shifted", "exp", "by_token", "by_expert",
                                               "chosen", "gates", "gates_out", "gates_T", "gates_T_out", "bias"))
    with nc.Block(f"{tag}_route", no_gpsimd_drain=True) as block:

        @block.tensor
        def _(pe):
            pe_logits(core, pe, tag, wr, logits_done)
            pe.wait_ge(ready, 1)
            nc.tensor.transpose(ps[1][0:64, 0:P], gates.rearrange("p e b -> p (e b)"), core.ident[:, :]) \
                .then_inc(turned, 1)
            pe.wait_ge(gated, 1)
            nc.tensor.transpose(ps[2][:, 0:64], own, core.ident[0:64, 0:64]).then_inc(back, 1)
            pe.wait_ge(given, 1)
            for b in range(B):
                mm = nc.tensor.transpose(ps[3 + b // 4][0:8, b % 4 * P:(b % 4 + 1) * P], gates[:, :, b],
                                         core.ident[:, :])
            mm.then_inc(spread, 1)
            pe.wait_ge(copied, 1)
            for b in range(B):
                mm = nc.tensor.matmul(ps[5 + b // 4][:, b % 4 * P:(b % 4 + 1) * P], gT[:, b * P:(b + 1) * P],
                                      b2[0:8, :], start=True, stop=True)
            mm.then_inc(biased, 1)

        @block.scalar
        def _(act):
            act.wait_ge(shifted, 1)
            nc.scalar.activation(prob, prob, ACT.Exp).then_inc(exp_done, 1)

        @block.vector
        def _(dve):
            link = Link(dve, chain)
            dve_softmax(core, dve, link, prob, col, logits_done, shifted, exp_done)
            nc.vector.tensor_copy(gates.rearrange("p e b -> p b e"), prob).then_inc(ready, 1)
            dve.wait_ge(turned, 1)
            link(nc.vector.tensor_copy(own, ps[1][0:64, 0:P]))
            link(nc.vector.tensor_copy(left, own))
            for r in range(CAP // 8 + 1):
                link(nc.vector.max(top, left))
                if CAP - 8 * r < 8:
                    link(nc.vector.memset(top[:, CAP - 8 * r:8], -1.0))
                link(nc.vector.match_replace(left, top, left, -1.0))
            link(nc.vector.tensor_tensor(left, own, left, ALU.not_equal))
            nc.vector.tensor_tensor(own, own, left, ALU.mult).then_inc(gated, 1)
            dve.wait_ge(back, 1)
            nc.vector.tensor_copy(gates.rearrange("p e b -> p (e b)"), ps[2][:, 0:64]).then_inc(given, 1)
            dve.wait_ge(spread, 1)
            link(nc.vector.tensor_copy(gT[:, 0:BANK], ps[3][0:8, :]))
            nc.vector.tensor_copy(gT[:, BANK:], ps[4][0:8, :]).then_inc(copied, 1)
            dve.wait_ge(biased, 1)
            for half in range(2):
                xs = core.x[:, half * 4:half * 4 + 4, :].rearrange("p b d -> p (b d)")
                link(nc.vector.tensor_tensor(xs, xs, ps[5 + half][:, :], ALU.add))

    mixture(core, tag, c, w1, w2, ACT.Gelu, gates, b1=b1, aside=lambda pool: conv_kernels(core, pool))


def layer_l0_attn(core, tag, w):
    nc, ps = core.nc, core.ps
    CH = 8
    c = Carve(core.scratch)
    wq, wk, wvT, wo = w.take(CH * P), w.take(CH * P), w.take(CH, P), w.take(CH, D)
    xn2, xnT2 = c.take(2, P), c.take(2, P)
    ek = [c.take(CH, P) for _ in range(2)]
    ekT = [c.take(CH * P) for _ in range(2)]
    us = [c.take(CH, P) for _ in range(2)]
    qk = [c.take(CH, P) for _ in range(2)]
    gg = [c.take(CH, P) for _ in range(2)]
    mm_ = [c.take(P) for _ in range(2)]
    top, tot, inv = c.take(2, CH), c.take(2, CH), c.take(2, CH)
    names2 = lambda *n: [f"{a}{u}" for a in n for u in range(2)]
    V = core.marks(f"{tag}_dve", ["maxA0", "maxB0", "maxA1", "maxB1", "inv0", "tA0", "inv1", "tA1", "uA0", "uA1",
                                  "qa0", "qa1", "gA0", "gA1", "gB0", "gB1", "m0", "m1", "x0", "x1"])
    A = core.marks(f"{tag}_act", ["exp0", "exp1", "tB0", "tB1", "uB0", "uB1", "qb0", "qb1"])
    G = core.marks(f"{tag}_pool", ["xn"])
    T = core.marks(f"{tag}_pe", ["k0", "k1", "t0", "t1", "u0", "u1", "q0", "q1", "g0", "g1", "m0", "m1", "y0", "y1"])
    zeroed = core.sem(f"{tag}_zeroed")
    layernorm_all(core, tag)

    def bank(u, n):
        return ps[4 * u + n]

    with nc.Block(tag, no_gpsimd_drain=True) as block:

        @block.gpsimd
        def _(pool):
            pool.sem_inc(G.sem, G.turn())
            for u in range(2):
                z = nc.gpsimd.memset(qk[u], 0.0)
            z.then_inc(zeroed, 1)
            with pool.Fori(0, PAIRS) as it:
                pool.wait_ge(T.sem, T.at("y1", it - 1))
                nc.gpsimd.tensor_copy(xnT2.rearrange("p a b -> p (a b)"), core.xnT[:, ds(it * 2 * P, 2 * P)])
                nc.gpsimd.tensor_copy(xn2, core.xn[:, ds(it * 2, 2), :]).then_inc(G.sem, G.mark("xn"))

        @block.tensor
        def _(pe):
            pe.sem_inc(T.sem, T.turn())
            pe.wait_ge(*core.w_loaded[tag])
            with pe.Fori(0, PAIRS) as it:
                pe.wait_ge(G.sem, G.at("xn", it))
                for u in range(2):
                    pe.wait_ge(V.sem, V.at(f"x{u}", it - 1))
                    for i in range(CH):
                        mm = nc.tensor.matmul(bank(u, i // 4)[:, i % 4 * P:(i % 4 + 1) * P], wk[:, i * P:(i + 1) * P],
                                              xnT2[:, u, :], start=True, stop=True)
                    mm.then_inc(T.sem, T.mark(f"k{u}"))
                for u in range(2):
                    pe.wait_ge(A.sem, A.at(f"exp{u}", it))
                    for i in range(CH):
                        mm = nc.tensor.transpose(bank(u, 2 + i // 4)[:, i % 4 * P:(i % 4 + 1) * P], ek[u][:, i, :],
                                                 core.ident[:, :])
                    mm.then_inc(T.sem, T.mark(f"t{u}"))
                for u in range(2):
                    pe.wait_ge(V.sem, V.at(f"tA{u}", it))
                    pe.wait_ge(A.sem, A.at(f"tB{u}", it))
                    for i in range(2):
                        mm = nc.tensor.matmul(bank(u, i)[:, :], xn2[:, u, :], ekT[u][:, i * BANK:(i + 1) * BANK],
                                              start=True, stop=True)
                    mm.then_inc(T.sem, T.mark(f"u{u}"))
                for u in range(2):
                    pe.wait_ge(V.sem, V.at(f"uA{u}", it))
                    pe.wait_ge(A.sem, A.at(f"uB{u}", it))
                    for i in range(CH):
                        mm = nc.tensor.matmul(bank(u, 2 + i // 4)[:, i % 4 * P:(i % 4 + 1) * P],
                                              wq[:, i * P:(i + 1) * P], us[u][:, i, :], start=True, stop=True)
                    mm.then_inc(T.sem, T.mark(f"q{u}"))
                for u in range(2):
                    pe.wait_ge(V.sem, V.at(f"qa{u}", it))
                    pe.wait_ge(A.sem, A.at(f"qb{u}", it))
                    for i in range(CH):
                        mm = nc.tensor.matmul(bank(u, i // 4)[:, i % 4 * P:(i % 4 + 1) * P], qk[u][:, i, :],
                                              wo[:, i, :], start=True, stop=True)
                    mm.then_inc(T.sem, T.mark(f"g{u}"))
                for u in range(2):
                    pe.wait_ge(V.sem, V.at(f"gB{u}", it))
                    for i in range(CH):
                        mm = nc.tensor.matmul(bank(u, 2)[:, 0:P], wvT[:, i, :], gg[u][:, i, :],
                                              start=(i == 0), stop=(i == CH - 1))
                    mm.then_inc(T.sem, T.mark(f"m{u}"))
                for u in range(2):
                    pe.wait_ge(V.sem, V.at(f"m{u}", it))
                    nc.tensor.matmul(bank(u, 3)[:, 0:P], xnT2[:, u, :], mm_[u], start=True, stop=True) \
                        .then_inc(T.sem, T.mark(f"y{u}"))

        @block.scalar
        def _(act):
            act.sem_inc(A.sem, A.turn())
            core.load_table(ACT.Exp)
            act.wait_ge(zeroed, 1)
            with act.Fori(0, PAIRS) as it:
                for u in range(2):
                    act.wait_ge(V.sem, V.at(f"maxB{u}", it))
                    for i in range(CH):
                        e = nc.scalar.activation(ek[u][:, i, :], bank(u, i // 4)[:, i % 4 * P:(i % 4 + 1) * P],
                                                 ACT.Exp, bias=top[:, u, i:i + 1], accum_out=tot[:, u, i:i + 1])
                    e.then_inc(A.sem, A.mark(f"exp{u}"))
                for u in range(2):
                    act.wait_ge(T.sem, T.at(f"t{u}", it))
                    nc.scalar.copy(ekT[u][:, BANK:], bank(u, 3)[:, :]).then_inc(A.sem, A.mark(f"tB{u}"))
                for u in range(2):
                    act.wait_ge(T.sem, T.at(f"u{u}", it))
                    nc.scalar.copy(us[u][:, 4:, :].rearrange("p a b -> p (a b)"), bank(u, 1)[:, :]) \
                        .then_inc(A.sem, A.mark(f"uB{u}"))
                for u in range(2):
                    act.wait_ge(T.sem, T.at(f"q{u}", it))
                    for half in range(2):
                        e = nc.scalar.copy(qk[u][64:, 4 * half:4 * half + 4, 64:],
                                           bank(u, 2 + half)[64:, :].rearrange("p (a b) -> p a b", a=4)[:, :, 64:])
                    e.then_inc(A.sem, A.mark(f"qb{u}"))

        @block.vector
        def _(dve):
            dve.sem_inc(V.sem, V.turn())
            dve.wait_ge(zeroed, 1)
            with dve.Fori(0, PAIRS) as it:
                for u in range(2):
                    dve.wait_ge(T.sem, T.at(f"k{u}", it))
                    for half, m in enumerate(("maxA", "maxB")):
                        nc.vector.tensor_reduce(top[:, u, 4 * half:4 * half + 4],
                                                bank(u, half)[:, :].rearrange("p (a b) -> p a b", a=4), AX_X,
                                                ALU.max, negate=True).then_inc(V.sem, V.mark(f"{m}{u}"))
                for u in range(2):
                    dve.wait_ge(A.sem, A.at(f"exp{u}", it))
                    nc.vector.reciprocal(inv[:, u, :], tot[:, u, :]).then_inc(V.sem, V.mark(f"inv{u}"))
                    dve.wait_ge(T.sem, T.at(f"t{u}", it))
                    nc.vector.tensor_copy(ekT[u][:, 0:BANK], bank(u, 2)[:, :]).then_inc(V.sem, V.mark(f"tA{u}"))
                for u in range(2):
                    dve.wait_ge(T.sem, T.at(f"u{u}", it))
                    nc.vector.tensor_copy(us[u][:, 0:4, :].rearrange("p a b -> p (a b)"), bank(u, 0)[:, :]) \
                        .then_inc(V.sem, V.mark(f"uA{u}"))
                for u in range(2):
                    dve.wait_ge(T.sem, T.at(f"q{u}", it))
                    for half in range(2):
                        v = nc.vector.tensor_copy(qk[u][0:64, 4 * half:4 * half + 4, 0:64],
                                                  bank(u, 2 + half)[0:64, :].rearrange("p (a b) -> p a b", a=4)[:, :, 0:64])
                    v.then_inc(V.sem, V.mark(f"qa{u}"))
                for u in range(2):
                    dve.wait_ge(T.sem, T.at(f"g{u}", it))
                    nc.vector.tensor_tensor(gg[u][:, 0:4, :], bank(u, 0)[:, :].rearrange("p (a b) -> p a b", a=4),
                                            inv[:, u, 0:4].unsqueeze(2).broadcast_to([P, 4, P]),
                                            ALU.mult).then_inc(V.sem, V.mark(f"gA{u}"))
                for u in range(2):
                    nc.vector.tensor_tensor(gg[u][:, 4:8, :], bank(u, 1)[:, :].rearrange("p (a b) -> p a b", a=4),
                                            inv[:, u, 4:8].unsqueeze(2).broadcast_to([P, 4, P]),
                                            ALU.mult).then_inc(V.sem, V.mark(f"gB{u}"))
                for u in range(2):
                    dve.wait_ge(T.sem, T.at(f"m{u}", it))
                    nc.vector.tensor_copy(mm_[u], bank(u, 2)[:, 0:P]).then_inc(V.sem, V.mark(f"m{u}"))
                for u in range(2):
                    dve.wait_ge(T.sem, T.at(f"y{u}", it))
                    xr = core.x[:, ds(it * 2 + u, 1), :].rearrange("p a d -> p (a d)")
                    nc.vector.tensor_tensor(xr, xr, bank(u, 3)[:, 0:D], ALU.add).then_inc(V.sem, V.mark(f"x{u}"))


def layer_l1_attn(core, tag, w):
    nc, ps = core.nc, core.ps
    H, K, TG = 16, 64, 8
    SEQ = P // TG
    c = Carve(core.scratch)
    wq, wk, wv = w.take(H * K), w.take(H * K), w.take(H * K)
    wp, bp, bias = w.take(H, D), w.take(D), w.take(P)
    q, k, vT = (c.take(SEQ, H, TG)[0:K] for _ in range(3))
    v = c.take(SEQ, K)
    oT = c.take(H, P)[0:K]
    groups = [dict(q=[q[:, 4 * g + i].rearrange("p a b -> p (a b)") for i in range(4)],
                   k=[k[:, 4 * g + i].rearrange("p a b -> p (a b)") for i in range(4)],
                   v=[v[:, 4 * g + i, :] for i in range(4)],
                   o=[ps[2 + g % 2][0:K, i * P:(i + 1) * P] for i in range(4)]) for g in range(4)]
    CHUNKS = [(n, half) for half in range(2) for n in "qkv"]
    dsts, wts = dict(q=q, k=k, v=vT), dict(q=wq, k=wk, v=wv)
    S_BANKS, T_BANKS, O_BANKS, Y_BANK = (6, 7, 4, 5), (0, 1), (2, 3), 2
    V = core.marks(f"{tag}_dve", [f"{n}{g}" for g in range(4) for n in ("mask", "max")]
                   + ["inv0", "inv1", "pT0", "inv2", "pT1", "odd_q0", "inv3", "pT2", "odd_k0", "pT3",
                      "odd_v0", "odd_q1", "odd_k1", "odd_v1", "x"])
    A = core.marks(f"{tag}_act", ["exp0", "v0", "exp1", "v1", "exp2", "exp3", "even_q0", "even_k0", "oT0", "even_v0",
                                  "oT1", "even_q1", "even_k1", "even_v1", "oT2", "oT3"])
    G = core.marks(f"{tag}_pool", [f"norm{g}" for g in range(4)])
    T = core.marks(f"{tag}_pe", ["s0", "s1", "s2", "s3", "vt0", "vt1", "q0", "k0", "v0", "q1", "t0", "t1", "o0", "t2",
                                 "o1", "k1", "t3", "o2", "v1", "o3", "y"])
    T.leave_out(B - 1, [f"{n}{half}" for n, half in CHUNKS])
    for m, part in ((V, "odd"), (A, "even")):
        m.leave_out(B - 1, [f"{part}_{n}{half}" for n, half in CHUNKS])
    sm = Softmax(core, c, groups, P, V, A, G, T, S_BANKS, T_BANKS, mask=lambda g: for_heads(bias))
    layernorm_all(core, tag)

    def halves(dst, half, par):
        return dst[:, :, 8 * half + par:8 * half + 8:2, :].rearrange("p s c t -> p c s t")

    def source(m, par):
        return ps[S_BANKS[m % 4]][64 * par:64 * par + 64, :].rearrange("p (c s t) -> p c s t", c=4, t=TG)

    def turns(eng, turn):
        with eng.Fori(0, B - 1) as it:
            turn(it, True)
        turn(B - 1, False)

    with nc.Block(tag, no_gpsimd_drain=True) as block:

        @block.gpsimd
        def _(pool):
            G.credit(pool)
            turns(pool, lambda it, more: sm.run_pool(pool, it))

        @block.tensor
        def _(pe):

            def project(it, m):
                n, half = CHUNKS[m]
                if m >= 4:
                    pe.wait_ge(V.sem, V.at("odd_{}{}".format(*CHUNKS[m - 4]), it))
                for i in range(4):
                    ch = 4 * half + i
                    mm = nc.tensor.matmul(ps[S_BANKS[m % 4]][:, i * P:(i + 1) * P], wts[n][:, ch * P:(ch + 1) * P],
                                          core.xnT[:, ds(it * P + P, P)], start=True, stop=True)
                mm.then_inc(T.sem, T.mark(f"{n}{half}"))

            def turn(it, more):
                pe.wait_ge(V.sem, V.at("odd_v1", it - 1))
                pe.wait_ge(A.sem, A.at("even_v1", it - 1))
                for g in range(4):
                    sm.pe_scores(pe, it, g)
                for half in range(2):
                    for s in range(8):
                        mm = nc.tensor.transpose(ps[T_BANKS[half]][:, s * K:(s + 1) * K],
                                                 vT[:, 8 * half + s].rearrange("p a b -> p (a b)"),
                                                 core.ident[0:K, 0:K])
                    mm.then_inc(T.sem, T.mark(f"vt{half}"))
                if more:
                    sm.pe_scores_read(pe, it)
                    for m in range(4):
                        project(it, m)
                pe.wait_ge(A.sem, A.at("v1", it))
                sm.pe_turn(pe, it, 0)
                sm.pe_turn(pe, it, 1)
                pe.wait_ge(V.sem, V.at("x", it - 1))
                sm.pe_values(pe, it, 0)
                sm.pe_turn(pe, it, 2)
                sm.pe_values(pe, it, 1)
                if more:
                    project(it, 4)
                sm.pe_turn(pe, it, 3)
                pe.wait_ge(A.sem, A.at("oT0", it))
                sm.pe_values(pe, it, 2)
                if more:
                    project(it, 5)
                pe.wait_ge(A.sem, A.at("oT1", it))
                sm.pe_values(pe, it, 3)
                pe.wait_ge(A.sem, A.at("oT3", it))
                for h in range(H):
                    nc.tensor.matmul(ps[Y_BANK][:, 0:D], oT[:, h, :], wp[0:K, h, :], start=(h == 0), stop=False)
                nc.tensor.matmul(ps[Y_BANK][:, 0:D], core.ones[0:1, 0:P], bp[0:1, :], start=False, stop=True) \
                    .then_inc(T.sem, T.mark("y"))

            pe.wait_ge(*core.w_loaded[tag])
            for m, (n, half) in enumerate(CHUNKS):
                T.credit(pe, f"{n}{half}")
                project(-1, m)
            T.credit(pe)
            turns(pe, turn)

        @block.scalar
        def _(act):

            def even(it, m):
                n, half = CHUNKS[m]
                act.wait_ge(T.sem, T.at(f"{n}{half}", it))
                nc.scalar.mul(halves(dsts[n], half, 0), source(m, 0), K ** -0.5 if n == "q" else 1.0) \
                    .then_inc(A.sem, A.mark(f"even_{n}{half}"))

            def out(it, g):
                act.wait_ge(T.sem, T.at(f"o{g}", it))
                nc.scalar.copy(oT.rearrange("p h (s t) -> p s h t", t=TG)[:, 4 * g:4 * g + 4],
                               ps[O_BANKS[g % 2]][0:K, :].rearrange("p (s h t) -> p s h t", s=4, t=TG)) \
                    .then_inc(A.sem, A.mark(f"oT{g}"))

            def turn(it, more):
                for g in range(4):
                    sm.act_exp(act, it, g)
                    if g < 2:
                        act.wait_ge(T.sem, T.at(f"vt{g}", it))
                        nc.scalar.copy(v[:, 8 * g:8 * g + 8, :].rearrange("p a b -> p (a b)"),
                                       ps[T_BANKS[g]][:, :]).then_inc(A.sem, A.mark(f"v{g}"))
                if more:
                    even(it, 0)
                    even(it, 1)
                out(it, 0)
                if more:
                    even(it, 2)
                out(it, 1)
                if more:
                    for m in (3, 4, 5):
                        even(it, m)
                out(it, 2)
                out(it, 3)

            for m, (n, half) in enumerate(CHUNKS):
                A.credit(act, f"even_{n}{half}")
                even(-1, m)
            A.credit(act)
            core.load_table(ACT.Exp)
            turns(act, turn)

        @block.vector
        def _(dve):

            def odd(it, m):
                n, half = CHUNKS[m]
                dve.wait_ge(A.sem, A.at(f"even_{n}{half}", it))
                nc.vector.tensor_scalar(halves(dsts[n], half, 1), source(m, 1), K ** -0.5 if n == "q" else 1.0, None,
                                        ALU.mult).then_inc(V.sem, V.mark(f"odd_{n}{half}"))

            def turn(it, more):
                for g in range(4):
                    sm.dve_max(dve, it, g)
                sm.dve_recip(dve, it, 0)
                sm.dve_recip(dve, it, 1)
                sm.dve_copy(dve, it, 0)
                sm.dve_recip(dve, it, 2)
                sm.dve_copy(dve, it, 1)
                if more:
                    odd(it, 0)
                sm.dve_recip(dve, it, 3)
                sm.dve_copy(dve, it, 2)
                if more:
                    odd(it, 1)
                sm.dve_copy(dve, it, 3)
                if more:
                    for m in (2, 3, 4, 5):
                        odd(it, m)
                dve.wait_ge(T.sem, T.at("y", it))
                xr = core.x[:, ds(it, 1), :].rearrange("p a d -> p (a d)")
                nc.vector.tensor_tensor(xr, xr, ps[Y_BANK][:, 0:D], ALU.add).then_inc(V.sem, V.mark("x"))

            for m, (n, half) in enumerate(CHUNKS):
                V.credit(dve, f"odd_{n}{half}")
                odd(-1, m)
            V.credit(dve)
            turns(dve, turn)


def layer_l3_xattn(core, tag, w):
    nc, ps = core.nc, core.ps
    H, K = 2, 64
    c = Carve(core.scratch)
    wqk, wvl = w.take(2 * P), w.take(P)
    wkc, wvc = w.take(P), w.take(P)
    wo, bo = w.take(D), w.take(D)
    gx, bx, gl, bl, gq, gk = (w.take(1) for _ in range(6))
    cn, cnT = c.take(B, CTX), c.take(B * P)
    lat, latT = c.take(B, D), c.take(B * P)
    latT2, cnT2, bias2 = c.take(2 * P), c.take(2 * P), c.take(2, 2 * P)
    sq, qkn = c.take(2, 3 * P), c.take(2, 3 * P)
    ss, rn, half = c.take(2, 6), c.take(2, 6), c.take(2, 6)
    qT, kT, v = c.take(2, P), c.take(2, 2 * P), c.take(2, 2 * P)
    oT = c.take(2, P)
    vs, as_, gs, ts = names_of(2, True, 2)
    V = core.marks(f"{tag}_dve", ["ss0", "ss1", "rn0", "rn1", "inv0n", "inv1n", "qkn0", "qkn1", "kT0", "kT1"]
                   + vs + ["x0", "x1"])
    A = core.marks(f"{tag}_act", ["sq0", "sq1", "v", "qT0", "qT1"] + as_ + ["oT"])
    G = core.marks(f"{tag}_pool", ["copies", "root0", "root1"] + gs)
    T = core.marks(f"{tag}_pe", ["p0", "p1", "v", "tq0", "tq1"] + ts + ["y0", "y1"])
    groups = []
    for h in range(H):
        r = slice(K * h, K * h + K)
        groups.append(dict(q=[qT[r, u, :] for u in range(2)], k=[kT[r, u, :] for u in range(2)],
                           v=[v[:, u, kb * P + h * K:kb * P + (h + 1) * K] for u in range(2) for kb in range(2)],
                           o=[ps[5][r, u * P:(u + 1) * P] for u in range(2)]))
    sm = Softmax(core, c, groups, 2 * P, V, A, G, T, (6, 7), (0, 1), mask=lambda g: bias2)
    layernorm_all(core, tag)
    with nc.Block(f"{tag}_weights", no_gpsimd_drain=True) as block:

        @block.scalar
        def _(act):
            act.wait_ge(*core.w_loaded[tag])

        @block.vector
        def _(dve):
            dve.wait_ge(*core.w_loaded[tag])

    layernorm_all(core, f"{tag}_latents", src=core.xn, out=lat, outT=latT, gain=gl, bias=bl)
    layernorm_all(core, f"{tag}_context", src=core.ctxk, out=cn, outT=cnT, gain=gx[0:CTX], bias=bx[0:CTX], width=CTX)
    ready = core.sem(f"{tag}_constants")
    with nc.Block(tag, no_gpsimd_drain=True) as block:

        @block.gpsimd
        def _(pool):
            pool.sem_inc(G.sem, G.turn())
            nc.gpsimd.memset(half, 0.5).then_inc(ready, 1)
            nc.gpsimd.memset(bias2, 0.0).then_inc(ready, 1)
            pool.wait_ge(ready, 2)
            with pool.Fori(0, PAIRS) as it:
                pool.wait_ge(T.sem, T.at("v", it - 1))
                pool.wait_ge(V.sem, V.at("mask1", it - 1))
                nc.gpsimd.tensor_copy(latT2, latT[:, ds(it * 2 * P, 2 * P)])
                nc.gpsimd.tensor_copy(bias2[:, :, 0:P], core.lat_bias[:, ds(it * 2 * P, 2 * P)]
                                      .rearrange("p (a b) -> p a b", a=2))
                nc.gpsimd.tensor_copy(cnT2[0:CTX, :], cnT[0:CTX, ds(it * 2 * P, 2 * P)]) \
                    .then_inc(G.sem, G.mark("copies"))
                for u in range(2):
                    pool.wait_ge(V.sem, V.at(f"ss{u}", it))
                    nc.gpsimd.tensor_tensor(rn[:, u, :], ss[:, u, :], half[:, u, :], ALU.pow) \
                        .then_inc(G.sem, G.mark(f"root{u}"))
                sm.run_pool(pool, it)

        @block.tensor
        def _(pe):
            pe.sem_inc(T.sem, T.turn())
            with pe.Fori(0, PAIRS) as it:
                pe.wait_ge(G.sem, G.at("copies", it))
                pe.wait_ge(V.sem, V.at("x1", it - 1))
                for u in range(2):
                    lt, ct = latT2[:, u * P:(u + 1) * P], cnT2[0:CTX, u * P:(u + 1) * P]
                    nc.tensor.matmul(ps[u][:, 0:2 * P], lt, wqk, start=True, stop=True)
                    nc.tensor.matmul(ps[u][:, 2 * P:3 * P], ct, wkc[0:CTX, :], start=True, stop=True) \
                        .then_inc(T.sem, T.mark(f"p{u}"))
                for u in range(2):
                    lt, ct = latT2[:, u * P:(u + 1) * P], cnT2[0:CTX, u * P:(u + 1) * P]
                    nc.tensor.matmul(ps[2][:, u * 2 * P:u * 2 * P + P], ct, wvc[0:CTX, :], start=True, stop=True)
                    mm = nc.tensor.matmul(ps[2][:, u * 2 * P + P:(u + 1) * 2 * P], lt, wvl, start=True, stop=True)
                mm.then_inc(T.sem, T.mark("v"))
                for u in range(2):
                    pe.wait_ge(V.sem, V.at(f"qkn{u}", it))
                    for n in range(3):
                        mm = nc.tensor.transpose(ps[3 + u][:, n * P:(n + 1) * P], qkn[:, u, n * P:(n + 1) * P],
                                                 core.ident[:, :])
                    mm.then_inc(T.sem, T.mark(f"tq{u}"))
                pe.wait_ge(A.sem, A.at("qT1", it))
                pe.wait_ge(V.sem, V.at("kT1", it))
                sm.run_pe(pe, it)
                pe.wait_ge(A.sem, A.at("oT", it))
                for u in range(2):
                    nc.tensor.matmul(ps[3 + u][:, 0:D], oT[:, u, :], wo, start=True, stop=False)
                    nc.tensor.matmul(ps[3 + u][:, 0:D], core.ones[0:1, 0:P], bo[0:1, :], start=False, stop=True) \
                        .then_inc(T.sem, T.mark(f"y{u}"))

        @block.scalar
        def _(act):
            act.sem_inc(A.sem, A.turn())
            core.load_table(ACT.Exp)
            with act.Fori(0, PAIRS) as it:
                for u in range(2):
                    act.wait_ge(T.sem, T.at(f"p{u}", it))
                    nc.scalar.activation(sq[:, u, :], ps[u][:, 0:3 * P], ACT.Square).then_inc(A.sem, A.mark(f"sq{u}"))
                act.wait_ge(T.sem, T.at("v", it))
                nc.scalar.copy(v.rearrange("p a b -> p (a b)"), ps[2][:, :]).then_inc(A.sem, A.mark("v"))
                for u in range(2):
                    act.wait_ge(T.sem, T.at(f"tq{u}", it))
                    nc.scalar.activation(qT[:, u, :], ps[3 + u][:, 0:P], ACT.Copy, scale=gq) \
                        .then_inc(A.sem, A.mark(f"qT{u}"))
                sm.run_act(act, it)
                act.wait_ge(T.sem, T.at("o1", it))
                nc.scalar.copy(oT.rearrange("p a b -> p (a b)"), ps[5][:, 0:2 * P]).then_inc(A.sem, A.mark("oT"))

        @block.vector
        def _(dve):
            dve.sem_inc(V.sem, V.turn())
            dve.wait_ge(ready, 2)
            with dve.Fori(0, PAIRS) as it:
                for u in range(2):
                    dve.wait_ge(A.sem, A.at(f"sq{u}", it))
                    nc.vector.tensor_reduce(ss[:, u, :], sq[:, u, :].rearrange("p (n k) -> p n k", k=K), AX_X,
                                            ALU.add).then_inc(V.sem, V.mark(f"ss{u}"))
                for u in range(2):
                    dve.wait_ge(G.sem, G.at(f"root{u}", it))
                    nc.vector.tensor_scalar(rn[:, u, :], rn[:, u, :], K ** -0.5, 1e-8, ALU.mult, ALU.max) \
                        .then_inc(V.sem, V.mark(f"rn{u}"))
                for u in range(2):
                    dve.wait_ge(V.sem, V.at(f"rn{u}", it))
                    nc.vector.reciprocal(rn[:, u, :], rn[:, u, :]).then_inc(V.sem, V.mark(f"inv{u}n"))
                for u in range(2):
                    dve.wait_ge(V.sem, V.at(f"inv{u}n", it))
                    nc.vector.tensor_tensor(qkn[:, u, :].rearrange("p (n k) -> p n k", k=K),
                                            ps[u][:, 0:3 * P].rearrange("p (n k) -> p n k", k=K),
                                            rn[:, u, :].unsqueeze(2).broadcast_to([P, 6, K]), ALU.mult) \
                        .then_inc(V.sem, V.mark(f"qkn{u}"))
                for u in range(2):
                    dve.wait_ge(A.sem, A.at(f"qT{u}", it))
                    nc.vector.tensor_scalar(kT[:, u, 0:P], ps[3 + u][:, 2 * P:3 * P], gk, K ** -0.5, ALU.mult, ALU.mult)
                    nc.vector.tensor_scalar(kT[:, u, P:], ps[3 + u][:, P:2 * P], gk, K ** -0.5, ALU.mult, ALU.mult) \
                        .then_inc(V.sem, V.mark(f"kT{u}"))
                dve.wait_ge(G.sem, G.at("copies", it))
                sm.run_dve(dve, it)
                for u in range(2):
                    dve.wait_ge(T.sem, T.at(f"y{u}", it))
                    xr = core.x[:, ds(it * 2 + u, 1), :].rearrange("p a d -> p (a d)")
                    nc.vector.tensor_tensor(xr, xr, ps[3 + u][:, 0:D], ALU.add).then_inc(V.sem, V.mark(f"x{u}"))


class RelativeSoftmax(Softmax):

    def __init__(self, core, c, groups, V, A, G, T, banks_a, banks_s, banks_t, rel, rel_at):
        super().__init__(core, c, groups, P, V, A, G, T, banks_s, banks_t)
        self.banks_a, self.rel, self.rel_at = banks_a, rel, rel_at
        self.summed = c.take(2, BANK)

    def slots(self, it, g):
        return self.rel[:, ds(self.rel_at(it, g), 8 * P)].rearrange("p (c y t) -> p c y t", c=4, y=2)[:, :, 0, :]

    def pe_scores(self, pe, it, g):
        grp = self.groups[g]
        pe.wait_ge(self.V.sem, self.before(self.V, "add", g - 2, it))
        for j, (q, k) in enumerate(zip(grp["q"], grp["k"])):
            mm = self.nc.tensor.matmul(self.core.ps[self.banks_a[g % 2]][:, j * P:(j + 1) * P], k, q,
                                       start=True, stop=True)
        mm.then_inc(self.T.sem, self.T.mark(f"a{g}"))

    def pe_scores_read(self, pe, it):
        last = len(self.groups) - 1
        pe.wait_ge(self.V.sem, self.V.at(f"add{last}", it))
        pe.wait_ge(self.A.sem, self.A.at(f"exp{last}", it))

    def dve_add(self, dve, it, g):
        dve.wait_ge(self.T.sem, self.T.at(f"a{g}", it))
        dve.wait_ge(self.T.sem, self.before(self.T, "s", g - 2, it))
        four = lambda a: a.rearrange("p (c t) -> p c t", c=4)
        self.nc.vector.tensor_tensor(four(self.summed[:, g % 2, :]), four(self.core.ps[self.banks_a[g % 2]][:, :]),
                                     self.slots(it, g), ALU.add).then_inc(self.V.sem, self.V.mark(f"add{g}"))

    def pe_sums(self, pe, it, g):
        pe.wait_ge(self.V.sem, self.V.at(f"add{g}", it))
        pe.wait_ge(self.A.sem, self.before(self.A, "exp", g - 2, it))
        for j in range(4):
            mm = self.nc.tensor.transpose(self.core.ps[self.banks_s[g % 2]][:, j * P:(j + 1) * P],
                                          self.summed[:, g % 2, j * P:(j + 1) * P], self.core.ident[:, :])
        mm.then_inc(self.T.sem, self.T.mark(f"s{g}"))

    def dve_copy(self, dve, it, g):
        dve.wait_ge(self.G.sem, self.before(self.G, "keep", g - 2, it))
        super().dve_copy(dve, it, g)

    def pool_keep(self, pool, it, g):
        pool.wait_ge(self.V.sem, self.V.at(f"pT{g}", it))
        self.nc.gpsimd.tensor_copy(self.slots(it, g), self.probT[:, g % 2, :].rearrange("p (c t) -> p c t", c=4)) \
            .then_inc(self.G.sem, self.G.mark(f"keep{g}"))

    def run_pool(self, pool, it):
        n = len(self.groups)
        for g in range(n):
            self.pool_norm(pool, it, g)
            if g > 0:
                self.pool_keep(pool, it, g - 1)
        self.pool_keep(pool, it, n - 1)

    def names(self):
        n, ahead = len(self.groups), self.ahead
        t = [f"a{g}" for g in range(ahead)] + [f"s{g}" for g in range(ahead)]
        v = [f"add{g}" for g in range(ahead)] + [f"max{g}" for g in range(ahead)]
        p = []
        for g in range(n):
            more, last = g + ahead < n, g > 0
            t += ([f"a{g + ahead}", f"s{g + ahead}"] if more else []) + [f"t{g}"] \
                + ([f"o{g - 1}"] if last else [])
            v += ([f"add{g + ahead}"] if more else []) + [f"inv{g}"] + ([f"max{g + ahead}"] if more else []) \
                + ([f"pT{g - 1}"] if last else [])
            p += [f"norm{g}"] + ([f"keep{g - 1}"] if last else [])
        return v + [f"pT{n - 1}"], [f"exp{g}" for g in range(n)], p + [f"keep{n - 1}"], t + [f"o{n - 1}"]

    def run_pe(self, pe, it, before_turns, before_values):
        n, ahead = len(self.groups), self.ahead
        for g in range(ahead):
            self.pe_scores(pe, it, g)
        for g in range(ahead):
            self.pe_sums(pe, it, g)
        before_turns()
        for g in range(n + 1):
            if g + ahead < n:
                self.pe_scores(pe, it, g + ahead)
                self.pe_sums(pe, it, g + ahead)
            if g < n:
                self.pe_turn(pe, it, g)
            if g > 0:
                before_values(g - 1)
                self.pe_values(pe, it, g - 1)

    def run_dve(self, dve, it):
        n, ahead = len(self.groups), self.ahead
        for g in range(ahead):
            self.dve_add(dve, it, g)
        for g in range(ahead):
            self.dve_max(dve, it, g)
        for g in range(n + 1):
            if g + ahead < n:
                self.dve_add(dve, it, g + ahead)
            if g < n:
                self.dve_recip(dve, it, g)
            if g + ahead < n:
                self.dve_max(dve, it, g + ahead)
            if g > 0:
                self.dve_copy(dve, it, g - 1)


def layer_l2_attn(core, tag, w):
    nc, ps = core.nc, core.ps
    SC = 8 ** -0.5
    TCH = 32
    c = Carve(core.scratch)
    wq, wk, wv, wo = w.take(BANK), w.take(BANK), w.take(BANK), w.take(4, D)
    bq, bk, bv, bo = w.take(4), w.take(4), w.take(BANK), w.take(D)
    relv, relk = w.take(P, 8), w.take(2 * P)
    rel = c.take(P * P + P)
    rel3 = rel[:, 0:P * P].rearrange("p (n t) -> p n t", t=P)
    start = c.at
    layernorm_all(core, tag)

    qTall, q8, window = c.take(4, B * P), c.take(2, 16 * B, TCH // 2), c.take(P + TCH - 1)
    T = core.marks(f"{tag}_qall_pe", [f"q{n}" for n in range(8)])
    V = core.marks(f"{tag}_qall_dve", [f"q{n}" for n in range(8)])
    with nc.Block(f"{tag}_qall", no_gpsimd_drain=True) as block:

        @block.tensor
        def _(pe):
            pe.wait_ge(*core.w_loaded[tag])
            for n in range(8):
                nc.tensor.matmul(ps[n][:, :], wq[:, n // 2 * P:(n // 2 + 1) * P],
                                 core.xnT[:, n % 2 * BANK:(n % 2 + 1) * BANK], start=True, stop=True) \
                    .then_inc(T.sem, T.mark(f"q{n}"))

        @block.vector
        def _(dve):
            dve.wait_ge(*core.w_loaded[tag])
            for n in range(8):
                dve.wait_ge(T.sem, T.at(f"q{n}", -1))
                nc.vector.tensor_scalar(qTall[:, n // 2, n % 2 * BANK:(n % 2 + 1) * BANK], ps[n][:, :],
                                        bq[:, n // 2:n // 2 + 1], SC, ALU.add, ALU.mult) \
                    .then_inc(V.sem, V.mark(f"q{n}"))

    QB = TCH // 4
    T = core.marks(f"{tag}_rel_pe", [f"r{n}" for n in range(QB)])
    V = core.marks(f"{tag}_rel_dve", [f"r{n}" for n in range(0, QB, 2)])
    A = core.marks(f"{tag}_rel_act", [f"r{n}" for n in range(1, QB, 2)])
    G = core.marks(f"{tag}_rel_pool", ["window"])
    q8_loaded = [core.sem(f"{tag}_q8_loaded{half}") for half in range(2)]

    def out_of_bank(eng, copy, marks, it, n):
        eng.wait_ge(T.sem, T.at(f"r{n}", it))
        copy(rel3[:, :, ds(it * TCH + 4 * n, 4)], ps[n][:, :].rearrange("p (t n) -> p n t", t=4)) \
            .then_inc(marks.sem, marks.mark(f"r{n}"))

    with nc.Block(f"{tag}_rel", no_gpsimd_drain=True) as block:

        @block.sync
        def _(sp):
            with sp.Fori(0, P // TCH) as it:
                for half in range(2):
                    sp.wait_ge(T.sem, T.at(f"r{QB // 2 * (half + 1) - 1}", it - 1))
                    for j in range(4):
                        sp.dma_start(q8[0:8, half, 32 * j:32 * j + 32], qTall[32 * j:32 * j + 8, :, :]
                                     .rearrange("p i (b t) -> p (i b) t", t=P)
                                     [:, :, ds(it * TCH + half * (TCH // 2), TCH // 2)]) \
                            .then_inc(q8_loaded[half], 16)

        @block.gpsimd
        def _(pool):
            pool.sem_inc(G.sem, G.turn())
            with pool.Fori(0, P // TCH) as it:
                pool.wait_ge(T.sem, T.at(f"r{QB - 1}", it - 1))
                nc.gpsimd.tensor_copy(window[0:8, :], relk[0:8, ds(it * (-TCH) + (P - TCH), P + TCH - 1)]) \
                    .then_inc(G.sem, G.mark("window"))

        @block.tensor
        def _(pe):
            pe.sem_inc(T.sem, T.turn())
            with pe.Fori(0, P // TCH) as it:
                pe.wait_ge(G.sem, G.at("window", it))
                for n in range(QB):
                    half = n // (QB // 2)
                    if n % (QB // 2) == 0:
                        pe.wait_ge(q8_loaded[half], it * 64 + 64)
                    m = A if n % 2 else V
                    pe.wait_ge(m.sem, m.at(f"r{n}", it - 1))
                    for i in range(4):
                        t = 4 * n + i
                        mm = nc.tensor.matmul(ps[n][:, i * P:(i + 1) * P], window[0:8, TCH - 1 - t:TCH - 1 - t + P],
                                              q8[0:8, half, :, t % (TCH // 2)]
                                              .rearrange("p (j i b) -> p i j b", j=4, i=4), start=True, stop=True)
                    mm.then_inc(T.sem, T.mark(f"r{n}"))

        @block.vector
        def _(dve):
            dve.sem_inc(V.sem, V.turn())
            with dve.Fori(0, P // TCH) as it:
                for n in range(0, QB, 2):
                    out_of_bank(dve, nc.vector.tensor_copy, V, it, n)

        @block.scalar
        def _(act):
            act.sem_inc(A.sem, A.turn())
            with act.Fori(0, P // TCH) as it:
                for n in range(1, QB, 2):
                    out_of_bank(act, nc.scalar.copy, A, it, n)

    c.at = start
    probe = RelativeSoftmax.__new__(RelativeSoftmax)
    probe.groups, probe.ahead = [None] * 8, 2
    softmax = []

    def rel_at(it, g):
        u, j = g // 4, g % 4
        return it * (2 * 8 * P) + ((j % 2) * 64 + u * 8 + j // 2) * P

    def make(groups, V, A, G, T, _):
        softmax.append(RelativeSoftmax(core, c, groups, V, A, G, T, (4, 5), (6, 7), (0, 1), rel, rel_at))
        return softmax[0]

    attention_by_pairs(core, tag, c, probe.names(), lambda qT, kT, v: small_groups(qT, kT, v, ps, (2, 3)),
                       make, wq, wk, wv, wo, core.xnT, P, SC, bq=bq, bk=bk, bv=bv, bo=bo)
    G = softmax[0].G
    kept = (G.sem, G.at(f"keep{len(softmax[0].groups) - 1}", PAIRS - 1))
    c.at = start
    VCH = 16
    HALF = VCH // 2
    out2, vecs = c.take(32, P), c.take(VCH, 32)
    turned = c.take(2, P, HALF)
    T = core.marks(f"{tag}_relv_pe", ["w0", "w1"])
    V = core.marks(f"{tag}_relv_dve", ["w0", "w1"])
    A = core.marks(f"{tag}_relv_act", ["p0", "p1"])
    G = core.marks(f"{tag}_relv_pool", ["vecs"])
    zeroed = core.sem(f"{tag}_relv_zeroed")
    with nc.Block(f"{tag}_relv", no_gpsimd_drain=True) as block:

        @block.gpsimd
        def _(pool):
            pool.sem_inc(G.sem, G.turn())
            nc.gpsimd.memset(vecs, 0.0).then_inc(zeroed, 1)
            pool.wait_ge(zeroed, 1)
            with pool.Fori(0, P // VCH) as it:
                pool.wait_ge(T.sem, T.at("w1", it - 1))
                nc.gpsimd.tensor_copy(vecs[:, :, 0:8], relv[:, ds(it * VCH, VCH), :]).then_inc(G.sem, G.mark("vecs"))

        @block.scalar
        def _(act):
            act.sem_inc(A.sem, A.turn())
            act.wait_ge(*kept)
            with act.Fori(0, P // VCH) as it:
                for n in range(2):
                    act.wait_ge(T.sem, T.at(f"w{n}", it - 1))
                    nc.scalar.copy(turned[:, n, :, :], rel3[:, :, ds(it * VCH + HALF * n, HALF)]) \
                        .then_inc(A.sem, A.mark(f"p{n}"))

        @block.tensor
        def _(pe):
            pe.sem_inc(T.sem, T.turn())
            with pe.Fori(0, P // VCH) as it:
                pe.wait_ge(G.sem, G.at("vecs", it))
                for n in range(2):
                    pe.wait_ge(A.sem, A.at(f"p{n}", it))
                    pe.wait_ge(V.sem, V.at(f"w{n}", it - 1))
                    probs = turned[:, n, :, :].rearrange("p (a c y z) t -> p a c y z t", a=2, c=4, y=2)
                    for i in range(HALF):
                        for j in range(4):
                            z = (j % 2) * 4
                            mm = nc.tensor.matmul(ps[n][32 * j:32 * j + 32, i * 32:(i + 1) * 32],
                                                  vecs[:, HALF * n + i, :], probs[:, :, :, j // 2, z:z + 4, i],
                                                  start=True, stop=True)
                    mm.then_inc(T.sem, T.mark(f"w{n}"))

        @block.vector
        def _(dve):
            dve.sem_inc(V.sem, V.turn())
            with dve.Fori(0, P // VCH) as it:
                for n in range(2):
                    dve.wait_ge(T.sem, T.at(f"w{n}", it))
                    nc.vector.tensor_copy(out2[:, :, ds(it * VCH + HALF * n, HALF)],
                                          ps[n][:, 0:32 * HALF].rearrange("p (t n) -> p n t", n=32)) \
                        .then_inc(V.sem, V.mark(f"w{n}"))

    done, added = core.sem(f"{tag}_relv_out"), core.sem(f"{tag}_relv_added")
    out4 = out2.rearrange("p (a c z) t -> p a c z t", a=2, c=4)
    with nc.Block(f"{tag}_relv_proj", no_gpsimd_drain=True) as block:

        @block.tensor
        def _(pe):
            for b in range(B):
                for i in range(4):
                    mm = nc.tensor.matmul(ps[b // 4][:, b % 4 * P:(b % 4 + 1) * P], out4[:, b % 2, i, b // 2, :],
                                          wo[:, i, :], start=(i == 0), stop=(i == 3))
                if b % 4 == 3:
                    mm.then_inc(done, 1)

        @block.vector
        def _(dve):
            for half in range(2):
                dve.wait_ge(done, half + 1)
                xs = core.x[:, half * 4:half * 4 + 4, :].rearrange("p b d -> p (b d)")
                nc.vector.tensor_tensor(xs, xs, ps[half][:, :], ALU.add).then_inc(added, 1)


def shift_tokens(core, tag, src, out, shift, outT=None, extra=None):
    nc, ps = core.nc, core.ps
    s_pe, s_dve, s_act = core.sem(f"{tag}_pe"), core.sem(f"{tag}_dve"), core.sem(f"{tag}_act")
    HF = D // 2
    with nc.Block(tag, no_gpsimd_drain=True) as block:

        @block.tensor
        def _(pe):
            nc.tensor.matmul(ps[0][:, :].rearrange("p (b d) -> p b d", d=HF), shift, src[:, :, HF:],
                             start=True, stop=True).then_inc(s_pe, 1)
            if outT is not None:
                pe.wait_ge(s_dve, 2)
                for b in range(B):
                    nc.tensor.transpose(ps[1 + b // 4][:, b % 4 * P:(b % 4 + 1) * P], out[:, b, :],
                                        core.ident[:, :]).then_inc(s_pe, 1)

        @block.vector
        def _(dve):
            nc.vector.tensor_copy(out[:, :, 0:HF], src[:, :, 0:HF]).then_inc(s_dve, 1)
            dve.wait_ge(s_pe, 1)
            nc.vector.tensor_copy(out[:, :, HF:], ps[0][:, :].rearrange("p (b d) -> p b d", d=HF)).then_inc(s_dve, 1)
            if extra is not None:
                extra(dve)
            if outT is not None:
                dve.wait_ge(s_pe, 1 + B)
                nc.vector.tensor_copy(outT[:, BANK:], ps[2][:, :]).then_inc(s_dve, 1)

        @block.scalar
        def _(act):
            if outT is not None:
                act.wait_ge(s_pe, 5)
                nc.scalar.copy(outT[:, 0:BANK], ps[1][:, :]).then_inc(s_act, 1)


def local_attention(core, tag, c, res, wqkv, wo, tables, bias):
    nc, ps = core.nc, core.ps
    H, K = 8, 64
    S_BANKS, Q_BANKS, K_BANKS, V_BANKS, Y_BANKS = (6, 7, 4, 5), (4, 5), (6, 7), (0, 1), (2, 3)
    hT2 = c.take(2, P)
    sq = c.take(2, 2 * BANK)
    ss, rn, half = c.take(2, 2 * H), c.take(2, 2 * H), c.take(2, 2 * H)
    unit_ = [c.take(H, K) for _ in range(4)]
    turned = [c.take(H, K) for _ in range(4)]
    qT, kT, v, oT = c.take(2, 4, P), c.take(2, 4, P), c.take(2, BANK), c.take(2, BANK)
    QK = [(u, n) for u in range(2) for n in range(2)]
    on_dve = ["ss0", "ss1", "rn0", "inv0n", "unit00", "unit01", "rn1", "inv1n", "unit10", "unit11"] \
        + [f"{a}{u}{n}" for u, n in QK for a in ("cos", "rot")] + ["kT0", "kT1"]
    on_act, on_pool = ["sq0", "sq1", "v0", "v1", "qT0", "qT1"], ["copy", "root0", "root1"] + [f"sin{u}{n}" for u, n in QK]
    on_pe = ["q0", "k0", "q1", "k1", "v0", "v1", "tq0", "tk0", "tq1", "tk1"]
    V = core.marks(f"{tag}_dve", [f"{n}{g}" for g in range(4) for n in ("mask", "max")]
                   + ["inv0", "inv1", "pT0", "inv2", "pT1", "ss0", "inv3", "pT2", "ss1", "pT3"]
                   + on_dve[2:-2] + ["x0", "x1", "kT0", "kT1"])
    A = core.marks(f"{tag}_act", [f"exp{g}" for g in range(4)] + ["sq0", "sq1", "oT0", "oT1", "v0", "v1", "qT0", "qT1"])
    G = core.marks(f"{tag}_pool", ["copy"] + [f"norm{g}" for g in range(4)] + on_pool[1:])
    T = core.marks(f"{tag}_pe", ["s0", "s1", "s2", "s3", "q0", "k0", "t0", "t1", "q1", "k1", "o0", "t2", "o1", "t3",
                                 "o2", "o3", "v0", "v1", "y0", "y1", "tq0", "tk0", "tq1", "tk1"])
    for m, names in ((V, on_dve), (A, on_act), (G, on_pool), (T, on_pe)):
        m.leave_out(PAIRS - 1, names)
    groups = []
    for u in range(2):
        for par in range(2):
            r = slice(K * par, K * par + K)
            groups.append(dict(q=[qT[r, u, i, :] for i in range(4)], k=[kT[r, u, i, :] for i in range(4)],
                               v=[v[:, u, (2 * i + par) * K:(2 * i + par + 1) * K] for i in range(4)],
                               o=[ps[Y_BANKS[u]][r, i * P:(i + 1) * P] for i in range(4)]))
    sm = Softmax(core, c, groups, P, V, A, G, T, S_BANKS, (0, 1), mask=lambda g: for_heads(bias))
    ready = core.sem(f"{tag}_constants")

    def turns(eng, turn):
        with eng.Fori(0, PAIRS - 1) as it:
            turn(it, True)
        turn(PAIRS - 1, False)

    def passed(m, eng, first, name):
        if first:
            m.credit(eng, name)

    with nc.Block(tag, no_gpsimd_drain=True) as block:

        @block.gpsimd
        def _(pool):

            def copy_rows(it, first=False):
                passed(G, pool, first, "copy")
                if not first:
                    pool.wait_ge(T.sem, T.at("v1", it - 1))
                nc.gpsimd.tensor_copy(hT2.rearrange("p a b -> p (a b)"), core.xnT[:, ds(it * (2 * P) + 2 * P, 2 * P)]) \
                    .then_inc(G.sem, G.mark("copy"))

            def rotate(it, first=False):
                for u in range(2):
                    passed(G, pool, first, f"root{u}")
                    pool.wait_ge(V.sem, V.at(f"ss{u}", it))
                    nc.gpsimd.tensor_tensor(rn[:, u, :], ss[:, u, :], half[:, u, :], ALU.pow) \
                        .then_inc(G.sem, G.mark(f"root{u}"))
                for u, n in QK:
                    pool.wait_ge(V.sem, V.at(f"unit{u}{n}", it))
                    src, dst, sin = unit_[2 * u + n], turned[2 * u + n], tables[2 * n + 1]
                    nc.gpsimd.tensor_tensor(dst[:, :, 0:32], src[:, :, 32:], for_heads(sin[:, 0:32], H), ALU.mult)
                    nc.gpsimd.tensor_tensor(dst[:, :, 32:], src[:, :, 0:32], for_heads(sin[:, 32:], H), ALU.mult) \
                        .then_inc(G.sem, G.mark(f"sin{u}{n}"))

            def turn(it, more):
                if more:
                    copy_rows(it)
                sm.run_pool(pool, it)
                if more:
                    rotate(it)

            nc.gpsimd.memset(half, 0.5).then_inc(ready, 1)
            pool.wait_ge(ready, 1)
            copy_rows(-1, True)
            rotate(-1, True)
            turns(pool, turn)

        @block.tensor
        def _(pe):

            def project_qk(it, u, first=False):
                passed(T, pe, first, f"q{u}")
                pe.wait_ge(G.sem, G.at("copy", it))
                for n, banks in enumerate((Q_BANKS, K_BANKS)):
                    nc.tensor.matmul(ps[banks[u]][:, :], hT2[:, u, :], wqkv[:, n * BANK:(n + 1) * BANK],
                                     start=True, stop=True).then_inc(T.sem, T.mark("qk"[n] + str(u)))

            def project_v(it, first=False):
                passed(T, pe, first, "v0")
                for u in range(2):
                    nc.tensor.matmul(ps[V_BANKS[u]][:, :], hT2[:, u, :], wqkv[:, 2 * BANK:3 * BANK],
                                     start=True, stop=True).then_inc(T.sem, T.mark(f"v{u}"))

            def turn_qk(it, first=False):
                passed(T, pe, first, "tq0")
                for u, n in QK:
                    pe.wait_ge(V.sem, V.at(f"rot{u}{n}", it))
                    for i in range(4):
                        mm = nc.tensor.transpose(ps[(Q_BANKS, K_BANKS)[n][u]][:, i * P:(i + 1) * P],
                                                 unit_[2 * u + n].rearrange("p h k -> p (h k)")[:, i * P:(i + 1) * P],
                                                 core.ident[:, :])
                    mm.then_inc(T.sem, T.mark("t" + "qk"[n] + str(u)))

            def turn(it, more):
                pe.wait_ge(A.sem, A.at("qT1", it - 1))
                pe.wait_ge(V.sem, V.at("kT1", it - 1))
                for g in range(4):
                    sm.pe_scores(pe, it, g)
                if more:
                    sm.pe_scores_read(pe, it)
                    project_qk(it, 0)
                pe.wait_ge(A.sem, A.at("v1", it - 1))
                sm.pe_turn(pe, it, 0)
                sm.pe_turn(pe, it, 1)
                if more:
                    project_qk(it, 1)
                pe.wait_ge(V.sem, V.at("x1", it - 1))
                sm.pe_values(pe, it, 0)
                sm.pe_turn(pe, it, 2)
                sm.pe_values(pe, it, 1)
                sm.pe_turn(pe, it, 3)
                sm.pe_values(pe, it, 2)
                sm.pe_values(pe, it, 3)
                if more:
                    project_v(it)
                for u in range(2):
                    pe.wait_ge(A.sem, A.at(f"oT{u}", it))
                    for i in range(4):
                        mm = nc.tensor.matmul(ps[Y_BANKS[u]][:, 0:D], oT[:, u, i * P:(i + 1) * P], wo[:, i, :],
                                              start=(i == 0), stop=(i == 3))
                    mm.then_inc(T.sem, T.mark(f"y{u}"))
                if more:
                    turn_qk(it)

            project_qk(-1, 0, True)
            project_qk(-1, 1, True)
            project_v(-1, True)
            turn_qk(-1, True)
            turns(pe, turn)

        @block.scalar
        def _(act):

            def squares(it, first=False):
                passed(A, act, first, "sq0")
                for u in range(2):
                    act.wait_ge(T.sem, T.at(f"k{u}", it))
                    if not first:
                        act.wait_ge(V.sem, V.at(f"ss{u}", it - 1))
                    nc.scalar.activation(sq[:, u, 0:BANK], ps[Q_BANKS[u]][:, :], ACT.Square)
                    nc.scalar.activation(sq[:, u, BANK:], ps[K_BANKS[u]][:, :], ACT.Square) \
                        .then_inc(A.sem, A.mark(f"sq{u}"))

            def copies_out(it, first=False):
                passed(A, act, first, "v0")
                for u in range(2):
                    act.wait_ge(T.sem, T.at(f"v{u}", it))
                    nc.scalar.copy(v[:, u, :], ps[V_BANKS[u]][:, :]).then_inc(A.sem, A.mark(f"v{u}"))
                for u in range(2):
                    act.wait_ge(T.sem, T.at(f"tq{u}", it))
                    nc.scalar.copy(qT[:, u].rearrange("p a b -> p (a b)"), ps[Q_BANKS[u]][:, :]) \
                        .then_inc(A.sem, A.mark(f"qT{u}"))

            def turn(it, more):
                sm.run_act(act, it)
                if more:
                    squares(it)
                for u in range(2):
                    act.wait_ge(T.sem, T.at(f"o{2 * u + 1}", it))
                    nc.scalar.copy(oT[:, u, :], ps[Y_BANKS[u]][:, :]).then_inc(A.sem, A.mark(f"oT{u}"))
                if more:
                    copies_out(it)

            core.load_table(ACT.Exp)
            squares(-1, True)
            copies_out(-1, True)
            turns(act, turn)

        @block.vector
        def _(dve):

            def sums(it, u, first=False):
                passed(V, dve, first, f"ss{u}")
                dve.wait_ge(A.sem, A.at(f"sq{u}", it))
                nc.vector.tensor_reduce(ss[:, u, :], sq[:, u, :].rearrange("p (n k) -> p n k", k=K), AX_X, ALU.add) \
                    .then_inc(V.sem, V.mark(f"ss{u}"))

            def rotate(it, first=False):
                passed(V, dve, first, "rn0")
                for u in range(2):
                    dve.wait_ge(G.sem, G.at(f"root{u}", it))
                    nc.vector.tensor_scalar(rn[:, u, :], rn[:, u, :], 1e-12, None, ALU.max) \
                        .then_inc(V.sem, V.mark(f"rn{u}"))
                    dve.wait_ge(V.sem, V.at(f"rn{u}", it))
                    nc.vector.reciprocal(rn[:, u, :], rn[:, u, :]).then_inc(V.sem, V.mark(f"inv{u}n"))
                    dve.wait_ge(V.sem, V.at(f"inv{u}n", it))
                    for n, banks in enumerate((Q_BANKS, K_BANKS)):
                        nc.vector.tensor_tensor(unit_[2 * u + n],
                                                ps[banks[u]][:, :].rearrange("p (h k) -> p h k", k=K),
                                                rn[:, u, n * H:(n + 1) * H].unsqueeze(2).broadcast_to([P, H, K]),
                                                ALU.mult).then_inc(V.sem, V.mark(f"unit{u}{n}"))
                for u, n in QK:
                    dve.wait_ge(G.sem, G.at(f"sin{u}{n}", it))
                    nc.vector.tensor_tensor(unit_[2 * u + n], unit_[2 * u + n], for_heads(tables[2 * n], H),
                                            ALU.mult).then_inc(V.sem, V.mark(f"cos{u}{n}"))
                    dve.wait_ge(V.sem, V.at(f"cos{u}{n}", it))
                    nc.vector.tensor_tensor(unit_[2 * u + n], unit_[2 * u + n], turned[2 * u + n], ALU.add) \
                        .then_inc(V.sem, V.mark(f"rot{u}{n}"))

            def keys_out(it, first=False):
                passed(V, dve, first, "kT0")
                for u in range(2):
                    dve.wait_ge(T.sem, T.at(f"tk{u}", it))
                    nc.vector.tensor_copy(kT[:, u].rearrange("p a b -> p (a b)"), ps[K_BANKS[u]][:, :]) \
                        .then_inc(V.sem, V.mark(f"kT{u}"))

            def turn(it, more):
                for g in range(4):
                    sm.dve_max(dve, it, g)
                sm.dve_recip(dve, it, 0)
                sm.dve_recip(dve, it, 1)
                sm.dve_copy(dve, it, 0)
                sm.dve_recip(dve, it, 2)
                sm.dve_copy(dve, it, 1)
                if more:
                    sums(it, 0)
                sm.dve_recip(dve, it, 3)
                sm.dve_copy(dve, it, 2)
                if more:
                    sums(it, 1)
                sm.dve_copy(dve, it, 3)
                if more:
                    rotate(it)
                for u in range(2):
                    dve.wait_ge(T.sem, T.at(f"y{u}", it))
                    xr = res[:, ds(it * 2 + u, 1), :].rearrange("p a d -> p (a d)")
                    nc.vector.tensor_tensor(xr, xr, ps[Y_BANKS[u]][:, 0:D], ALU.add).then_inc(V.sem, V.mark(f"x{u}"))
                if more:
                    keys_out(it)

            dve.wait_ge(ready, 1)
            for u in range(2):
                sums(-1, u, True)
            rotate(-1, True)
            keys_out(-1, True)
            turns(dve, turn)


def gated_ffn(core, tag, c, res, w1, ba, bg, w2, b2, widths):
    nc, ps = core.nc, core.ps
    HID, N = sum(widths), len(widths)
    gl, hT = c.take(2, BANK), [c.take(N, BANK) for _ in range(2)]
    pe_up, act_gelu, dve_gate, pe_down, dve_add = (core.sem(f"{tag}_{n}") for n in ("up", "gelu", "gate", "down", "add"))
    with nc.Block(tag, no_gpsimd_drain=True) as block:

        @block.tensor
        def _(pe):
            for half in range(2):
                for i, m in enumerate(widths):
                    n = half * N + i
                    if n >= 2:
                        pe.wait_ge(dve_gate, n - 1)
                    for part in range(2):
                        mm = nc.tensor.matmul(ps[2 * (n % 2) + part][0:m, :],
                                              w1[:, part * HID + i * P:part * HID + i * P + m],
                                              core.xnT[:, half * BANK:(half + 1) * BANK], start=True, stop=True)
                    mm.then_inc(pe_up, 1)
            for half in range(2):
                pe.wait_ge(dve_gate, N * (half + 1))
                for t in range(4):
                    for i, m in enumerate(widths):
                        nc.tensor.matmul(ps[4 + half][:, t * P:(t + 1) * P], hT[half][0:m, i, t * P:(t + 1) * P],
                                         w2[0:m, i, :], start=(i == 0), stop=False)
                    mm = nc.tensor.matmul(ps[4 + half][:, t * P:(t + 1) * P], core.ones[0:1, 0:P], b2[0:1, :],
                                          start=False, stop=True)
                mm.then_inc(pe_down, 1)

        @block.scalar
        def _(act):
            for n in range(2 * N):
                i, m = n % N, widths[n % N]
                act.wait_ge(pe_up, n + 1)
                if n >= 2:
                    act.wait_ge(dve_gate, n - 1)
                nc.scalar.activation(gl[0:m, n % 2, :], ps[2 * (n % 2) + 1][0:m, :], ACT.Gelu, bias=bg[0:m, i:i + 1]) \
                    .then_inc(act_gelu, 1)

        @block.vector
        def _(dve):
            for n in range(2 * N):
                i, m = n % N, widths[n % N]
                dve.wait_ge(act_gelu, n + 1)
                nc.vector.scalar_tensor_tensor(out=hT[n // N][0:m, i, :], in0=ps[2 * (n % 2)][0:m, :],
                                               scalar=ba[0:m, i:i + 1], in1=gl[0:m, n % 2, :],
                                               op0=ALU.add, op1=ALU.mult).then_inc(dve_gate, 1)
            for half in range(2):
                dve.wait_ge(pe_down, half + 1)
                xs = res[:, half * 4:half * 4 + 4, :].rearrange("p b d -> p (b d)")
                nc.vector.tensor_tensor(xs, xs, ps[4 + half][:, :], ALU.add).then_inc(dve_add, 1)


def layer_l1_ffn(core, tag, w):
    nc = core.nc
    DEPTH, HID, K = 2, 341, 64
    widths = [P, P, HID - 2 * P]
    c = Carve(core.scratch)
    res, shifted = c.take(B, D), c.take(B, D)
    tables = [c.take(K) for _ in range(4)]
    base = [w.take(K) for _ in range(4)]
    bias, shift = w.take(P), w.take(P)
    start = c.at
    layernorm_all(core, tag, out=res)
    for d in range(DEPTH):
        wqkv, wo, w1, w2 = w.take(3 * BANK), w.take(4, D), w.take(2 * HID), w.take(3, D)
        ba, bg, b2, lg, lb = w.take(3), w.take(3), w.take(D), w.take(1), w.take(1)
        gains = [w.take(K) for _ in range(4)]
        made = core.sem(f"{tag}{d}_tables")
        if d == 0:
            with nc.Block(f"{tag}_weights", no_gpsimd_drain=True) as block:

                @block.tensor
                def _(pe):
                    pe.wait_ge(*core.w_loaded[tag])

                @block.vector
                def _(dve):
                    dve.wait_ge(*core.w_loaded[tag])

        def make_tables(dve):
            for n in range(4):
                nc.vector.tensor_tensor(tables[n], base[n], gains[n], ALU.mult).then_inc(made, 1)

        shift_tokens(core, f"{tag}{d}_shift", res, shifted, shift, outT=core.xnT, extra=make_tables)
        c.at = start
        local_attention(core, f"{tag}{d}_attn", c, res, wqkv, wo, tables, bias)
        shift_tokens(core, f"{tag}{d}_shift2", res, shifted, shift)
        layernorm_all(core, f"{tag}{d}_norm", src=shifted, out=shifted, gain=lg, bias=lb)
        c.at = start
        gated_ffn(core, f"{tag}{d}_ffn", c, res, w1, ba, bg, w2, b2, widths)
    added = core.sem(f"{tag}_added")
    with nc.Block(f"{tag}_add", no_gpsimd_drain=True) as block:

        @block.vector
        def _(dve):
            nc.vector.tensor_tensor(core.x[:, :, :], core.x[:, :, :], res, ALU.add).then_inc(added, 1)


SSM = 64
TAPS = 16
SEGMENTS = P // TAPS


def conv_angles_act(core, act):
    nc, s = core.nc, core.ssm
    act.wait_ge(s.loaded, 16)
    nc.scalar.activation(s.dt, s.log_dt, ACT.Exp).then_inc(s.exped, 1)
    act.wait_ge(s.scaled, 1)
    nc.scalar.activation(s.er, s.ar, ACT.Exp).then_inc(s.exped, 1)
    act.wait_ge(s.scaled, 2)
    nc.scalar.activation(s.ang, s.ang, ACT.Sin).then_inc(s.sined, 1)


def conv_angles_dve(core, dve):
    nc, s = core.nc, core.ssm
    PI = float(np.pi)
    ROUND = 1.5 * 2 ** 23
    TAU_HI = 6.28125
    TAU_LO = 2 * PI - TAU_HI
    link = Link(dve, s.chain)
    tt, ts, stt = nc.vector.tensor_tensor, nc.vector.tensor_scalar, nc.vector.scalar_tensor_tensor
    dve.wait_ge(s.exped, 1)
    ts(s.ar, s.a_re, s.dt, None, ALU.mult).then_inc(s.scaled, 1)
    link(ts(s.ai, s.a_im, s.dt, None, ALU.mult))
    link(ts(s.ang[:, 0], s.ai, 0.0, None, ALU.add), ts(s.ang[:, 1], s.ai, PI / 2, None, ALU.add))
    link(ts(s.turns, s.ang, 1 / (2 * PI), None, ALU.mult))
    link(ts(s.turns, s.turns, ROUND, None, ALU.add))
    link(ts(s.turns, s.turns, ROUND, None, ALU.subtract))
    link(stt(s.ang, s.turns, -TAU_HI, s.ang, ALU.mult, ALU.add))
    link(stt(s.ang, s.turns, -TAU_LO, s.ang, ALU.mult, ALU.add))
    ts(s.ang, s.ang, -3.1415925, 3.1415925, ALU.max, ALU.min).then_inc(s.scaled, 1)
    link(tt(s.den, s.a_re, s.a_re, ALU.mult), tt(s.ai, s.a_im, s.a_im, ALU.mult))
    link(tt(s.den, s.den, s.ai, ALU.add))
    link(nc.vector.reciprocal(s.den, s.den))
    link(ts(s.den, s.den, 2.0, None, ALU.mult))
    dve.wait_ge(s.exped, 2)
    dve.wait_ge(s.sined, 1)


def conv_kernels(core, pool):
    nc, s = core.nc, core.ssm
    N, R, S = SSM, TAPS, SEGMENTS
    c = Carve(core.scratch)
    c.at = SCRATCH - (6 * R * N + 2 * S * N + 4 * N)
    t = [c.take(R // 2, N) for _ in range(4)]
    z = c.take(R, 2 * N)
    wa = c.take(S, 2 * N)
    pw = c.take(2, 2 * N)
    prod = c.take(R, 2 * N)
    er, ang, den = s.er, s.ang, s.den
    link = Link(pool, s.pool_chain)
    tt, ts = nc.gpsimd.tensor_tensor, nc.gpsimd.tensor_scalar

    def cmul(out, a, b):
        sh = out[0].shape
        u = [x[:, 0:sh[1]] if len(sh) == 3 else x[:, 0] for x in t]
        link(tt(u[0], a[0], b[0], ALU.mult), tt(u[1], a[1], b[1], ALU.mult),
             tt(u[2], a[0], b[1], ALU.mult), tt(u[3], a[1], b[0], ALU.mult))
        link(tt(out[0], u[0], u[1], ALU.subtract), tt(out[1], u[2], u[3], ALU.add))

    def pair(v):
        return v[:, 0:N], v[:, N:2 * N]

    one = pair(z[:, 1])
    link(tt(one[0], er, ang[:, 1], ALU.mult), tt(one[1], er, ang[:, 0], ALU.mult))
    link(ts(s.ar, one[0], -1.0, None, ALU.add), ts(s.ai, s.a_im, -1.0, None, ALU.mult))
    w0 = pair(wa[:, 0])
    cmul(w0, (s.c_re, s.c_im), (s.ar, one[1]))
    cmul((ang[:, 0], ang[:, 1]), w0, (s.a_re, s.ai))
    link(tt(w0[0], ang[:, 0], den, ALU.mult), tt(ang[:, 1], ang[:, 1], den, ALU.mult))
    link(ts(w0[1], ang[:, 1], -1.0, None, ALU.mult),
         nc.gpsimd.memset(z[:, 0, 0:N], 1.0), nc.gpsimd.memset(z[:, 0, N:], 0.0),
         nc.gpsimd.memset(core.conv_kp, 0.0))
    cmul(pair(pw[:, 0]), one, one)
    k, at = 2, 0
    while k < R:
        lo, hi = z[:, 0:k], z[:, k:2 * k]
        p = [x.unsqueeze(1).broadcast_to([P, k, N]) for x in pair(pw[:, at])]
        cmul((hi[:, :, 0:N], hi[:, :, N:]), (lo[:, :, 0:N], lo[:, :, N:]), p)
        cmul(pair(pw[:, 1 - at]), pair(pw[:, at]), pair(pw[:, at]))
        k, at = 2 * k, 1 - at
    q = pair(pw[:, at])
    link(ts(q[1], q[1], -1.0, None, ALU.mult))
    for a in range(1, S):
        cmul(pair(wa[:, a]), pair(wa[:, a - 1]), q)
    for a in range(S):
        link(tt(prod, z, wa[:, a].unsqueeze(1).broadcast_to([P, R, 2 * N]), ALU.mult))
        h = N
        while h:
            out = prod[:, :, 0:h] if h > 1 else core.conv_kp[:, P - 1 + R * a:P - 1 + R * (a + 1)].unsqueeze(2)
            link(tt(out, prod[:, :, 0:h], prod[:, :, h:2 * h], ALU.add))
            h //= 2
    tap0 = core.conv_kp[:, P - 1:P]
    link(tt(tap0, tap0, s.skip, ALU.add))


class StateSpace:

    def __init__(self, core):
        c = Carve(core.sbuf("ssm_sb", [P, 10 * SSM + 3]))
        self.inputs = c.tensor[:, 0:4 * SSM + 2]
        self.a_re, self.a_im, self.c_re, self.c_im = (c.take(SSM) for _ in range(4))
        self.log_dt, self.skip = c.take(1), c.take(1)
        self.er, self.ar, self.ai, self.den = (c.take(SSM) for _ in range(4))
        self.ang, self.dt = c.take(2, SSM), c.take(1)
        self.turns = core.scratch[:, 0:2 * SSM].rearrange("p (a b) -> p a b", a=2)
        self.loaded, self.chain, self.scaled, self.exped, self.sined, self.pool_chain = (
            core.sem(f"ssm_{n}") for n in ("loaded", "chain", "angles", "exp", "sin", "pool_chain"))


def top_attention(core, tag, c, wq, wk, wv, wfi, bfi, wfo, bfo, gate, ln, u_all, film_out):
    nc, ps = core.nc, core.ps
    H, K, TOP = 4, 32, 32
    ctx2, bias2 = c.take(2 * P), c.take(2, P)
    qT, kT, v = c.take(2 * P), c.take(2 * P), c.take(2, P)
    s, e, left = c.take(H, 2, P), c.take(H, 2, P), c.take(H, 2, P)
    best, best0 = c.take(2 * H, 8), c.take(2 * H, 8)
    nmax, tot = c.take(2 * H), c.take(2 * H)
    mean, meanT, ctT = c.take(2, P), c.take(2, P), c.take(2, P)
    carrier = c.take(1)
    HU = [(h, u) for h in range(H) for u in range(2)]
    V = core.marks(f"{tag}_dve", ["k"] + [f"s{h}" for h in range(H)]
                   + [f"{n}{i}" for r in range(TOP // 8) for n in ("top", "out") for i in (r,)] + ["nmax", "kept", "prob"]
                   + ["tot", "inv", "quarter", "coef"] + [f"mean{h}" for h in range(H)] + ["meanT"]
                   + [f"{n}{u}" for u in range(2) for n in ("sc", "mod", "u")])
    A = core.marks(f"{tag}_act", ["q", "v", "exp", "ctT", "fo0", "fo1", "fo2", "fo3"])
    G = core.marks(f"{tag}_pool", ["copies"])
    T = core.marks(f"{tag}_pe", ["qk", "v", "s", "meanT", "ct", "film0", "film1"])
    with nc.Block(tag, no_gpsimd_drain=True) as block:

        @block.gpsimd
        def _(pool):
            pool.sem_inc(G.sem, G.turn())
            with pool.Fori(0, PAIRS) as it:
                pool.wait_ge(T.sem, T.at("v", it - 1))
                pool.wait_ge(V.sem, V.at(f"s{H - 1}", it - 1))
                nc.gpsimd.tensor_copy(ctx2[:CTX, :], core.ctxT[:CTX, ds(it * 2 * P, 2 * P)])
                nc.gpsimd.tensor_copy(bias2.rearrange("p a b -> p (a b)"),
                                      core.ctx_bias[:, ds(it * 2 * P, 2 * P)]).then_inc(G.sem, G.mark("copies"))

        @block.tensor
        def _(pe):
            pe.sem_inc(T.sem, T.turn())
            pe.wait_ge(*core.w_loaded["l1_xattn"])
            with pe.Fori(0, PAIRS) as it:
                pe.wait_ge(A.sem, A.at("fo3", it - 1))
                pe.wait_ge(V.sem, V.at("u1", it - 1))
                nc.tensor.matmul(ps[0][:, 0:2 * P], wq, core.xnT[:, ds(it * 2 * P, 2 * P)], start=True, stop=True)
                nc.tensor.matmul(ps[0][:, 2 * P:], wk[:CTX, :], core.ctxT[:CTX, ds(it * 2 * P, 2 * P)],
                                 start=True, stop=True).then_inc(T.sem, T.mark("qk"))
                pe.wait_ge(G.sem, G.at("copies", it))
                for u in range(2):
                    mm = nc.tensor.matmul(ps[1][:, u * P:(u + 1) * P], ctx2[:CTX, u * P:(u + 1) * P], wv[:CTX, :],
                                          start=True, stop=True)
                mm.then_inc(T.sem, T.mark("v"))
                pe.wait_ge(A.sem, A.at("q", it))
                pe.wait_ge(V.sem, V.at("k", it))
                for h, u in HU:
                    r, tok = slice(K * h, K * h + K), slice(u * P, (u + 1) * P)
                    mm = nc.tensor.matmul(ps[2 + h][:, tok], qT[r, tok], kT[r, tok], start=True, stop=True)
                mm.then_inc(T.sem, T.mark("s"))
                pe.wait_ge(V.sem, V.at(f"mean{H - 1}", it))
                for u in range(2):
                    mm = nc.tensor.transpose(ps[6][:, u * P:(u + 1) * P], mean[:, u, :], core.ident[:, :])
                mm.then_inc(T.sem, T.mark("meanT"))
                pe.wait_ge(V.sem, V.at("meanT", it))
                for u in range(2):
                    mm = nc.tensor.matmul(ps[7][:, u * P:(u + 1) * P], v[:, u, :], meanT[:, u, :],
                                          start=True, stop=True)
                mm.then_inc(T.sem, T.mark("ct"))
                pe.wait_ge(A.sem, A.at("ctT", it))
                for n, (wf, bf) in enumerate(((wfi, bfi), (wfo, bfo))):
                    for u in range(2):
                        bank = ps[2 * n + u][:, 0:2 * P]
                        nc.tensor.matmul(bank, ctT[:, u, :], wf, start=True, stop=False)
                        mm = nc.tensor.matmul(bank, core.ones[0:1, 0:P], bf[0:1, :], start=False, stop=True)
                    mm.then_inc(T.sem, T.mark(f"film{n}"))

        @block.scalar
        def _(act):
            act.sem_inc(A.sem, A.turn())
            core.load_table(ACT.Exp)
            act.wait_ge(*core.w_loaded["l1_xattn"])
            with act.Fori(0, PAIRS) as it:
                act.wait_ge(T.sem, T.at("qk", it))
                nc.scalar.mul(qT, ps[0][:, 0:2 * P], K ** -0.5).then_inc(A.sem, A.mark("q"))
                act.wait_ge(T.sem, T.at("v", it))
                nc.scalar.copy(v.rearrange("p a b -> p (a b)"), ps[1][:, 0:2 * P]).then_inc(A.sem, A.mark("v"))
                act.wait_ge(V.sem, V.at("nmax", it))
                for i, (h, u) in enumerate(HU):
                    a = nc.scalar.activation(e[:, h, u, :], s[:, h, u, :], ACT.Exp, bias=nmax[:, i:i + 1])
                a.then_inc(A.sem, A.mark("exp"))
                act.wait_ge(T.sem, T.at("ct", it))
                nc.scalar.copy(ctT.rearrange("p a b -> p (a b)"), ps[7][:, 0:2 * P]).then_inc(A.sem, A.mark("ctT"))
                act.wait_ge(T.sem, T.at("film1", it))
                for u in range(2):
                    dst = film_out[:, ds(it * 2 + u, 1), :].rearrange("p a d -> p (a d)")
                    nc.scalar.activation(dst[:, 0:P], ps[2 + u][:, 0:P], ACT.Identity, scale=gate, bias=core.ones[:, 0:1]) \
                        .then_inc(A.sem, A.mark(f"fo{2 * u}"))
                    nc.scalar.activation(dst[:, P:], ps[2 + u][:, P:2 * P], ACT.Copy, scale=gate) \
                        .then_inc(A.sem, A.mark(f"fo{2 * u + 1}"))

        @block.vector
        def _(dve):
            dve.sem_inc(V.sem, V.turn())
            with dve.Fori(0, PAIRS) as it:
                dve.wait_ge(A.sem, A.at("q", it))
                nc.vector.tensor_copy(kT, ps[0][:, 2 * P:]).then_inc(V.sem, V.mark("k"))
                dve.wait_ge(T.sem, T.at("s", it))
                dve.wait_ge(G.sem, G.at("copies", it))
                for h in range(H):
                    nc.vector.tensor_tensor(s[:, h], ps[2 + h][:, 0:2 * P].rearrange("p (a b) -> p a b", a=2), bias2,
                                            ALU.add).then_inc(V.sem, V.mark(f"s{h}"))
                dve.wait_ge(V.sem, V.at(f"s{H - 1}", it))
                nc.vector.memset(carrier, 0.0)
                for r in range(TOP // 8):
                    src, top = (s, best0) if r == 0 else (left, best)
                    for i, (h, u) in enumerate(HU):
                        m = nc.vector.max(top[:, i, :], src[:, h, u, :])
                    m.then_inc(V.sem, V.mark(f"top{r}"))
                    dve.wait_ge(V.sem, V.at(f"top{r}", it))
                    nc.vector.memset(carrier, 0.0)
                    for i, (h, u) in enumerate(HU):
                        m = nc.vector.match_replace(left[:, h, u, :], top[:, i, :], src[:, h, u, :], -FLT_MAX)
                    m.then_inc(V.sem, V.mark(f"out{r}"))
                    dve.wait_ge(V.sem, V.at(f"out{r}", it))
                    nc.vector.memset(carrier, 0.0)
                nc.vector.tensor_scalar(nmax, best0[:, :, 0], -1.0, None, ALU.mult).then_inc(V.sem, V.mark("nmax"))
                nc.vector.tensor_tensor(left, s, left, ALU.not_equal).then_inc(V.sem, V.mark("kept"))
                dve.wait_ge(A.sem, A.at("exp", it))
                dve.wait_ge(V.sem, V.at("kept", it))
                nc.vector.tensor_tensor(e, e, left, ALU.mult).then_inc(V.sem, V.mark("prob"))
                dve.wait_ge(V.sem, V.at("prob", it))
                nc.vector.tensor_reduce(tot, e.rearrange("p h u k -> p (h u) k"), AX_X, ALU.add) \
                    .then_inc(V.sem, V.mark("tot"))
                dve.wait_ge(V.sem, V.at("tot", it))
                nc.vector.reciprocal(tot, tot).then_inc(V.sem, V.mark("inv"))
                dve.wait_ge(V.sem, V.at("inv", it))
                nc.vector.tensor_scalar(tot, tot, 1.0 / H, None, ALU.mult).then_inc(V.sem, V.mark("quarter"))
                dve.wait_ge(V.sem, V.at("quarter", it))
                hu = tot.rearrange("p (h u) -> p h u", u=2)
                nc.vector.tensor_tensor(hu, hu, core.text_on[:, ds(it * 2, 2)].unsqueeze(1).broadcast_to([P, H, 2]),
                                        ALU.mult).then_inc(V.sem, V.mark("coef"))
                dve.wait_ge(V.sem, V.at("coef", it))
                for h in range(H):
                    for u in range(2):
                        w = tot[:, 2 * h + u:2 * h + u + 1]
                        if h == 0:
                            m = nc.vector.tensor_scalar(mean[:, u, :], e[:, h, u, :], w, None, ALU.mult)
                        else:
                            m = nc.vector.scalar_tensor_tensor(out=mean[:, u, :], in0=e[:, h, u, :], scalar=w,
                                                               in1=mean[:, u, :], op0=ALU.mult, op1=ALU.add)
                    m.then_inc(V.sem, V.mark(f"mean{h}"))
                    dve.wait_ge(V.sem, V.at(f"mean{h}", it))
                dve.wait_ge(T.sem, T.at("meanT", it))
                nc.vector.tensor_copy(meanT.rearrange("p a b -> p (a b)"), ps[6][:, 0:2 * P]) \
                    .then_inc(V.sem, V.mark("meanT"))
                dve.wait_ge(T.sem, T.at("film0", it))
                for u in range(2):
                    sc = s[:, 0, u, :]
                    dst = u_all[:, ds(it * 2 + u, 1), :].rearrange("p a d -> p (a d)")
                    row = ln[:, ds(it * 2 + u, 1), :].rearrange("p a d -> p (a d)")
                    nc.vector.tensor_scalar(sc, ps[u][:, 0:P], gate, 1.0, ALU.mult, ALU.add) \
                        .then_inc(V.sem, V.mark(f"sc{u}"))
                    dve.wait_ge(V.sem, V.at(f"sc{u}", it))
                    nc.vector.tensor_tensor(sc, sc, row, ALU.mult).then_inc(V.sem, V.mark(f"mod{u}"))
                    dve.wait_ge(V.sem, V.at(f"mod{u}", it))
                    nc.vector.scalar_tensor_tensor(out=dst, in0=ps[u][:, P:2 * P], scalar=gate, in1=sc,
                                                   op0=ALU.mult, op1=ALU.add).then_inc(V.sem, V.mark(f"u{u}"))


def causal_conv(core, tag, c, u, y, flip):
    nc, ps = core.nc, core.ps
    CHN = 16
    BUFS = 4
    rev = c.take(B, D)
    toe = [c.take(CHN, P) for _ in range(BUFS)]
    loads = [core.sem(f"{tag}_toeplitz{s}") for s in range(BUFS)]
    turned, copied = core.sem(f"{tag}_reversed"), core.sem(f"{tag}_reversed_out")
    T = core.marks(f"{tag}_pe", [f"y{s}" for s in range(BUFS)])
    V = core.marks(f"{tag}_dve", [f"y{s}" for s in range(BUFS)])
    TURNS = D // (CHN * BUFS)
    with nc.Block(tag, no_gpsimd_drain=True) as block:

        @block.sync
        def _(sp):
            for it in range(TURNS):
                for s in range(BUFS):
                    if it:
                        sp.wait_ge(T.sem, T.at(f"y{s}", it - 1))
                    src = bass.AP(tensor=core.conv_dram.ap().tensor, offset=(it * BUFS + s) * CHN * 2 * P,
                                  ap=[[1, P], [2 * P, CHN], [1, P]])
                    sp.dma_start(toe[s], src).then_inc(loads[s], 16)

        @block.tensor
        def _(pe):
            pe.sem_inc(T.sem, T.turn())
            for half in range(2):
                mm = nc.tensor.matmul(ps[4 + half][:, :], flip,
                                      u[:, 4 * half:4 * half + 4, :].rearrange("p b d -> p (b d)"),
                                      start=True, stop=True)
            mm.then_inc(turned, 1)
            pe.wait_ge(copied, 2)
            with pe.Fori(0, TURNS) as it:
                for s in range(BUFS):
                    pe.wait_ge(loads[s], it * 16 + 16)
                    pe.wait_ge(V.sem, V.at(f"y{s}", it - 1))
                    for i in range(CHN):
                        mm = nc.tensor.matmul(ps[s][:, i * B:(i + 1) * B], toe[s][:, i, :],
                                              rev[:, :, ds(it * (BUFS * CHN) + (s * CHN + i), 1)]
                                              .rearrange("p b a -> p (b a)"), start=True, stop=True)
                    mm.then_inc(T.sem, T.mark(f"y{s}"))

        @block.vector
        def _(dve):
            dve.sem_inc(V.sem, V.turn())
            dve.wait_ge(turned, 1)
            for half in range(2):
                nc.vector.tensor_copy(rev[:, 4 * half:4 * half + 4, :].rearrange("p b d -> p (b d)"),
                                      ps[4 + half][:, :]).then_inc(copied, 1)
            with dve.Fori(0, TURNS) as it:
                for s in range(BUFS):
                    dve.wait_ge(T.sem, T.at(f"y{s}", it))
                    nc.vector.tensor_copy(y[:, :, ds(it * (BUFS * CHN) + s * CHN, CHN)],
                                          ps[s][:, 0:CHN * B].rearrange("p (d b) -> p b d", b=B)) \
                        .then_inc(V.sem, V.mark(f"y{s}"))


def plain_ffn(core, tag, c, res, w1, b1, w2, b2):
    nc, ps = core.nc, core.ps
    HC = 4
    hT = [c.take(HC, BANK) for _ in range(2)]
    up, gelu, down, add = (core.sem(f"{tag}_{n}") for n in ("up", "gelu", "down", "add"))
    with nc.Block(tag, no_gpsimd_drain=True) as block:

        @block.tensor
        def _(pe):
            for n in range(2 * HC):
                half, i = n // HC, n % HC
                if n >= 4:
                    pe.wait_ge(gelu, n - 3)
                nc.tensor.matmul(ps[n % 4][:, :], w1[:, i * P:(i + 1) * P],
                                 core.xnT[:, half * BANK:(half + 1) * BANK], start=True, stop=True).then_inc(up, 1)
            for half in range(2):
                pe.wait_ge(gelu, HC * (half + 1))
                for t in range(4):
                    bank = ps[4 + half][:, t * P:(t + 1) * P]
                    for i in range(HC):
                        nc.tensor.matmul(bank, hT[half][:, i, t * P:(t + 1) * P], w2[:, i, :],
                                         start=(i == 0), stop=False)
                    mm = nc.tensor.matmul(bank, core.ones[0:1, 0:P], b2[0:1, :], start=False, stop=True)
                mm.then_inc(down, 1)

        @block.scalar
        def _(act):
            for n in range(2 * HC):
                act.wait_ge(up, n + 1)
                nc.scalar.activation(hT[n // HC][:, n % HC, :], ps[n % 4][:, :], ACT.Gelu,
                                     bias=b1[:, n % HC:n % HC + 1]).then_inc(gelu, 1)

        @block.vector
        def _(dve):
            for half in range(2):
                dve.wait_ge(down, half + 1)
                xs = res[:, half * 4:half * 4 + 4, :].rearrange("p b d -> p (b d)")
                nc.vector.tensor_tensor(xs, xs, ps[4 + half][:, :], ALU.add).then_inc(add, 1)


def layer_l1_xattn(core, tag, w):
    nc = core.nc
    c = Carve(core.scratch)
    wq, wk, wv = w.take(P), w.take(P), w.take(P)
    wfi, bfi, wfo, bfo = w.take(2 * P), w.take(2 * P), w.take(2 * P), w.take(2 * P)
    w1, w2, b1, b2, gf, bf = w.take(4 * P), w.take(4, D), w.take(4), w.take(D), w.take(1), w.take(1)
    g_in, b_in, g_out, b_out = (w.take(D) for _ in range(4))
    gate, flip = w.take(1), w.take(P)
    ln, u, y, film_out = c.take(B, D), c.take(B, D), c.take(B, D), c.take(B, 2 * D)
    start = c.at
    every = lambda a: a.unsqueeze(1).broadcast_to([P, B, D])
    layernorm_all(core, tag)
    layernorm_all(core, f"{tag}_in", src=core.xn, out=ln, turn=False)
    affine, stored = core.sem(f"{tag}_affine"), core.sem(f"{tag}_kernels_stored")
    with nc.Block(f"{tag}_affine", no_gpsimd_drain=True) as block:

        @block.sync
        def _(sp):
            sp.dma_start(core.conv_dram.ap(), core.conv_kp).then_inc(stored, 16)
            sp.wait_ge(stored, 16)

        @block.vector
        def _(dve):
            dve.wait_ge(*core.w_loaded[tag])
            link = Link(dve, affine)
            link(nc.vector.tensor_tensor(ln, ln, every(g_in), ALU.mult))
            link(nc.vector.tensor_tensor(ln, ln, every(b_in), ALU.add))

    top_attention(core, f"{tag}_top", c, wq, wk, wv, wfi, bfi, wfo, bfo, gate, ln, u, film_out)
    c.at = start
    causal_conv(core, f"{tag}_conv", c, u, y, flip)
    modulated = core.sem(f"{tag}_modulated")
    with nc.Block(f"{tag}_mod", no_gpsimd_drain=True) as block:

        @block.vector
        def _(dve):
            link = Link(dve, modulated)
            link(nc.vector.tensor_tensor(y, y, film_out[:, :, 0:D], ALU.mult))
            link(nc.vector.tensor_tensor(y, y, film_out[:, :, D:], ALU.add))
            link(nc.vector.tensor_tensor(y, y, core.xn[:, :, :], ALU.add))

    layernorm_all(core, f"{tag}_mid", src=y, out=ln, gain=gf, bias=bf)
    c.at = start
    plain_ffn(core, f"{tag}_ffn", c, y, w1, b1, w2, b2)
    layernorm_all(core, f"{tag}_out", src=y, out=ln, turn=False)
    added = core.sem(f"{tag}_added")
    with nc.Block(f"{tag}_add", no_gpsimd_drain=True) as block:

        @block.vector
        def _(dve):
            link = Link(dve, added)
            link(nc.vector.tensor_tensor(ln, ln, every(g_out), ALU.mult))
            link(nc.vector.tensor_tensor(ln, ln, every(b_out), ALU.add))
            link(nc.vector.tensor_tensor(core.x[:, :, :], core.x[:, :, :], ln, ALU.add))


def wide(*parts):
    out = []
    for a in parts:
        a = np.asarray(a)
        a = a.reshape(a.shape[0], -1)
        out.append(np.pad(a, ((0, P - a.shape[0]), (0, 0))))
    return np.ascontiguousarray(np.concatenate(out, 1))


def rows(a):
    a = np.asarray(a)
    return a.reshape(-1, P, a.shape[-1]).transpose(1, 0, 2).reshape(P, -1)


def lay_weights(i):
    g = {k: np.asarray(v) for k, v in i.items()}
    lay = {}
    lay["l0_xattn"] = wide(g["L0_xattn_Wq"], g["L0_xattn_Wk"], g["L0_xattn_Wv"],
                           rows(g["L0_xattn_Wout"]), g["L0_xattn_bout"][None])
    lay["l2_xattn"] = wide(cols32(g["L2_xattn_Wq"]), cols32(g["L2_xattn_Wk"]), cols32(g["L2_xattn_Wv"]),
                           rows(cols32(g["L2_xattn_Wo"].T).T))
    lay["l2_ffn"] = wide(g["L2_ffn_gate_w"])
    tri = np.triu(np.ones((P, P), np.float32))
    lay["l3_ffn"] = wide(g["L3_ffn_w_g"], tri)
    lay["l0_ffn"] = wide(g["L0_ffn_router_w"].T, g["L0_ffn_b1"].reshape(8, 4, P).transpose(2, 0, 1), g["L0_ffn_b2"])
    lay["l0_attn"] = wide(g["L0_attn_Wq"], g["L0_attn_Wk"], rows(g["L0_attn_Wv"].T), rows(g["L0_attn_Wo"]))
    heads = lambda a: a.transpose(1, 0, 2).reshape(D, 16 * 64)
    pos = np.arange(P) % 8 * 16 + np.arange(P) // 8
    interleaved = np.where(pos[:, None] >= pos[None, :], 0.0, -FLT_MAX).astype(np.float32)
    lay["l1_attn"] = wide(*[heads(g[f"L1_attn_W{n}"]) for n in "qkv"],
                          g["L1_attn_proj_w"].T.reshape(16, 64, D).transpose(1, 0, 2),
                          g["L1_attn_proj_b"][None], interleaved)
    twice = lambda a: np.concatenate([a, a])[:, None]
    lkv = g["L3_xattn_Wlkv"].T
    lay["l3_xattn"] = wide(g["L3_xattn_Wq"].T, lkv, g["L3_xattn_Wkv"].T, g["L3_xattn_Wo"].T, g["L3_xattn_bo"][None],
                           *[g[f"L3_xattn_ln_{n}"][:, None] for n in ("x_g", "x_b", "l_g", "l_b")],
                           twice(g["L3_xattn_qn_g"]), twice(g["L3_xattn_kn_g"]))
    t = np.arange(P)
    seen = (t[:, None] >= t[None, :]) & (t[:, None] <= t[None, :] + 64)
    parts = [*xpos_tables(), np.where(seen, 0.0, -FLT_MAX).astype(np.float32), np.eye(P, k=1, dtype=np.float32)]
    swapped = lambda a: np.concatenate([a[32:], a[:32]])
    every = lambda a: np.broadcast_to(a[None], (P, a.shape[0]))
    for d in range(2):
        b1 = np.pad(g["L1_ffn_b1"][d].reshape(2, 341), ((0, 0), (0, 43))).reshape(2, 3, P)
        qs, ks = g["L1_ffn_q_scale"][d], g["L1_ffn_k_scale"][d]
        parts += [g["L1_ffn_wqkv"][d], rows(g["L1_ffn_wo"][d]), g["L1_ffn_w1"][d],
                  rows(np.pad(g["L1_ffn_w2"][d], ((0, 43), (0, 0)))), b1[0].T, b1[1].T, g["L1_ffn_b2"][d][None],
                  g["L1_ffn_ln_g"][d][:, None], g["L1_ffn_ln_b"][d][:, None],
                  every(qs), every(swapped(qs)), every(ks), every(swapped(ks))]
    lay["l1_ffn"] = wide(*parts)
    n = "L1_xattn_"
    lay["l1_xattn"] = wide(
        g[n + "Wq"], g[n + "Wk"], g[n + "Wv"], g[n + "W_film_in"], g[n + "b_film_in"][None],
        g[n + "W_film_out"], g[n + "b_film_out"][None], g[n + "W1"], rows(g[n + "W2"]),
        g[n + "b1"].reshape(4, P).T, g[n + "b2"][None], g[n + "g_ffn"][:, None], g[n + "b_ffn"][:, None],
        *[every(g[n + m]) for m in ("g_norm_in", "b_norm_in", "g_norm_out", "b_norm_out")],
        every(g[n + "mod_gate"].reshape(1)), np.eye(P, dtype=np.float32)[::-1])
    n = "L2_attn_"
    by_part = lambda a: cols32(a[None]).reshape(4, P).T
    at = np.arange(P)[None, :] - np.arange(P)[:, None] + 128
    lay["l2_attn"] = wide(cols32(g[n + "Wq"].T), cols32(g[n + "Wk"].T), cols32(g[n + "Wv"].T),
                          rows(cols32(g[n + "Wo"]).T), by_part(g[n + "bq"]), by_part(g[n + "bk"]),
                          cols32(g[n + "bv"][None]), g[n + "bo"][None], g[n + "rel_v_emb"][at],
                          g[n + "rel_k_emb"][255::-1].T)
    half = lambda a: np.concatenate([a, a], 0)
    swap = [1, 0, 3, 2]
    ups = []
    for n in "qk":
        cc, ee = g[f"L3_attn_W{n}_up_c"], g[f"L3_attn_W{n}_up_e"]
        ups += [half(np.concatenate([cc, ee], 1)), half(np.concatenate([cc, ee[:, swap]], 1))]
    ups.append(half(g["L3_attn_Wv_up"]))
    lay["l3_attn"] = wide(*[rows(g[f"L3_attn_W{n}_down"].T) for n in "qkv"], *ups,
                          rows(cols32(g["L3_attn_Wc"].T).T), *rope_tables(), causal_bias())
    return lay


def cols32(a):
    a = np.asarray(a)
    return np.pad(a.reshape(a.shape[0], 16, 8), ((0, 0), (0, 0), (0, 24))).reshape(a.shape[0], 512)


FLT_MAX = float(np.finfo(np.float32).max)


def causal_bias():
    t = np.arange(P)
    return np.where(t[:, None] >= t[None, :], 0.0, -FLT_MAX).astype(np.float32)


def rope_tables():
    inv = 1.0 / 10000.0 ** (np.arange(0, 4, 2, dtype=np.float32) / 4)
    fr = np.arange(P, dtype=np.float32)[:, None] * inv[None, :]
    emb = np.concatenate((fr, fr), -1)
    cos, sin = np.zeros((4, 32, P), np.float32), np.zeros((4, 32, P), np.float32)
    cos[:, 0:4] = 1.0
    cos[:, 4:8] = np.cos(emb).T
    sin[:, 4:8] = (np.sin(emb) * np.array([-1, 1, -1, 1])).T
    cos, sin = cos.reshape(P, P), sin.reshape(P, P)
    return [(a * s).astype(np.float32) for s in (8 ** -0.5, 1.0) for a in (cos, sin)]


def xpos_tables():
    half = np.arange(0, 64, 2, dtype=np.float32)
    t = np.arange(P, dtype=np.float32)
    fr = t[:, None] * (1.0 / 10000.0 ** (half / 64))[None, :]
    scale = ((half + 0.4 * 64) / (1.4 * 64))[None, :] ** ((t - P // 2) / 32.0)[:, None]
    cos, sin = np.tile(np.cos(fr), 2), np.concatenate([-np.sin(fr), np.sin(fr)], -1)
    scale = np.tile(scale, 2)
    return [a.astype(np.float32) for a in (cos * scale * 8, sin * scale * 8, cos / scale, sin / scale)]


LAYER_NAMES = ["l0_attn", "l0_xattn", "l0_ffn", "l1_attn", "l1_xattn", "l1_ffn",
               "l2_attn", "l2_xattn", "l2_ffn", "l3_attn", "l3_xattn", "l3_ffn"]
WEIGHTS = 7680
SCRATCH = 25088


def build(nc, x_in, ctx_in, ctxk_in, masks_in, text_in, ssm_in, out, weights, experts):
    names = [LAYER_NAMES[n] for n in LAYERS]
    with ExitStack() as ctx:
        core = Core(nc, ctx)
        core.x = core.sbuf("x_res", [P, B, D])
        core.xn = core.sbuf("xn", [P, B, D])
        core.xnT = core.sbuf("xnT", [P, B * P])
        core.ctxT = core.sbuf("ctxT_sb", [P, B * P])
        core.ident = core.sbuf("ident", [P, P])
        core.ones = core.sbuf("ones", [P, P])
        core.ln_st = core.sbuf("ln_st", [P, B, 6])
        core.ln_mv = core.sbuf("ln_mv", [P, B, 2])
        core.ln_rstd = core.sbuf("ln_rstd", [P, B])
        core.ln_ve = core.sbuf("ln_ve", [P, 2 * B])
        core.ctxk = core.sbuf("ctx_tokens", [P, B, CTX])
        core.ctx_bias = core.sbuf("ctx_bias", [P, B * P])
        core.lat_bias = core.sbuf("lat_bias", [P, B * P])
        core.text_on = core.sbuf("text_on", [P, B])
        mask_b = core.sbuf("mask_bytes", [P, 2 * B * P], mybir.dt.uint8)
        text_b = core.sbuf("text_bytes", [P, B], mybir.dt.uint8)
        core.scratch = core.sbuf("scratch", [P, SCRATCH])
        wbuf = [core.sbuf(f"weights{n}", [P, WEIGHTS]) for n in range(2)]
        core.conv_kp = core.sbuf("conv_kernels_sb", [P, 2 * P])[:, :]
        core.ssm = StateSpace(core)
        core.unused = core.sbuf("unused", [P, 1])
        core.ps = [ctx.enter_context(nc.psum_tensor(f"bank{n}", [P, BANK], F32)) for n in range(8)]
        buffer_loaded = [core.sem(f"weights{n}_loaded") for n in range(2)]
        core.w_loaded = {name: (buffer_loaded[n % 2], 16 * (n // 2 + 1)) for n, name in enumerate(names)}
        core.conv_dram = nc.dram_tensor("conv_kernels", (P, 2 * P), F32, kind="Internal")
        loaded, prepared, stored = core.sem("inputs_loaded"), core.sem("constants_ready"), core.sem("out_stored")

        def load_weights(eng, n):
            name = names[n]
            width = weights[name].shape[1]
            eng.dma_start(wbuf[n % 2][:, 0:width], weights[name]).then_inc(buffer_loaded[n % 2], 16)

        with nc.Block("start", no_gpsimd_drain=True) as block:

            @block.sync
            def _(sp):
                sp.dma_start(core.ssm.inputs, ssm_in).then_inc(core.ssm.loaded, 16)
                sp.dma_start(core.x[:, :, :], x_in.rearrange("b s d -> s b d")).then_inc(loaded, 16)
                sp.dma_start(core.ctxT[:CTX, :], ctx_in).then_inc(loaded, 16)
                sp.dma_start(mask_b[:, :], masks_in.broadcast_to([P, 2 * B * P])).then_inc(loaded, 16)
                sp.dma_start(text_b[:, :], text_in).then_inc(loaded, 16)
                load_weights(sp, 0)
                sp.dma_start(core.ctxk[:, :, :], ctxk_in.rearrange("b s d -> s b d")).then_inc(loaded, 16)
                sp.wait_ge(loaded, 80)

            @block.scalar
            def _(act):
                conv_angles_act(core, act)

            @block.vector
            def _(dve):
                conv_angles_dve(core, dve)
                dve.wait_ge(loaded, 80)
                nc.vector.tensor_copy(core.text_on[:, :], text_b[:, :])
                for n, bias in enumerate((core.ctx_bias, core.lat_bias)):
                    nc.vector.tensor_scalar(bias[:, :], mask_b[:, n * B * P:(n + 1) * B * P], 1.0, FLT_MAX,
                                            ALU.subtract, ALU.mult)

            @block.gpsimd
            def _(pool):
                nc.gpsimd.memset(core.ident[:, :], 0.0).then_inc(prepared, 1)
                nc.gpsimd.memset(core.ones[:, :], 1.0).then_inc(prepared, 1)
                pool.wait_ge(prepared, 2)
                nc.gpsimd.affine_select(out=core.ident[:, :], in_=core.ident[:, :], compare_op=ALU.not_equal,
                                        fill=1.0, base=0, pattern=[[-1, P]], channel_multiplier=1) \
                    .then_inc(prepared, 1)
                pool.wait_ge(prepared, 3)

        for n, name in enumerate(names):
            if n + 1 < len(names):
                with nc.Block(f"{name}_prefetch", no_gpsimd_drain=True) as block:

                    @block.sync
                    def _(sp):
                        load_weights(sp, n + 1)

            if name.endswith("_ffn") and name != "l1_ffn":
                LAYER_FUNCS[name](core, name, Carve(wbuf[n % 2]), experts[name + "_w1"], experts[name + "_w2"])
            else:
                LAYER_FUNCS[name](core, name, Carve(wbuf[n % 2]))

        with nc.Block("finish", no_gpsimd_drain=True) as block:

            @block.sync
            def _(sp):
                sp.dma_start(out.rearrange("b s d -> s b d"), core.x[:, :, :]).then_inc(stored, 16)
                sp.wait_ge(stored, 16)


LAYER_FUNCS = {
    "l0_attn": layer_l0_attn, "l0_xattn": layer_l0_xattn, "l0_ffn": layer_l0_ffn,
    "l1_attn": layer_l1_attn, "l1_xattn": layer_l1_xattn, "l1_ffn": layer_l1_ffn,
    "l2_attn": layer_l2_attn, "l2_xattn": layer_l2_xattn, "l2_ffn": layer_l2_ffn,
    "l3_attn": layer_l3_attn, "l3_xattn": layer_l3_xattn, "l3_ffn": layer_l3_ffn}


def kernel(**inputs):
    import concourse.bacc as _bacc
    from concourse.bass_utils import run_bass_kernel_spmd as _run

    nc = _bacc.Bacc("TRN2", target_bir_lowering=False, num_devices=1)
    g = {k: np.asarray(v) for k, v in inputs.items()}
    arrays = {"x": np.ascontiguousarray(g["x"]),
              "ctxT": np.ascontiguousarray(g["ctx_768"].transpose(2, 0, 1).reshape(CTX, B * P)),
              "ctxk": np.ascontiguousarray(g["ctx_768"]),
              "masks": np.stack([g["mask_BxS2_bf1"], g["mask_BxS2_bk0"]]).reshape(1, 2 * B * P),
              "ssm": wide(*[g["L1_xattn_" + n] for n in ("A_re", "A_im", "C_re", "C_im")],
                          g["L1_xattn_log_dt"][:, None], g["L1_xattn_D_skip"][:, None]),
              "text_mask": np.ascontiguousarray(g["mask_BxS_bf1"].T)}
    lay = lay_weights(g)
    for n in LAYERS:
        arrays["w_" + LAYER_NAMES[n]] = lay[LAYER_NAMES[n]]
        key = {2: ("L0_ffn_w1", "L0_ffn_w2"), 8: ("L2_ffn_w1", "L2_ffn_w2"), 11: ("L3_ffn_c_fc", "L3_ffn_c_proj")}.get(n)
        if key:
            arrays["e_" + LAYER_NAMES[n] + "_w1"] = np.ascontiguousarray(g[key[0]])
            arrays["e_" + LAYER_NAMES[n] + "_w2"] = np.stack([rows(a) for a in g[key[1]]])
    aps = {k: nc.dram_tensor(k, a.shape, mybir.dt.from_np(a.dtype), kind="ExternalInput").ap()
           for k, a in arrays.items()}
    out = nc.dram_tensor("out", (B, P, D), F32, kind="ExternalOutput").ap()
    build(nc, aps["x"], aps["ctxT"], aps["ctxk"], aps["masks"], aps["text_mask"], aps["ssm"], out,
          {k[2:]: a for k, a in aps.items() if k.startswith("w_")},
          {k[2:]: a for k, a in aps.items() if k.startswith("e_")})
    return _run(nc, [arrays], core_ids=[0]).results[0]["out"]
```
